# Optimizing a Trainium2 kernel written in Bass

```python
import numpy as np
import jax
import jax.numpy as jnp

def _softmax(x, axis=-1):
    return jax.nn.softmax(x, axis=axis)

def _gelu(x):
    return jax.nn.gelu(x, approximate=True)

def _silu(x):
    return jax.nn.silu(x)

def _sigmoid(x):
    return jax.nn.sigmoid(x)

def _layernorm(x, axis=-1, eps=1e-05):
    m = jnp.mean(x, axis=axis, keepdims=True)
    v = jnp.var(x, axis=axis, keepdims=True)
    return (x - m) / jnp.sqrt(v + eps)

def _scatter_add(tgt, idx, src, axis=0):
    return tgt.at[idx].add(src)

def _segment_sum(src, seg, n):
    return jax.ops.segment_sum(src, seg, n)
kernel_name = 'mk_decoder_preln_d1_seqx_r4_8493af'

def setup_inputs(seed: int=0):
    np.random.seed(seed)
    _w = jnp.asarray

    def _rec_inputs():
        import jax
        import jax.numpy as jnp
        _rk = jax.random.key(seed)
        x = 4.136e-05 + 0.9999 * jax.random.normal(jax.random.fold_in(_rk, 1), (4, 512, 512), jnp.float32)
        _lenS = 512 - jax.random.randint(jax.random.fold_in(_rk, 7), (4,), 0, max(1, 512 // 4) + 1, jnp.int32)
        _lenS2 = 512 - jax.random.randint(jax.random.fold_in(_rk, 8), (4,), 0, max(1, 512 // 4) + 1, jnp.int32)
        _ctx_1024P = jax.random.normal(jax.random.fold_in(_rk, 11), (4, 16, 256), jnp.float32)
        _ctx_1024c = jax.random.dirichlet(jax.random.fold_in(_rk, 511), 0.3 * jnp.ones((16,), jnp.float32), (4, 512))
        _ctx_1024t = jnp.einsum('bsk,bkd->bsd', _ctx_1024c, _ctx_1024P)
        _ctx_1024t = _ctx_1024t * jax.lax.rsqrt(jnp.mean(jnp.square(_ctx_1024t)) + 1e-12) * 0.953939
        ctx_1024 = -0.000292821 + 1.00034 * (_ctx_1024t + 0.3 * jax.random.normal(jax.random.fold_in(_rk, 611), (4, 512, 256), jnp.float32))
        return (x, ctx_1024)
    x, ctx_1024 = _rec_inputs()

    def _L0_attn_setup():
        import jax, jax.numpy as jnp
        import numpy as np
        EMBED_DIM = 512
        HEADS = 16
        HEAD_DIM = EMBED_DIM // HEADS
        NEG_INF = -1e+30

        def _bitlinear(x, w):
            sw = 1.0 / jnp.clip(jnp.mean(jnp.abs(w)), 1e-05, None)
            wq = jnp.clip(jnp.round(w * sw), -1.0, 1.0) / sw
            w_eff = w + jax.lax.stop_gradient(wq - w)
            sx = 127.0 / jnp.clip(jnp.max(jnp.abs(x), axis=-1, keepdims=True), 1e-05, None)
            xq = jnp.clip(jnp.round(x * sx), -128.0, 127.0) / sx
            x_eff = x + jax.lax.stop_gradient(xq - x)
            return jnp.einsum('bse,oe->bso', x_eff, w_eff)
        key = jax.random.key(seed)
        ks = jax.random.split(key, 5)
        B, S, E = (2, 512, EMBED_DIM)
        std = 1.0 / np.sqrt(E)
        return {'x': jax.random.normal(ks[0], (B, S, E), dtype=jnp.float32), 'w_q': jax.random.normal(ks[1], (E, E), dtype=jnp.float32) * std, 'w_k': jax.random.normal(ks[2], (E, E), dtype=jnp.float32) * std, 'w_v': jax.random.normal(ks[3], (E, E), dtype=jnp.float32) * std, 'w_o': jax.random.normal(ks[4], (E, E), dtype=jnp.float32) * std}
    _L0_attn_all = _L0_attn_setup()
    _L0_attn_in = {k: v for k, v in _L0_attn_all.items() if k in ('w_q', 'w_k', 'w_v', 'w_o')}
    del _L0_attn_all

    def _L0_xattn_setup():
        import jax, jax.numpy as jnp
        import numpy as np
        import math
        B, L, DM = (2, 512, 256)
        DS, DC, EXP = (16, 4, 2)
        DI = EXP * DM
        DR = math.ceil(DM / 16)
        DT_MIN, DT_MAX, DT_FLOOR = (0.001, 0.1, 0.0001)

        def _ssm_forward(hidden_states, z, in_proj_w, conv_w, conv_b, x_proj_w, dt_proj_w, dt_proj_b, A_log, D):
            b = hidden_states.shape[0]
            x = jnp.einsum('ed,bld->bel', in_proj_w, hidden_states)
            xp = jnp.pad(x, ((0, 0), (0, 0), (DC - 1, 0)))
            xc = jax.lax.conv_general_dilated(xp, conv_w[:, None, :], window_strides=(1,), padding='VALID', dimension_numbers=('NCH', 'OIH', 'NCH'), feature_group_count=DI)
            u = jax.nn.silu(xc + conv_b[None, :, None])
            x_dbl = jnp.einsum('ke,bel->bkl', x_proj_w, u)
            dt_lo = x_dbl[:, :DR]
            Bm = x_dbl[:, DR:DR + DS]
            Cm = x_dbl[:, DR + DS:]
            delta = jax.nn.softplus(jnp.einsum('er,brl->bel', dt_proj_w, dt_lo) + dt_proj_b[None, :, None])
            A = -jnp.exp(A_log)

            def step(state, xs):
                d_t, B_t, C_t, u_t = xs
                dA = jnp.exp(d_t[..., None] * A)
                state = state * dA + (d_t * u_t)[..., None] * B_t[:, None, :]
                y_t = jnp.einsum('ben,bn->be', state, C_t)
                return (state, y_t)
            xs = (jnp.moveaxis(delta, -1, 0), jnp.moveaxis(Bm, -1, 0), jnp.moveaxis(Cm, -1, 0), jnp.moveaxis(u, -1, 0))
            state0 = jnp.zeros((b, DI, DS), delta.dtype)
            _, ys = jax.lax.scan(step, state0, xs)
            y = jnp.moveaxis(ys, 0, -1)
            y = y + D[None, :, None] * u
            y = y * jax.nn.silu(z)
            return jnp.swapaxes(y, 1, 2)
        key = jax.random.key(seed)
        ks = jax.random.split(key, 8)
        hidden_states = jax.random.normal(ks[0], (B, L, DM), jnp.float32)
        z = jax.random.normal(ks[1], (B, DI, L), jnp.float32)
        in_proj_w = jax.random.normal(ks[2], (DI, DM), jnp.float32) * DM ** (-0.5)
        conv_w = jax.random.normal(ks[3], (DI, DC), jnp.float32) * DC ** (-0.5)
        conv_b = jnp.zeros((DI,), jnp.float32)
        x_proj_w = jax.random.normal(ks[4], (DR + 2 * DS, DI), jnp.float32) * DI ** (-0.5)
        dt_std = DR ** (-0.5)
        dt_proj_w = jax.random.uniform(ks[5], (DI, DR), jnp.float32, -dt_std, dt_std)
        dt = jnp.exp(jax.random.uniform(ks[6], (DI,), jnp.float32) * (math.log(DT_MAX) - math.log(DT_MIN)) + math.log(DT_MIN))
        dt = jnp.clip(dt, DT_FLOOR)
        dt_proj_b = dt + jnp.log(-jnp.expm1(-dt))
        A_log = jnp.log(jnp.broadcast_to(jnp.arange(1, DS + 1, dtype=jnp.float32), (DI, DS)))
        D = jnp.ones((DI,), jnp.float32)
        return dict(hidden_states=hidden_states, z=z, in_proj_w=in_proj_w, conv_w=conv_w, conv_b=conv_b, x_proj_w=x_proj_w, dt_proj_w=dt_proj_w, dt_proj_b=dt_proj_b, A_log=A_log, D=D)
    _L0_xattn_all = _L0_xattn_setup()
    _L0_xattn_in = {k: v for k, v in _L0_xattn_all.items() if k in ('in_proj_w', 'conv_w', 'conv_b', 'x_proj_w', 'dt_proj_w', 'dt_proj_b', 'A_log', 'D')}
    del _L0_xattn_all

    def _L0_ffn_setup():
        import jax, jax.numpy as jnp
        import numpy as np
        HIDDEN = 512
        INTER = 352
        N_EXPERTS = 8
        TOP_K = 2
        BSZ, SEQ = (1, 512)
        key = jax.random.key(seed)
        k1, k2, k3, k4, k5 = jax.random.split(key, 5)
        scale_h = 1.0 / np.sqrt(HIDDEN)
        scale_i = 1.0 / np.sqrt(INTER)
        return {'hidden_states': jax.random.normal(k1, (BSZ, SEQ, HIDDEN), dtype=jnp.float32), 'router_w': jax.random.uniform(k2, (N_EXPERTS, HIDDEN), jnp.float32, -scale_h, scale_h), 'w_gate': jax.random.uniform(k3, (N_EXPERTS, INTER, HIDDEN), jnp.float32, -scale_h, scale_h), 'w_up': jax.random.uniform(k4, (N_EXPERTS, INTER, HIDDEN), jnp.float32, -scale_h, scale_h), 'w_down': jax.random.uniform(k5, (N_EXPERTS, HIDDEN, INTER), jnp.float32, -scale_i, scale_i)}
    _L0_ffn_all = _L0_ffn_setup()
    _L0_ffn_in = {k: v for k, v in _L0_ffn_all.items() if k in ('router_w', 'w_gate', 'w_up', 'w_down')}
    del _L0_ffn_all
    return {'x': x, 'ctx_1024': ctx_1024, 'L0_attn_w_q': _L0_attn_in['w_q'], 'L0_attn_w_k': _L0_attn_in['w_k'], 'L0_attn_w_v': _L0_attn_in['w_v'], 'L0_attn_w_o': _L0_attn_in['w_o'], 'L0_xattn_in_proj_w': _L0_xattn_in['in_proj_w'], 'L0_xattn_conv_w': _L0_xattn_in['conv_w'], 'L0_xattn_conv_b': _L0_xattn_in['conv_b'], 'L0_xattn_x_proj_w': _L0_xattn_in['x_proj_w'], 'L0_xattn_dt_proj_w': _L0_xattn_in['dt_proj_w'], 'L0_xattn_dt_proj_b': _L0_xattn_in['dt_proj_b'], 'L0_xattn_A_log': _L0_xattn_in['A_log'], 'L0_xattn_D': _L0_xattn_in['D'], 'L0_ffn_router_w': _L0_ffn_in['router_w'], 'L0_ffn_w_gate': _L0_ffn_in['w_gate'], 'L0_ffn_w_up': _L0_ffn_in['w_up'], 'L0_ffn_w_down': _L0_ffn_in['w_down']}

def reference(x, ctx_1024, L0_attn_w_q, L0_attn_w_k, L0_attn_w_v, L0_attn_w_o, L0_xattn_in_proj_w, L0_xattn_conv_w, L0_xattn_conv_b, L0_xattn_x_proj_w, L0_xattn_dt_proj_w, L0_xattn_dt_proj_b, L0_xattn_A_log, L0_xattn_D, L0_ffn_router_w, L0_ffn_w_gate, L0_ffn_w_up, L0_ffn_w_down):
    import jax
    import jax.numpy as jnp

    def _L0_attn_ref(x, w_q, w_k, w_v, w_o):
        import jax, jax.numpy as jnp
        import numpy as np
        EMBED_DIM = 512
        HEADS = 16
        HEAD_DIM = EMBED_DIM // HEADS
        NEG_INF = -1e+30

        def _bitlinear(x, w):
            sw = 1.0 / jnp.clip(jnp.mean(jnp.abs(w)), 1e-05, None)
            wq = jnp.clip(jnp.round(w * sw), -1.0, 1.0) / sw
            w_eff = w + jax.lax.stop_gradient(wq - w)
            sx = 127.0 / jnp.clip(jnp.max(jnp.abs(x), axis=-1, keepdims=True), 1e-05, None)
            xq = jnp.clip(jnp.round(x * sx), -128.0, 127.0) / sx
            x_eff = x + jax.lax.stop_gradient(xq - x)
            return jnp.einsum('bse,oe->bso', x_eff, w_eff)
        B, S, E = x.shape
        H, D = (HEADS, HEAD_DIM)
        q = _bitlinear(x, w_q).reshape(B, S, H, D).transpose(0, 2, 1, 3)
        k = _bitlinear(x, w_k).reshape(B, S, H, D).transpose(0, 2, 1, 3)
        v = _bitlinear(x, w_v).reshape(B, S, H, D).transpose(0, 2, 1, 3)
        attn = jnp.einsum('bhsd,bhtd->bhst', q, k) / np.sqrt(D).astype(np.float32)
        causal = jnp.tril(jnp.ones((S, S), dtype=bool))
        attn = jnp.where(causal[None, None], attn, NEG_INF)
        attn = jax.nn.softmax(attn, axis=-1)
        out = jnp.einsum('bhst,bhtd->bhsd', attn, v)
        out = out.transpose(0, 2, 1, 3).reshape(B, S, E)
        return _bitlinear(out, w_o)

    def _L0_xattn_ref(hidden_states, z, in_proj_w, conv_w, conv_b, x_proj_w, dt_proj_w, dt_proj_b, A_log, D):
        import jax, jax.numpy as jnp
        import numpy as np
        import math
        B, L, DM = (2, 512, 256)
        DS, DC, EXP = (16, 4, 2)
        DI = EXP * DM
        DR = math.ceil(DM / 16)
        DT_MIN, DT_MAX, DT_FLOOR = (0.001, 0.1, 0.0001)

        def _ssm_forward(hidden_states, z, in_proj_w, conv_w, conv_b, x_proj_w, dt_proj_w, dt_proj_b, A_log, D):
            b = hidden_states.shape[0]
            x = jnp.einsum('ed,bld->bel', in_proj_w, hidden_states)
            xp = jnp.pad(x, ((0, 0), (0, 0), (DC - 1, 0)))
            xc = jax.lax.conv_general_dilated(xp, conv_w[:, None, :], window_strides=(1,), padding='VALID', dimension_numbers=('NCH', 'OIH', 'NCH'), feature_group_count=DI)
            u = jax.nn.silu(xc + conv_b[None, :, None])
            x_dbl = jnp.einsum('ke,bel->bkl', x_proj_w, u)
            dt_lo = x_dbl[:, :DR]
            Bm = x_dbl[:, DR:DR + DS]
            Cm = x_dbl[:, DR + DS:]
            delta = jax.nn.softplus(jnp.einsum('er,brl->bel', dt_proj_w, dt_lo) + dt_proj_b[None, :, None])
            A = -jnp.exp(A_log)

            def step(state, xs):
                d_t, B_t, C_t, u_t = xs
                dA = jnp.exp(d_t[..., None] * A)
                state = state * dA + (d_t * u_t)[..., None] * B_t[:, None, :]
                y_t = jnp.einsum('ben,bn->be', state, C_t)
                return (state, y_t)
            xs = (jnp.moveaxis(delta, -1, 0), jnp.moveaxis(Bm, -1, 0), jnp.moveaxis(Cm, -1, 0), jnp.moveaxis(u, -1, 0))
            state0 = jnp.zeros((b, DI, DS), delta.dtype)
            _, ys = jax.lax.scan(step, state0, xs)
            y = jnp.moveaxis(ys, 0, -1)
            y = y + D[None, :, None] * u
            y = y * jax.nn.silu(z)
            return jnp.swapaxes(y, 1, 2)
        return _ssm_forward(hidden_states, z, in_proj_w, conv_w, conv_b, x_proj_w, dt_proj_w, dt_proj_b, A_log, D)

    def _L0_ffn_ref(hidden_states, router_w, w_gate, w_up, w_down):
        import jax, jax.numpy as jnp
        import numpy as np
        HIDDEN = 512
        INTER = 352
        N_EXPERTS = 8
        TOP_K = 2
        BSZ, SEQ = (1, 512)
        B, S, H = hidden_states.shape
        x = hidden_states.reshape(-1, H)
        T = x.shape[0]
        logits = jnp.einsum('th,eh->te', x.astype(jnp.float32), router_w.astype(jnp.float32))
        probs = jax.nn.softmax(logits, axis=-1)
        scores, topk_idx = jax.lax.top_k(probs, TOP_K)
        topk_w = scores / (jnp.sum(scores, axis=-1, keepdims=True) + 1e-20)
        g = jnp.einsum('th,eih->tei', x, w_gate)
        u = jnp.einsum('th,eih->tei', x, w_up)
        act = jax.nn.silu(g) * u
        y = jnp.einsum('tei,ehi->teh', act, w_down)
        comb = jnp.zeros((T, N_EXPERTS), x.dtype).at[jnp.arange(T)[:, None], topk_idx].set(topk_w.astype(x.dtype))
        out = jnp.einsum('te,teh->th', comb, y)
        return out.reshape(B, S, H)
    x = x + _L0_attn_ref(_layernorm(x, axis=-1), L0_attn_w_q, L0_attn_w_k, L0_attn_w_v, L0_attn_w_o)
    x = x + _L0_xattn_ref(ctx_1024, _layernorm(x, axis=-1), L0_xattn_in_proj_w, L0_xattn_conv_w, L0_xattn_conv_b, L0_xattn_x_proj_w, L0_xattn_dt_proj_w, L0_xattn_dt_proj_b, L0_xattn_A_log, L0_xattn_D)
    x = x + _L0_ffn_ref(_layernorm(x, axis=-1), L0_ffn_router_w, L0_ffn_w_gate, L0_ffn_w_up, L0_ffn_w_down)
    return x

_drawn_inputs = setup_inputs


def setup_inputs(seed=0):
    import zlib

    import numpy as np

    out = dict(_drawn_inputs(seed))
    spreads = {'L0_xattn_conv_b': (0.0, 0.1), 'L0_xattn_D': (1.0, 0.2)}
    factors = {'L0_xattn_dt_proj_w': 4.765}
    for name, (base, spread) in spreads.items():
        noise = np.random.default_rng([zlib.crc32(name.encode()), seed]).standard_normal(out[name].shape)
        drawn = base * np.exp(spread * noise) if base else spread * noise
        out[name] = jnp.asarray(drawn.astype(out[name].dtype))
    for name, factor in factors.items():
        out[name] = (out[name] * factor).astype(out[name].dtype)
    return out
```

```python
from contextlib import ExitStack

import concourse.bass as bass
from concourse import mybir

P = 128
NB, S, E = 4, 512, 512
KT = E // P
TOK = NB * S
TT = TOK // P
TB = S // P
HD, HG = 32, 4
NG = 4
NST = 16
DCX, KC = 256, 2
DC = 4
DR = 16
NBC = 2 * NST
XR = 3 * NBC + DR
TURNS = NB * NG
NE, FI = 8, 352
FK = 3
FL = FI - 2 * P
TILES = (2 * TOK) // P + NE
EPS = 1e-5
ROUND = 1.5 * 2.0**23
KB = 1024
FRONT_DVE, JOIN_DVE = 37, 29

ALU = mybir.AluOpType
ACT = mybir.ActivationFunctionType
AX = mybir.AxisListType.X
F32 = mybir.dt.float32
BF16 = mybir.dt.bfloat16
I32 = mybir.dt.int32
U32 = mybir.dt.uint32

MAX_STEP = [[m for m in range(16) if 2 + m // 4 == n] for n in range(NST)]
AT_STEP = [[i for i in range(16) if 7 + i * 9 // 16 == n] for n in range(NST)]
QZ_STEP = {4: [0], 5: [1], 9: [2], 11: [3]}
HEAD_STEP = [9, 11, 13, NST]
NDA, NBS, NH, NHC, NPT = 4, 4, 3, 4, 3


class Chain:

    def __init__(self, eng, sem):
        self.eng, self.sem, self.done, self.at, self.n, self.per = eng, sem, 0, 0, 0, None

    def turn(self, i, per):
        self.at, self.n, self.per = i * per + self.done, 0, per

    def ended(self, turns):
        assert self.n == self.per, (self.n, self.per)
        self.done, self.n, self.per = self.done + turns * self.per, 0, None
        self.at = self.done

    def mark(self, ins):
        ins.then_inc(self.sem, 1)
        self.n += 1
        if self.per is None:
            self.done, self.at, self.n = self.done + 1, self.done + 1, 0
        return self.at + self.n

    def link(self, ins):
        self.eng.wait_ge(self.sem, self.mark(ins))


def apart(eng, steps):
    eng.sem_inc(steps, 1)


def decoder_layer(nc, x, ctx_t, w_attn_t, in_w_t, ssm_par, xp_t, dt_w_t, router_t, wg_t, wu_t, wd_t,
                  k_square, k_sel, k_shift, k_head, k_route, out):
    x_tok = x.rearrange("b (t p) c -> b p t c", p=P)
    with ExitStack() as ctx:
        base = (nc.sbuf_base + 63) // 64 * 64

        def at(name, offset, shape, dt):
            return nc.alloc_sbuf_tensor_at(name, shape, dt, offset=base + int(offset))

        def psum(name, shape, dt):
            return ctx.enter_context(nc.psum_tensor(name, shape, dt))

        def sem(name):
            return ctx.enter_context(nc.semaphore(name))

        o = 0

        def take(name, shape, dt, size):
            nonlocal o
            t = at(name, o, shape, dt)
            o += size
            return t

        delta = take("delta", [P, 2, S], F32, 4 * KB)
        du = take("du", [P, 2, S], F32, 4 * KB)
        dA = take("dA", [P, NDA, S], F32, NDA * 2 * KB)
        dBu = take("dBu", [P, NDA, S], F32, NDA * 2 * KB)
        Bs = take("Bs", [P, NBS, S], F32, NBS * 2 * KB)
        hC = take("hC", [P, NHC, S], F32, NHC * 2 * KB)
        qf = take("qf", [P, S], F32, 2 * KB)
        kf = take("kf", [P, S], F32, 2 * KB)
        q16 = take("q16", [P, S], BF16, KB)
        k16 = take("k16", [P, S], BF16, KB)
        vf = take("vf", [P, TB, HG, HD + 1], F32, 2112)
        pT = take("pT", [P, NPT, S], F32, NPT * 2 * KB)
        sp_ab = take("sp_ab", [P, S], F32, 2 * KB)
        sp_ex = take("sp_ex", [P, S], F32, 2 * KB)
        sp_u1 = take("sp_u1", [P, S], F32, 2 * KB)
        sp_one = take("sp_one", [P, 1], F32, 32)
        dt_wc = take("dt_wc", [XR, P], F32, 512)
        mT = take("mT", [P, S], BF16, KB)
        xqT = take("xqT", [P, KT, TOK], BF16, 16 * KB)
        scale_row = take("scale_row", [P, TOK], F32, 8 * KB)
        assert o <= 86 * KB, o
        f_junk = at("f_junk", 0, [P, KT, E], F32)
        f_xc = at("f_xc", 8 * KB, [P, TB, E], F32)
        f_xm = at("f_xm", 16 * KB, [P, TB, E], F32)
        f_xq = at("f_xq", 24 * KB, [P, TB, E], BF16)
        f_dg = at("f_dg", 28 * KB, [P, TB, P], F32)
        f_ctx = at("f_ctx", 30 * KB, [P, NB, KC, S], F32)
        f_xp = at("f_xp", 46 * KB, [P, NG, S + DC - 1], F32)
        f_cv = at("f_cv", 55 * KB, [P, 2, S], F32)
        f_r1 = at("f_r1", 134 * KB, [P, S], F32)
        uy = at("uy", 88 * KB, [P, TURNS, S], F32)
        w_stage = at("w_stage", 88 * KB, [P, 4, KT, E], F32)
        bcs = at("bcs", 120 * KB, [3 * NBC, TOK], BF16)
        dt_w = at("dt_w", 124 * KB, [XR, E], F32)
        in_w = at("in_w", 126 * KB, [P, KC, E], F32)
        h = at("h", 126 * KB, [P, NH, S], F32)
        xp_w = at("xp_w", 130 * KB, [P, NG, XR], F32)
        Du = at("Du", 134 * KB, [P, S], F32)
        qz = [at("qz0", 86 * KB, [P, S], F32), at("qz1", 132 * KB, [P, S], F32)]
        zeros = at("zeros", 132 * KB, [P, E], F32)
        j_z = at("j_z", 120 * KB, [P, TB, E], F32)
        j_x = at("j_x", 128 * KB, [P, TB, E], F32)
        wT = at("wT", 136 * KB, [P, 4, KT, E], BF16)
        j_q = at("j_q", 136 * KB, [P, TB, E], BF16)
        j_qT = at("j_qT", 140 * KB, [P, KT, S], BF16)
        j_m = at("j_m", 144 * KB, [P, 2, E], F32)
        j_g = at("j_g", 136 * KB, [P, E], F32)
        xa = at("xa", 152 * KB, [P, TT, E], F32)
        o = 184 * KB
        identF = take("identF", [P, P], F32, 512)
        identB = take("identB", [P, P], BF16, 256)
        maskQ = take("maskQ", [P, P], BF16, 256)
        maskK = take("maskK", [P, P], BF16, 256)
        triB = take("triB", [P, P], BF16, 256)
        onesF = take("onesF", [P, P], F32, 512)
        onesB = take("onesB", [P, P], BF16, 256)
        headm = take("headm", [P, HG], F32, 32)
        sel = take("sel", [3 * NBC, NBC, P], BF16, 8 * KB)
        shift = take("shift", [P, HG, P], BF16, KB)
        par = take("par", [P, NG, DC + 3 + NST], F32, 384)
        negA = take("negA", [P, NG, NST], F32, 256)
        wstat = take("wstat", [P, 3, 4], F32, 64)
        cqk = take("cqk", [P, 2], F32, 64)
        dq = take("dq", [P, TT], F32, 64)
        dqv = take("dqv", [P, TT], F32, 64)
        bn6 = take("bn6", [P, TB, 6], F32, 128)
        mv = take("mv", [P, TB, 2], F32, 64)
        nmean = take("nmean", [P, TB], F32, 32)
        vare = take("vare", [P, TB], F32, 32)
        halfs = take("halfs", [P, TB], F32, 32)
        rstd = take("rstd", [P, TB], F32, 32)
        amax = take("amax", [P, TB], F32, 32)
        clip = take("clip", [P, TB], F32, 32)
        qs = take("qs", [P, TB], F32, 32)
        tmp4 = take("tmp4", [P, TB], F32, 32)
        mx = take("mx", [P, TB, HG], F32, 64)
        mhl = take("mhl", [P, TB, 2 * HG], BF16, 64)
        rden = take("rden", [P, TB], F32, 32)
        nm2 = take("nm2", [P, TT], F32, 64)
        rs2 = take("rs2", [P, TT], F32, 64)
        w12 = take("w12", [P, 2, TT], F32, 128)
        slot = take("slot", [P, 2, TT], I32, 128)
        tile_e = take("tile_e", [P, TILES], I32, 192)
        rw = take("rw", [P, KT, NE], F32, 128)
        assert o <= 198 * KB + 256, o / KB
        xd = at("xd", 199 * KB, [XR, TOK], F32)
        j_n = at("j_n", 199 * KB, [P, 2, E], F32)
        j_nT = at("j_nT", 203 * KB, [P, 2, E], F32)
        c_sq = at("c_sq", 84 * KB, [P, 4, P], F32)
        c_sel = at("c_sel", 86 * KB, [3 * NBC, NBC], F32)
        c_shift = at("c_shift", 199 * KB, [P, HG, P], F32)
        wg = at("wg", 0, [P, NE, KT, FI], F32)
        wu = at("wu", 44 * KB, [P, NE, KT, FI], F32)
        wd = at("wd", 88 * KB, [P, NE, FK, E], F32)
        e_x = at("e_x", 136 * KB, [P, 2, E], F32)
        e_xT = at("e_xT", 140 * KB, [P, 2, E], F32)
        e_s = at("e_s", 144 * KB, [P, 2, FI], F32)
        e_a = at("e_a", 147 * KB, [P, 2, FI], F32)
        e_aT = at("e_aT", 199 * KB, [P, 2, FK, P], F32)
        e_y = at("e_y", 203 * KB, [P, 2, E], F32)
        o_r = at("o_r", 0, [P, 4, 2, E], F32)
        o_o = at("o_o", 20 * KB, [P, 4, E], F32)
        j_n4 = at("j_n4", 199 * KB, [P, 4, E], F32)
        ro = 136 * KB
        lg = at("lg", 198 * KB + 256, [P, TT, NE], F32)
        o = ro
        pr = take("pr", [P, TT, NE], F32, 512)
        m16 = take("m16", [P, TT], F32, 64)
        z16 = take("z16", [P, TT], F32, 64)
        top8 = take("top8", [P, TT, 8], F32, 512)
        ix8 = take("ix8", [P, TT, 8], U32, 512)
        ixf = take("ixf", [P, 2, TT], F32, 128)
        oh = take("oh", [P, 2, TT, NE], F32, 1024)
        ohB = take("ohB", [P, TT, NE], BF16, 256)
        cnt = take("cnt", [P, NE, TT], F32, 512)
        keep = take("keep", [P, NE, TT], F32, 512)
        incl = take("incl", [P, NE, TT], F32, 512)
        nt = take("nt", [P, 4, NE], F32, 128)
        ones8 = take("ones8", [P, NE], F32, 32)
        smat = take("smat", [P, TT, NE], F32, 512)
        sx = take("sx", [P, TT, NE], F32, 512)
        slf = take("slf", [P, 2, TT], F32, 128)
        cmp = take("cmp", [P, TILES, NE], F32, 1280)
        tef = take("tef", [P, TILES], F32, 192)
        c_route = take("c_route", [P, TT * NE + NE * TT + TILES * NE], F32, 2304)
        assert o <= 148 * KB, o / KB
        iota_e = c_route[:, 0:TT * NE].rearrange("p (t e) -> p t e", e=NE)
        keep_c = c_route[:, TT * NE:2 * TT * NE].rearrange("p (e t) -> p e t", t=TT)
        tile_no = c_route[:, 2 * TT * NE:].rearrange("p (j e) -> p j e", e=NE)

        bank = [psum(f"bank{i}", [P, 512], F32) for i in range(8)]
        ps_misc, ps_sc, ps_o, ps_y, ps_C, ps_B = bank[0], bank[1:3], bank[3], bank[4], bank[5:7], bank[7]

        slots_x = nc.dram_tensor("slots_x", (TILES * P, E), F32, kind="Internal").ap()
        slots_y = nc.dram_tensor("slots_y", (TILES * P, E), F32, kind="Internal").ap()

        d_const, d_ssm, d_ctx = sem("d_const"), sem("d_ssm"), sem("d_ctx")
        d_w = [sem(f"d_w{i}") for i in range(4)]
        d_x = [sem(f"d_x{i}") for i in range(NB)]
        d_zero, d_route = sem("d_zero"), sem("d_route")
        consts, zeroed = sem("consts"), sem("zeroed")
        wabs_done, wsum_done, wt_done = sem("wabs_done"), sem("wsum_done"), sem("wt_done")
        negA_done = sem("negA_done")
        dve_steps, act_steps, pe_steps = sem("dve_steps"), sem("act_steps"), sem("pe_steps")
        dve_own, act_own, pool_own = sem("dve_own"), sem("act_own"), sem("pool_own")
        f_stats, f_rstd, f_centred, f_quant, f_tr, f_trev, f_diag, f_row, f_rowev = map(
            sem, ("f_stats", "f_rstd", "f_centred", "f_quant", "f_tr", "f_trev", "f_diag", "f_row", "f_rowev"))
        f_in, f_inev, f_conv, f_silu, f_xd, f_xdev, f_split = map(
            sem, ("f_in", "f_inev", "f_conv", "f_silu", "f_xd", "f_xdev", "f_split"))
        dt_ps, dt_abs, dt_exp, dt_u1, dt_ln, dt_relu, dt_done, du_done = map(
            sem, ("dt_ps", "dt_abs", "dt_exp", "dt_u1", "dt_ln", "dt_relu", "dt_done", "du_done"))
        dA_done, B_ps, B_ev, dBu_done, scan_done, C_ps, hC_done, y_acc, y_ev, Du_done = map(
            sem, ("dA_done", "B_ps", "B_ev", "dBu_done", "scan_done", "C_ps", "hC_done", "y_acc",
                  "y_ev", "Du_done"))
        q_ps, q_ev, k_ps, k_ev, v_ps, v_ev, s_ps, max_done, mhl_done, mT_ps, mT_ev = map(
            sem, ("q_ps", "q_ev", "k_ps", "k_ev", "v_ps", "v_ev", "s_ps", "max_done", "mhl_done",
                  "mT_ps", "mT_ev"))
        q16_done, k16_done, qz_done = sem("q16_done"), sem("k16_done"), sem("qz_done")
        st_ps, exp_done, pv_done, o_ev, dtw_ev = map(sem, ("st_ps", "exp_done", "pv_done", "o_ev", "dtw_ev"))
        main_done = sem("main_done")
        d_jx, j_used, j_quant, j_tr, j_trev, j_proj, j_x1, j_stats, j_rstd, j_silu, j_zt, j_gate, j_x2 = map(
            sem, ("d_jx", "j_used", "j_quant", "j_tr", "j_trev", "j_proj", "j_x1", "j_stats", "j_rstd",
                  "j_silu", "j_zt", "j_gate", "j_x2"))
        j_stats2, j_rstd2, j_nm2, j_norm, j_nt, j_ntev, j_lg, j_lgev = map(
            sem, ("j_stats2", "j_rstd2", "j_nm2", "j_norm", "j_nt", "j_ntev", "j_lg", "j_lgev"))
        r_c, r_exp, r_mask, r_rank, r_slots, r_norm = map(
            sem, ("r_c", "r_exp", "r_mask", "r_rank", "r_slots", "r_norm"))
        sc_done = [sem(f"sc_done{i}") for i in range(4)]
        d_wg, d_wu, d_wd = sem("d_wg"), sem("d_wu"), sem("d_wd")
        d_ex = [sem("d_ex0"), sem("d_ex1")]
        d_ey = [sem("d_ey0"), sem("d_ey1")]
        e_tr, e_trev, e_g, e_silu, e_act, e_at, e_atev, e_d, e_dev = map(
            sem, ("e_tr", "e_trev", "e_g", "e_silu", "e_act", "e_at", "e_atev", "e_d", "e_dev"))
        vf_ones = sem("vf_ones")
        g_row = [sem(f"g_row{i}") for i in range(4)]
        o_done = sem("o_done")
        d_out = [sem(f"d_out{i}") for i in range(4)]

        block = ctx.enter_context(nc.Block())

        @block.sync
        def _(sp):
            for w in range(4):
                sp.dma_start(w_stage[:, w], w_attn_t[w].rearrange("(k p) o -> p k o", p=P)).then_inc(d_w[w], 16)
            sp.dma_start(c_sq[:], k_square.rearrange("k p c -> p k c")).then_inc(d_const, 16)
            sp.dma_start(c_sel[:], k_sel).then_inc(d_const, 16)
            sp.dma_start(c_shift[:], k_shift).then_inc(d_const, 16)
            sp.dma_start(headm[:], k_head).then_inc(d_const, 16)
            sp.dma_start(par[:], ssm_par.rearrange("(g p) c -> p g c", p=P)).then_inc(d_ssm, 16)
            sp.dma_start(in_w[:], in_w_t.rearrange("(k p) o -> p k o", p=P)).then_inc(d_ssm, 16)
            sp.dma_start(dt_w[:], dt_w_t).then_inc(d_ssm, 16)
            sp.dma_start(xp_w[:], xp_t.rearrange("(g p) c -> p g c", p=P)).then_inc(d_ssm, 16)
            sp.dma_start(rw[:], router_t.rearrange("(k p) e -> p k e", p=P)).then_inc(d_const, 16)
            for b in range(NB):
                sp.dma_start(xa[:, b * TB:(b + 1) * TB], x_tok[b]).then_inc(d_x[b], 16)
            sp.dma_start(f_ctx[:], ctx_t.rearrange("b (k p) l -> p (b k) l", p=P).rearrange(
                "p (b k) l -> p b k l", k=KC)).then_inc(d_ctx, 16)
            sp.wait_ge(zeroed, 1)
            sp.dma_start(slots_x.rearrange("(t p) c -> p t c", p=P),
                         zeros[:, None, :].broadcast_to([P, TILES, E])).then_inc(d_zero, 16)
            sp.wait_ge(main_done, 4)
            with sp.Fori(0, NB) as b:
                sp.wait_ge(j_used, b + 1)
                sp.dma_start(j_x[:], x_tok[b]).then_inc(d_jx, 16)
            sp.dma_start(wg[:], wg_t.rearrange("e (k p) i -> p (e k) i", p=P).rearrange(
                "p (e k) i -> p e k i", k=KT)).then_inc(d_wg, 16)
            sp.dma_start(wu[:], wu_t.rearrange("e (k p) i -> p (e k) i", p=P).rearrange(
                "p (e k) i -> p e k i", k=KT)).then_inc(d_wu, 16)
            sp.wait_ge(j_lgev, NB + 1)
            sp.dma_start(c_route[:], k_route).then_inc(d_route, 16)
            for c in range(2):
                sp.dma_start(wd[:, :, c], wd_t[:, c * P:(c + 1) * P, :].rearrange("e p o -> p e o")).then_inc(d_wd, 16)
            sp.dma_start(wd[0:FL, :, 2], wd_t[:, 2 * P:FI, :].rearrange("e p o -> p e o")).then_inc(d_wd, 16)
            for c in range(4):
                sp.wait_ge(sc_done[c], 8 * TT)
            slots_xt = slots_x.rearrange("(t p) c -> t p c", p=P)
            with sp.Fori(0, TILES // 2) as i:
                for c in range(2):
                    sp.wait_ge(e_tr, i * 2 + c + 1)
                    sp.dma_start(e_x[:, c], slots_xt[i * 2 + c]).then_inc(d_ex[c], 16)
            for c in range(4):
                sp.wait_ge(d_out[c], 16 * (TT // 4))

        @block.gpsimd
        def _(pool):
            own = Chain(pool, pool_own)
            nc.gpsimd.memset(zeros[:], 0.0).then_inc(zeroed, 1)
            nc.gpsimd.memset(onesF[:], 1.0).then_inc(consts, 1)
            nc.gpsimd.memset(onesB[:], 1.0).then_inc(consts, 1)
            own.link(nc.gpsimd.memset(halfs[:], -0.5))
            pool.sem_inc(dBu_done, NBS)
            with pool.Fori(0, NB) as b:
                pool.wait_ge(f_stats, b + 1)
                nc.gpsimd.tensor_tensor(rstd[:], vare[:], halfs[:], ALU.pow).then_inc(f_rstd, 1)

            def softplus_end(nx, par_, i):
                pool.wait_ge(dt_u1, i)
                own.link(nc.gpsimd.tensor_tensor(sp_ab[:], sp_u1[:], sp_one[:, 0:1].broadcast_to([P, S]), ALU.subtract))
                own.link(nc.gpsimd.tensor_tensor(sp_ex[:], sp_ex[:], sp_ab[:], ALU.subtract))
                pool.wait_ge(dt_relu, i)
                own.link(nc.gpsimd.tensor_tensor(sp_ab[:], sp_ex[:], du[:, par_], ALU.add))
                pool.wait_ge(dt_ln, i)
                own.link(nc.gpsimd.tensor_tensor(delta[:, par_], delta[:, par_], sp_ab[:], ALU.add))
                pool.sem_inc(dt_done, 1)
                nc.gpsimd.tensor_tensor(du[:, par_], delta[:, par_], uy[:, nx], ALU.mult).then_inc(du_done, 1)

            pool.wait_ge(f_split, NB)
            own.link(nc.gpsimd.memset(sp_one[:], 1.0))
            softplus_end(0, 0, 1)
            with pool.Fori(0, TURNS // 2) as pair:
              own.turn(pair, 8)
              for c in range(2):
                it = pair * 2 + c
                pool.wait_ge(du_done, it + 1)
                for n in range(NST):
                    pool.wait_ge(B_ev, it * NST + n + 2)
                    pool.wait_ge(scan_done, it * NST + n + 1)
                    nc.gpsimd.tensor_tensor(dBu[:, n % NDA], du[:, c], Bs[:, n % NBS],
                                            ALU.mult).then_inc(dBu_done, 1)
                    if n == 10:
                        softplus_end((it + 1) % TURNS, 1 - c, it + 2)
            own.ended(TURNS // 2)
            pool.wait_ge(du_done, TURNS + 1)
            pool.sem_inc(main_done, 1)
            with pool.Fori(0, NB) as b:
                pool.wait_ge(j_stats, b + 1)
                nc.gpsimd.tensor_tensor(rstd[:], vare[:], halfs[:], ALU.pow).then_inc(j_rstd, 1)
                pool.wait_ge(j_stats2, b + 1)
                nc.gpsimd.tensor_tensor(rs2[:, bass.ts(b, TB)], vare[:], halfs[:], ALU.pow).then_inc(j_rstd2, 1)
            pool.wait_ge(r_slots, 1)
            pool.wait_ge(d_zero, 16)
            for t in range(TT):
                pool.wait_ge(r_norm, t + 1)
                for j in range(2):
                    pool.indirect_dma_start(
                        out=slots_x, out_offset=bass.IndirectOffsetOnAxis(ap=slot[:, j, t:t + 1], axis=0),
                        in_=j_n4[:, t % 4], in_offset=None).then_inc(sc_done[t % 4], 16)
            for c in range(2):
                pool.wait_ge(d_ey[c], 16 * (TILES // 2) + 16)
            for t in range(TT):
                if t >= 4:
                    pool.wait_ge(o_done, t - 3)
                for j in range(2):
                    pool.indirect_dma_start(
                        out=o_r[:, t % 4, j], out_offset=None, in_=slots_y,
                        in_offset=bass.IndirectOffsetOnAxis(ap=slot[:, j, t:t + 1], axis=0)).then_inc(g_row[t % 4], 16)

        @block.scalar
        def _(act):
            own = Chain(act, act_own)
            for free, count in ((B_ev, 1), (exp_done, 1), (y_ev, 1), (f_trev, 2), (f_rowev, 1), (f_inev, 2),
                                (f_xdev, 1), (f_silu, 2), (j_trev, 2), (j_ntev, 2), (e_trev, 1), (d_ey[0], 16),
                                (d_ey[1], 16)):
                act.sem_inc(free, count)
            for w in range(4):
                act.wait_ge(d_w[w], 16)
                own.link(nc.scalar.activation(f_junk[:], w_stage[:, w], ACT.Abs, accum_out=wstat[:, 0, w:w + 1]))
                act.sem_inc(wabs_done, 1)
            act.wait_ge(d_ssm, 64)
            own.link(nc.scalar.activation(negA[:], par[:, :, DC + 3:], ACT.Exp))
            nc.scalar.activation(negA[:], negA[:], ACT.Copy, scale=-1.0).then_inc(negA_done, 1)
            with act.Fori(0, NB) as b:
                act.wait_ge(f_stats, b + 1)
                for t in range(TB):
                    nc.scalar.activation(f_xc[:, t], xa[:, b * TB + t], ACT.Identity,
                                         bias=nmean[:, t:t + 1]).then_inc(f_centred, 1)
                for t in range(TB):
                    act.wait_ge(f_tr, b * TB + t + 1)
                    nc.scalar.activation(xqT[:, :, bass.ds(b * S + t * P, P)],
                                         bank[t % 2].bitcast(BF16)[:, 0:E].rearrange("p (k c) -> p k c", k=KT),
                                         ACT.Copy).then_inc(f_trev, 1)
                act.wait_ge(f_row, b + 1)
                nc.scalar.activation(scale_row[:, bass.ts(b, S)], bank[2][:], ACT.Copy).then_inc(f_rowev, 1)
                for g in range(NG):
                    act.wait_ge(f_in, b * NG + g + 1)
                    nc.scalar.activation(f_xp[:, g, DC - 1:], bank[3 + g % 2][:], ACT.Copy).then_inc(f_inev, 1)
                for g in range(NG):
                    act.wait_ge(f_conv, b * NG + g + 1)
                    nc.scalar.activation(uy[:, b * NG + g], f_cv[:, g % 2], ACT.Silu).then_inc(f_silu, 1)
                act.wait_ge(f_xd, b + 1)
                nc.scalar.activation(xd[:, bass.ts(b, S)], bank[5][0:XR, :], ACT.Copy).then_inc(f_xdev, 1)

            dtb = DC + 1

            def softplus_mid(g, i, to):
                act.wait_ge(dt_relu, i)
                nc.scalar.activation(sp_ab[:], ps_misc[:], ACT.Abs, bias=par[:, g, dtb:dtb + 1]).then_inc(dt_abs, 1)
                act.wait_ge(dt_abs, i)
                nc.scalar.activation(sp_ex[:], sp_ab[:], ACT.Exp, scale=-1.0).then_inc(dt_exp, 1)
                act.wait_ge(dt_exp, i)
                nc.scalar.activation(sp_u1[:], sp_ex[:], ACT.Copy, bias=1.0).then_inc(dt_u1, 1)
                act.wait_ge(dt_u1, i)
                nc.scalar.activation(delta[:, to], sp_u1[:], ACT.Ln).then_inc(dt_ln, 1)

            act.wait_ge(f_split, NB)
            nc.scalar.preload_act_table_set("natural_log_exp_and_others")
            softplus_mid(0, 1, 0)
            act.wait_ge(vf_ones, 1)
            act.wait_ge(B_ps, 1)
            nc.scalar.activation(Bs[:, 0], ps_B[:], ACT.Copy).then_inc(B_ev, 1)
            act.wait_ge(dt_done, 1)
            for n in range(2):
                nc.scalar.activation(dA[:, n], delta[:, 0], ACT.Exp, scale=negA[:, 0, n:n + 1]).then_inc(dA_done, 1)
            with act.Fori(0, TURNS) as it:
                b, g = it // NG, it % NG
                for n in range(NST):
                    act.wait_ge(B_ps, it * NST + n + 2)
                    act.wait_ge(dBu_done, it * NST + n + 2)
                    nc.scalar.activation(Bs[:, (n + 1) % NBS], ps_B[:], ACT.Copy).then_inc(B_ev, 1)
                    if n == NST - 2:
                        act.wait_ge(dt_done, it + 2)
                    act.wait_ge(scan_done, it * NST + n + 3)
                    nx = it if n < NST - 2 else it + 1
                    nc.scalar.activation(dA[:, (n + 2) % NDA], delta[:, nx % 2], ACT.Exp,
                                         scale=negA[:, nx % NG, (n + 2) % NST:(n + 2) % NST + 1]).then_inc(dA_done, 1)
                    if n == 0:
                        act.wait_ge(y_acc, it * NST + NHC)
                        nc.scalar.activation(Du[:], uy[:, it], ACT.Identity,
                                             scale=par[:, g, DC + 2:DC + 3]).then_inc(Du_done, 1)
                    if n == 3:
                        act.wait_ge(v_ps, it + 1)
                        for t in range(TB):
                            ins = nc.scalar.activation(vf[:, t, :, 0:HD],
                                                       ps_misc[:, t * P:(t + 1) * P].rearrange("p (h d) -> p h d", d=HD),
                                                       ACT.Identity, scale=dqv[:, bass.ds(b * TB + t, 1)])
                        ins.then_inc(v_ev, 1)
                    if n == 5:
                        nc.scalar.activation(dt_wc[:], dt_w[:, bass.ds((it + 1) % NG * P, P)], ACT.Copy).then_inc(dtw_ev, 1)
                    if n == 7:
                        act.wait_ge(mT_ps, it + 1)
                        nc.scalar.activation(mT[0:2 * HG], ps_misc.bitcast(BF16)[0:2 * HG, 0:S], ACT.Copy).then_inc(mT_ev, 1)
                    if n == 9:
                        softplus_mid((it + 1) % NG, it + 2, (it + 1) % 2)
                    for i in AT_STEP[n]:
                        hh, kt = i // TB, i % TB
                        w = S - kt * P
                        act.wait_ge(st_ps, it * 16 + i + 1)
                        act.wait_ge(pv_done, it * 16 + (i + 1 if i else NPT))
                        nc.scalar.activation(pT[:, i % NPT, 0:w], ps_sc[i % 2][:, 0:w], ACT.Exp).then_inc(exp_done, 1)
                act.wait_ge(y_acc, it * NST + NST + NHC)
                apart(act, act_steps)
                nc.scalar.activation(uy[:, it], ps_y[:], ACT.Copy).then_inc(y_ev, 1)
            act.wait_ge(y_ev, TURNS + 1)
            act.sem_inc(main_done, 1)
            with act.Fori(0, NB) as b:
                for t in range(TB):
                    act.wait_ge(j_tr, b * TB + t + 1)
                    nc.scalar.activation(j_qT[:, :, t * P:(t + 1) * P],
                                         bank[t % 2].bitcast(BF16)[:, 0:E].rearrange("p (k c) -> p k c", k=KT),
                                         ACT.Copy).then_inc(j_trev, 1)
                act.wait_ge(j_nm2, b * 2 + 1)
                act.wait_ge(j_zt, b * TB + 1)
                for t in range(TB):
                    nc.scalar.activation(j_z[:, t], xa[:, b * TB + t], ACT.Silu, bias=nmean[:, t:t + 1],
                                         scale=rstd[:, t:t + 1]).then_inc(j_silu, 1)
                act.wait_ge(j_nm2, b * 2 + 2)

                def norm_back(t):
                    act.wait_ge(j_nt, b * TB + t + 3)
                    nc.scalar.activation(j_nT[:, t % 2], bank[5 + t % 2][:], ACT.Copy).then_inc(j_ntev, 1)

                for t in range(TB):
                    act.wait_ge(j_nt, b * TB + t + 1)
                    nc.scalar.activation(j_n[:, t % 2], xa[:, b * TB + t], ACT.Identity,
                                         bias=nm2[:, bass.ds(b * TB + t, 1)],
                                         scale=rs2[:, bass.ds(b * TB + t, 1)]).then_inc(j_norm, 1)
                    if t >= 1:
                        norm_back(t - 1)
                norm_back(TB - 1)
            act.wait_ge(r_c, 1)
            nc.scalar.activation(pr[:], pr[:], ACT.Exp).then_inc(r_exp, 1)
            act.wait_ge(r_slots, 1)
            for t in range(TT):
                if t >= 4:
                    act.wait_ge(sc_done[t % 4], 32 * (t // 4))
                nc.scalar.activation(j_n4[:, t % 4], xa[:, t], ACT.Identity, bias=nm2[:, t:t + 1],
                                     scale=rs2[:, t:t + 1]).then_inc(r_norm, 1)

            slots_yt = slots_y.rearrange("(t p) c -> t p c", p=P)

            def transposed(j, c):
                act.wait_ge(e_tr, j + 3)
                act.wait_ge(e_g, j + 1)
                nc.scalar.activation(e_xT[:, c], bank[0][:], ACT.Copy).then_inc(e_trev, 1)

            def silu(j, c):
                act.wait_ge(e_g, j + 3)
                act.wait_ge(e_act, j + 1)
                nc.scalar.activation(e_s[:, c], bank[1 + c][:, 0:FI], ACT.Silu).then_inc(e_silu, 1)

            def store(j, c):
                act.wait_ge(e_dev, j + 3)
                act.dma_start(slots_yt[j], e_y[:, c]).then_inc(d_ey[c], 16)

            transposed(0, 0)
            transposed(1, 1)
            silu(0, 0)
            with act.Fori(0, TILES // 2 - 1) as i:
                for c in range(2):
                    j = i * 2 + c + 1
                    transposed(j + 1, c)
                    silu(j, 1 - c)
                    store(j - 1, c)
            silu(TILES - 1, 1)
            store(TILES - 2, 0)
            store(TILES - 1, 1)
            for t in range(TT):
                act.wait_ge(o_done, t + 1)
                act.dma_start(out[t * P:(t + 1) * P, :], o_o[:, t % 4]).then_inc(d_out[t % 4], 16)

        @block.tensor
        def _(pe):
            mm = nc.tensor.matmul
            for free, count in ((y_acc, NHC), (pv_done, NPT), (j_zt, 1), (j_nt, 2), (e_tr, 2),
                                (e_g, 2), (e_at, 2), (e_d, 2)):
                pe.sem_inc(free, count)
            pe.wait_ge(consts, 3)
            pe.wait_ge(wabs_done, 4)
            mm(bank[6][:, 0:4], onesF[:], wstat[:, 0, :], start=True, stop=True).then_inc(wsum_done, 1)
            pe.wait_ge(d_ssm, 64)
            pe.wait_ge(d_ctx, 16)
            with pe.Fori(0, NB) as b:
                for t in range(TB):
                    pe.wait_ge(f_quant, b * TB + t + 1)
                    pe.wait_ge(f_trev, b * TB + t + 1)
                    for k in range(KT):
                        last = nc.tensor.transpose(bank[t % 2].bitcast(BF16)[:, k * P:(k + 1) * P],
                                                   f_xq[:, t, k * P:(k + 1) * P], identB[:])
                    last.then_inc(f_tr, 1)
                pe.wait_ge(f_diag, b + 1)
                pe.wait_ge(f_rowev, b + 1)
                mm(bank[2][:], onesF[:], f_dg[:].rearrange("p t c -> p (t c)"), start=True, stop=True).then_inc(f_row, 1)
                for g in range(NG):
                    pe.wait_ge(f_inev, b * NG + g + 1)
                    for k in range(KC):
                        last = mm(bank[3 + g % 2][:], in_w[:, k, g * P:(g + 1) * P], f_ctx[:, b, k],
                                  start=k == 0, stop=k == KC - 1)
                    last.then_inc(f_in, 1)
                pe.wait_ge(f_silu, b * NG + NG + 2)
                pe.wait_ge(f_xdev, b + 1)
                for g in range(NG):
                    last = mm(bank[5][0:XR, :], xp_w[:, g], uy[:, b * NG + g], start=g == 0, stop=g == NG - 1)
                last.then_inc(f_xd, 1)

            pe.wait_ge(f_split, NB)
            pe.wait_ge(wt_done, 4)
            pe.wait_ge(vf_ones, 1)
            mm(ps_misc[:], dt_w[:, 0:P], xd[:, 0:S], start=True, stop=True).then_inc(dt_ps, 1)
            mm(ps_B[:], sel[:, 0], bcs[:, 0:S], start=True, stop=True).then_inc(B_ps, 1)
            with pe.Fori(0, TURNS) as it:
                b, g = it // NG, it % NG

                def accumulate(n):
                    pe.wait_ge(hC_done, it * NST + n + 3)
                    if n == 0:
                        pe.wait_ge(y_ev, it + 1)
                    for t in range(TB):
                        last = mm(ps_y[:, t * P:(t + 1) * P], hC[:, n % NHC, t * P:(t + 1) * P], identF[:],
                                  start=n == 0 and t == 0, stop=n == NST - 1, is_transpose=True, skip_group_check=True)
                    last.then_inc(y_acc, 1)

                def scores(m):
                    hh, qt = m // TB, m % TB
                    if m == 0:
                        pe.wait_ge(exp_done, it * 16 + 1)
                        pe.wait_ge(q16_done, it + 1)
                        pe.wait_ge(k16_done, it + 1)
                    if m >= 2:
                        pe.wait_ge(max_done, it * 16 + m - 1)
                    w = (qt + 1) * P
                    r = slice(hh * HD, (hh + 1) * HD)
                    mm(ps_sc[m % 2][:, 0:w], q16[r, qt * P:(qt + 1) * P], k16[r, 0:w],
                       start=True, stop=False, skip_group_check=True)
                    mm(ps_sc[m % 2][:, w - P:w], identB[:], maskQ[:], start=False, stop=True,
                       skip_group_check=True).then_inc(s_ps, 1)

                def scores_t(i):
                    hh, kt = i // TB, i % TB
                    if i == 0:
                        pe.wait_ge(max_done, it * 16 + 16)
                        pe.wait_ge(mT_ev, it + 1)
                    if i >= 2:
                        pe.wait_ge(exp_done, it * 16 + i)
                    w = S - kt * P
                    if kt == 0:
                        pe.wait_ge(qz_done, it * HG + hh + 1)
                    mm(ps_sc[i % 2][:, 0:w], kf[:, kt * P:(kt + 1) * P], qz[hh % 2][:, kt * P:S],
                       start=True, stop=False, skip_group_check=True)
                    mm(ps_sc[i % 2][:, 0:P], identB[:], maskK[:], start=False, stop=False, skip_group_check=True)
                    mm(ps_sc[i % 2][:, 0:w], shift[:, hh], mT[:, kt * P:S], start=False, stop=True,
                       skip_group_check=True).then_inc(st_ps, 1)

                def values(i):
                    hh, kt = i // TB, i % TB
                    pe.wait_ge(exp_done, it * 16 + i + 2)
                    if kt == 0:
                        pe.wait_ge(o_ev, it * HG + hh + 1)
                    for qt in range(kt, TB):
                        last = mm(ps_o[:, qt * (HD + 1):(qt + 1) * (HD + 1)], pT[:, i % NPT, (qt - kt) * P:(qt - kt + 1) * P],
                                  vf[:, kt, hh], start=kt == 0 and qt == 0, stop=kt == qt, skip_group_check=True)
                    last.then_inc(pv_done, 1)

                for n in range(NST):
                    pe.wait_ge(B_ev, it * NST + n + 2)
                    b_n = b if n < NST - 1 else (it + 1) % TURNS // NG
                    mm(ps_B[:], sel[:, (n + 1) % NST], bcs[:, bass.ds(b_n * S, S)], start=True, stop=True).then_inc(B_ps, 1)
                    pe.wait_ge(hC_done, it * NST + n + 1)
                    mm(ps_C[n % 2][:], sel[:, NST + n], bcs[:, bass.ds(b * S, S)], start=True, stop=True).then_inc(C_ps, 1)
                    if n >= 2:
                        accumulate(n - 2)
                    if n == 4:
                        pe.wait_ge(Du_done, it + 1)
                        for t in range(TB):
                            mm(ps_y[:, t * P:(t + 1) * P], Du[:, t * P:(t + 1) * P], identF[:], start=False, stop=False,
                               is_transpose=True, skip_group_check=True)
                    if n == 0:
                        pe.wait_ge(dt_abs, it + 1)
                        pe.wait_ge(dt_relu, it + 1)
                        for k in range(KT):
                            last = mm(ps_misc[:], wT[:, 0, k, bass.ds(g * P, P)], xqT[:, k, bass.ds(b * S, S)],
                                      start=k == 0, stop=k == KT - 1)
                        last.then_inc(q_ps, 1)
                    if n == 1:
                        pe.wait_ge(q_ev, it + 1)
                        for k in range(KT):
                            last = mm(ps_misc[:], wT[:, 1, k, bass.ds(g * P, P)], xqT[:, k, bass.ds(b * S, S)],
                                      start=k == 0, stop=k == KT - 1)
                        last.then_inc(k_ps, 1)
                    for m in MAX_STEP[n]:
                        if m == 0:
                            pe.wait_ge(k_ev, it + 1)
                            for t in range(TB):
                                for k in range(KT):
                                    last = mm(ps_misc[:, t * P:(t + 1) * P], xqT[:, k, bass.ds(b * S + t * P, P)],
                                              wT[:, 2, k, bass.ds(g * P, P)], start=k == 0, stop=k == KT - 1)
                            last.then_inc(v_ps, 1)
                        scores(m)
                    if n == 6:
                        pe.wait_ge(mhl_done, it + 1)
                        pe.wait_ge(v_ev, it + 1)
                        for t in range(TB):
                            last = nc.tensor.transpose(ps_misc.bitcast(BF16)[0:2 * HG, t * P:(t + 1) * P],
                                                       mhl[:, t], identB[:])
                        last.then_inc(mT_ps, 1)
                    for i in AT_STEP[n]:
                        scores_t(i)
                        if i >= 1:
                            values(i - 1)
                    if n == 7:
                        pe.wait_ge(mT_ev, it + 1)
                        pe.wait_ge(dtw_ev, it + 1)
                        mm(ps_misc[:], dt_wc[:], xd[:, bass.ds((it + 1) % TURNS // NG * S, S)],
                           start=True, stop=True).then_inc(dt_ps, 1)
                accumulate(14)
                accumulate(15)
                values(15)

            pe.wait_ge(y_acc, TURNS * NST + NHC)
            pe.sem_inc(main_done, 1)
            with pe.Fori(0, NB) as b:
                for t in range(TB):
                    pe.wait_ge(j_quant, b * TB + t + 1)
                    pe.wait_ge(j_trev, b * TB + t + 1)
                    for k in range(KT):
                        last = nc.tensor.transpose(bank[t % 2].bitcast(BF16)[:, k * P:(k + 1) * P],
                                                   j_q[:, t, k * P:(k + 1) * P], identB[:])
                    last.then_inc(j_tr, 1)
                for t in range(TB):
                    pe.wait_ge(j_trev, b * TB + t + 3)
                    pe.wait_ge(j_x1, b * TB + t + 1)
                    for k in range(KT):
                        last = mm(bank[2 + t % 2][:], j_qT[:, k, t * P:(t + 1) * P], wT[:, 3, k],
                                  start=k == 0, stop=k == KT - 1)
                    last.then_inc(j_proj, 1)
                for t in range(TB):
                    pe.wait_ge(j_silu, b * TB + t + 1)
                    pe.wait_ge(j_gate, b * TB + t + 1)
                    for k in range(KT):
                        last = nc.tensor.transpose(bank[4][:, k * P:(k + 1) * P], j_z[:, t, k * P:(k + 1) * P], identF[:])
                    last.then_inc(j_zt, 1)

                def logits(t):
                    pe.wait_ge(j_ntev, b * TB + t + 3)
                    for k in range(KT):
                        last = mm(bank[7][:, t * NE:(t + 1) * NE], j_nT[:, t % 2, k * P:(k + 1) * P], rw[:, k],
                                  start=k == 0, stop=k == KT - 1)
                    return last

                for t in range(TB):
                    pe.wait_ge(j_norm, b * TB + t + 1)
                    pe.wait_ge(j_ntev, b * TB + t + 1)
                    for k in range(KT):
                        last = nc.tensor.transpose(bank[5 + t % 2][:, k * P:(k + 1) * P], j_n[:, t % 2, k * P:(k + 1) * P],
                                                   identF[:])
                    last.then_inc(j_nt, 1)
                    if t == 1:
                        pe.wait_ge(j_lgev, b + 1)
                    if t >= 1:
                        logits(t - 1)
                logits(TB - 1).then_inc(j_lg, 1)
            pe.wait_ge(r_mask, 1)
            mm(bank[0][:, 0:TT * NE], triB[:], ohB[:].rearrange("p t e -> p (t e)"), start=True, stop=True)
            mm(bank[1][:, 0:TT * NE], onesB[:], ohB[:].rearrange("p t e -> p (t e)"),
               start=True, stop=True).then_inc(r_rank, 1)
            pe.wait_ge(r_slots, 1)

            def rows_t(j, c, half):
                pe.wait_ge(d_ex[c], half * 16 + 16)
                pe.wait_ge(e_trev, j + 1)
                for k in range(KT):
                    last = nc.tensor.transpose(bank[0][:, k * P:(k + 1) * P], e_x[:, c, k * P:(k + 1) * P], identF[:])
                last.then_inc(e_tr, 1)

            def gate_up(j, c):
                pe.wait_ge(e_trev, j + 2)
                pe.wait_ge(e_act, j + 1)
                apart(pe, pe_steps)
                e = pe.value_load(tile_e[0:1, bass.ds(j, 1)], min_val=0, max_val=NE - 1)
                for k in range(KT):
                    mm(bank[1 + c][:, 0:FI], e_xT[:, c, k * P:(k + 1) * P], wg[:, e, k], start=k == 0, stop=k == KT - 1)
                for k in range(KT):
                    last = mm(bank[3 + c][:, 0:FI], e_xT[:, c, k * P:(k + 1) * P], wu[:, e, k],
                              start=k == 0, stop=k == KT - 1)
                last.then_inc(e_g, 1)

            def act_t(j, c):
                pe.wait_ge(e_act, j + 3)
                pe.wait_ge(e_atev, j + 1)
                for f in range(FK):
                    w = P if f < FK - 1 else FL
                    last = nc.tensor.transpose(bank[5][0:w, f * P:(f + 1) * P], e_a[:, c, f * P:f * P + w], identF[:])
                last.then_inc(e_at, 1)

            def down(j, c):
                pe.wait_ge(e_atev, j + 2)
                pe.wait_ge(e_dev, j + 1)
                apart(pe, pe_steps)
                e = pe.value_load(tile_e[0:1, bass.ds(j, 1)], min_val=0, max_val=NE - 1)
                for f in range(FK):
                    w = P if f < FK - 1 else FL
                    last = mm(bank[6 + c][:], e_aT[0:w, c, f], wd[0:w, e, f], start=f == 0, stop=f == FK - 1)
                last.then_inc(e_d, 1)

            rows_t(0, 0, 0)
            rows_t(1, 1, 0)
            pe.wait_ge(d_wg, 16)
            pe.wait_ge(d_wu, 16)
            gate_up(0, 0)
            pe.wait_ge(d_wd, 48)
            with pe.Fori(0, TILES // 2 - 1) as i:
                for c in range(2):
                    j = i * 2 + c + 1
                    rows_t(j + 1, c, i + 1)
                    act_t(j - 1, c)
                    gate_up(j, 1 - c)
                    down(j - 1, c)
            act_t(TILES - 2, 0)
            gate_up(TILES - 1, 1)
            down(TILES - 2, 0)
            act_t(TILES - 1, 1)
            down(TILES - 1, 1)

        @block.vector
        def _(dve):
            own = Chain(dve, dve_own)
            v = nc.vector
            for free, count in ((scan_done, NDA), (hC_done, 2), (o_ev, 1), (j_x1, 2), (j_gate, 1), (j_used, 1),
                                (j_lgev, 1), (e_act, 2), (e_atev, 1), (e_dev, 2)):
                dve.sem_inc(free, count)
            own.link(v.memset(f_xp[:, :, 0:DC - 1], 0.0))
            dve.wait_ge(d_const, 80)
            v.tensor_copy(identF[:], c_sq[:, 0])
            v.tensor_copy(identB[:], c_sq[:, 0])
            v.tensor_copy(maskQ[:], c_sq[:, 1])
            v.tensor_copy(maskK[:], c_sq[:, 2])
            v.tensor_copy(triB[:], c_sq[:, 3])
            v.tensor_copy(shift[:], c_shift[:])
            v.tensor_copy(sel[:], c_sel[:, :, None].broadcast_to([3 * NBC, NBC, P])).then_inc(consts, 1)
            dve.wait_ge(wsum_done, 1)
            own.link(v.tensor_scalar(wstat[:, 1], bank[6][:, 0:4], 1.0 / (E * E), 1e-5, ALU.mult, ALU.max))
            own.link(v.reciprocal(wstat[:, 2], wstat[:, 1]))
            own.link(v.tensor_scalar(cqk[:, 0:1], wstat[:, 1, 0:1], wstat[:, 1, 1:2], HD ** -0.5, ALU.mult, ALU.mult))
            for w in range(4):
                own.link(v.tensor_scalar(w_stage[:, w], w_stage[:, w], wstat[:, 2, w:w + 1], 1.0, ALU.mult, ALU.min))
                own.link(v.tensor_scalar(w_stage[:, w], w_stage[:, w], -1.0, ROUND, ALU.max, ALU.add))
                v.tensor_scalar(wT[:, w], w_stage[:, w], ROUND, None, ALU.subtract).then_inc(wt_done, 1)

            dve.wait_ge(wt_done, 4)
            for bb in range(NB):
                dve.wait_ge(d_x[bb], 16)
            with dve.Fori(0, NB) as b:
                own.turn(b, FRONT_DVE)
                for t in range(TB):
                    own.mark(v.bn_stats(bn6[:, t], xa[:, b * TB + t]))
                dve.wait_ge(dve_own, own.at + own.n)
                apart(dve, dve_steps)
                for t in range(TB):
                    own.mark(v.bn_aggr(mv[:, t], bn6[:, t]))
                dve.wait_ge(dve_own, own.at + own.n)
                own.mark(v.tensor_scalar(nmean[:], mv[:, :, 0], -1.0, None, ALU.mult))
                v.tensor_scalar(vare[:], mv[:, :, 1], EPS, None, ALU.add).then_inc(f_stats, 1)
                dve.wait_ge(f_centred, b * TB + TB)
                own.link(v.tensor_reduce(amax[:], f_xc[:], AX, ALU.max, apply_absolute_value=True))
                dve.wait_ge(f_rstd, b + 1)
                own.link(v.tensor_tensor(clip[:], amax[:], rstd[:], ALU.mult))
                own.link(v.tensor_scalar(clip[:], clip[:], 1e-5, None, ALU.max))
                own.mark(v.tensor_scalar(dq[:, bass.ts(b, TB)], clip[:], 1.0 / 127, None, ALU.mult))
                own.mark(v.tensor_scalar(dqv[:, bass.ts(b, TB)], clip[:], 1.0 / 127, wstat[:, 1, 2:3], ALU.mult, ALU.mult))
                own.link(v.reciprocal(tmp4[:], clip[:]))
                own.link(v.scalar_tensor_tensor(out=qs[:], in0=tmp4[:], scalar=127.0, in1=rstd[:], op0=ALU.mult, op1=ALU.mult))
                for t in range(TB):
                    own.link(v.tensor_scalar(f_xm[:, t], f_xc[:, t], qs[:, t:t + 1], ROUND, ALU.mult, ALU.add))
                    v.tensor_scalar(f_xq[:, t], f_xm[:, t], ROUND, 127.0, ALU.subtract, ALU.min).then_inc(f_quant, 1)
                for t in range(TB):
                    last = v.tensor_scalar(f_dg[:, t], identF[:], dq[:, bass.ds(b * TB + t, 1)], None, ALU.mult)
                last.then_inc(f_diag, 1)
                for g in range(NG):
                    dve.wait_ge(f_inev, b * NG + g + 3)
                    dve.wait_ge(f_silu, b * NG + g + 1)
                    own.link(v.tensor_scalar(f_cv[:, g % 2], f_xp[:, g, 0:S], par[:, g, 0:1], par[:, g, DC:DC + 1],
                                             ALU.mult, ALU.add))
                    for j in range(1, DC):
                        ins = v.scalar_tensor_tensor(out=f_cv[:, g % 2], in0=f_xp[:, g, j:j + S], scalar=par[:, g, j:j + 1],
                                                     in1=f_cv[:, g % 2], op0=ALU.mult, op1=ALU.add)
                        if j < DC - 1:
                            own.link(ins)
                    ins.then_inc(f_conv, 1)
                dve.wait_ge(f_xdev, b + 2)
                apart(dve, dve_steps)
                cols = bass.ts(b, S)
                own.link(v.tensor_copy(bcs[:, cols], xd[0:3 * NBC, cols]))
                own.link(v.tensor_tensor(f_r1[0:3 * NBC], xd[0:3 * NBC, cols], bcs[:, cols], ALU.subtract))
                apart(dve, dve_steps)
                own.mark(v.tensor_copy(bcs[NBC:2 * NBC, cols], f_r1[NBC:2 * NBC]))
                own.link(v.tensor_copy(bcs[2 * NBC:, cols], f_r1[2 * NBC:3 * NBC]))
                own.link(v.tensor_tensor(f_r1[2 * NBC:3 * NBC], f_r1[2 * NBC:3 * NBC], bcs[2 * NBC:, cols], ALU.subtract))
                apart(dve, dve_steps)
                v.tensor_copy(bcs[2 * NBC:, cols], f_r1[2 * NBC:3 * NBC]).then_inc(f_split, 1)
            own.ended(NB)

            def relu(g, i, to):
                dve.wait_ge(dt_ps, i)
                v.tensor_scalar(du[:, to], ps_misc[:], par[:, g, DC + 1:DC + 2], 0.0, ALU.add, ALU.max).then_inc(dt_relu, 1)

            dve.wait_ge(f_split, NB)
            v.memset(mT[:], 0.0)
            v.memset(vf[:, :, :, HD:], 1.0).then_inc(vf_ones, 1)
            relu(0, 1, 0)
            dve.wait_ge(d_zero, 16)
            with dve.Fori(0, TURNS) as it:
                own.turn(it, 1 + HG)
                b, g = it // NG, it % NG

                def times_C(n):
                    dve.wait_ge(scan_done, it * NST + n + 1 + NDA)
                    dve.wait_ge(C_ps, it * NST + n + 1)
                    dve.wait_ge(y_acc, it * NST + n + 1)
                    v.tensor_tensor(hC[:, n % NHC], h[:, n % NH], ps_C[n % 2][:], ALU.mult).then_inc(hC_done, 1)

                def head_out(hh):
                    dve.wait_ge(pv_done, it * 16 + (hh + 1) * TB + NPT)
                    po = ps_o[:, 0:TB * (HD + 1)].rearrange("p (t d) -> p t d", d=HD + 1)
                    own.link(v.reciprocal(rden[:], po[:, :, HD]))
                    v.tensor_tensor(xa[:, bass.ts(b, TB), bass.ds(g * P + hh * HD, HD)], po[:, :, 0:HD],
                                    rden[:, :, None].broadcast_to([P, TB, HD]), ALU.mult).then_inc(o_ev, 1)

                for n in range(NST):
                    dve.wait_ge(hC_done, it * NST + (n if n else 2))
                    dve.wait_ge(dA_done, it * NST + n + 1)
                    dve.wait_ge(dBu_done, it * NST + n + 1 + NBS)
                    v.tensor_tensor_scan(h[:, n % NH], dA[:, n % NDA], dBu[:, n % NDA], 0.0,
                                         ALU.mult, ALU.add).then_inc(scan_done, 1)
                    if n >= 1:
                        times_C(n - 1)
                    if n == 0:
                        dve.wait_ge(q_ps, it + 1)
                        v.scalar_tensor_tensor(out=qf[:], in0=ps_misc[:], scalar=cqk[:, 0:1],
                                               in1=scale_row[:, bass.ts(b, S)], op0=ALU.mult, op1=ALU.mult).then_inc(q_ev, 1)
                        dve.wait_ge(q_ev, it + 1)
                        apart(dve, dve_steps)
                        v.tensor_copy(q16[:], qf[:]).then_inc(q16_done, 1)
                    if n == 1:
                        dve.wait_ge(k_ps, it + 1)
                        v.tensor_tensor(kf[:], ps_misc[:], scale_row[:, bass.ts(b, S)], ALU.mult).then_inc(k_ev, 1)
                        dve.wait_ge(k_ev, it + 1)
                        apart(dve, dve_steps)
                        v.tensor_copy(k16[:], kf[:]).then_inc(k16_done, 1)
                    for m in MAX_STEP[n]:
                        hh, qt = m // TB, m % TB
                        dve.wait_ge(s_ps, it * 16 + m + 1)
                        v.tensor_reduce(mx[:, qt, hh:hh + 1], ps_sc[m % 2][:, 0:(qt + 1) * P], AX, ALU.max).then_inc(max_done, 1)
                    if n == 5:
                        dve.wait_ge(max_done, it * 16 + 16)
                        own.link(v.tensor_copy(mhl[:, :, 0:HG], mx[:]))
                        v.tensor_tensor(mhl[:, :, HG:], mx[:], mhl[:, :, 0:HG], ALU.subtract).then_inc(mhl_done, 1)
                    if n in QZ_STEP:
                        for hh in QZ_STEP[n]:
                            if hh >= 2:
                                dve.wait_ge(st_ps, it * 16 + (hh - 1) * TB)
                            else:
                                dve.wait_ge(exp_done, it * 16 + 1)
                            v.tensor_scalar(qz[hh % 2][:], qf[:], headm[:, hh:hh + 1], None, ALU.mult).then_inc(qz_done, 1)
                    if n == 8:
                        relu((it + 1) % NG, it + 2, (it + 1) % 2)
                    if n in HEAD_STEP:
                        head_out(HEAD_STEP.index(n))
                times_C(NST - 1)
                head_out(HG - 1)
            own.ended(TURNS)
            dve.wait_ge(o_ev, TURNS * HG + 1)
            dve.sem_inc(main_done, 1)

            def stats(b, done):
                apart(dve, dve_steps)
                for t in range(TB):
                    own.mark(v.bn_stats(bn6[:, t], xa[:, b * TB + t]))
                dve.wait_ge(dve_own, own.at + own.n)
                apart(dve, dve_steps)
                for t in range(TB):
                    own.mark(v.bn_aggr(mv[:, t], bn6[:, t]))
                dve.wait_ge(dve_own, own.at + own.n)
                v.tensor_scalar(vare[:], mv[:, :, 1], EPS, None, ALU.add).then_inc(done, 1)

            with dve.Fori(0, NB) as b:
                own.turn(b, JOIN_DVE)
                rows = xa[:, bass.ts(b, TB)]
                own.link(v.tensor_reduce(amax[:], rows, AX, ALU.max, apply_absolute_value=True))
                own.link(v.tensor_scalar(clip[:], amax[:], 1e-5, None, ALU.max))
                own.link(v.reciprocal(qs[:], clip[:]))
                own.mark(v.tensor_scalar(tmp4[:], clip[:], 1.0 / 127, wstat[:, 1, 3:4], ALU.mult, ALU.mult))
                own.link(v.tensor_scalar(qs[:], qs[:], 127.0, None, ALU.mult))
                for t in range(TB):
                    own.link(v.tensor_scalar(j_m[:, t % 2], xa[:, b * TB + t], qs[:, t:t + 1], ROUND, ALU.mult, ALU.add))
                    v.tensor_scalar(j_q[:, t], j_m[:, t % 2], ROUND, 127.0, ALU.subtract, ALU.min).then_inc(j_quant, 1)
                dve.wait_ge(d_jx, b * 16 + 16)
                for t in range(TB):
                    dve.wait_ge(j_proj, b * TB + t + 1)
                    v.scalar_tensor_tensor(out=xa[:, b * TB + t], in0=bank[2 + t % 2][:], scalar=tmp4[:, t:t + 1],
                                           in1=j_x[:, t], op0=ALU.mult, op1=ALU.add).then_inc(j_x1, 1)
                dve.wait_ge(j_x1, b * TB + TB + 2)
                dve.sem_inc(j_used, 1)
                stats(b, j_stats)
                dve.wait_ge(j_rstd, b + 1)
                v.scalar_tensor_tensor(out=nmean[:], in0=mv[:, :, 0], scalar=-1.0, in1=rstd[:], op0=ALU.mult,
                                       op1=ALU.mult).then_inc(j_nm2, 1)
                dve.wait_ge(j_silu, b * TB + TB)
                for t in range(TB):
                    dve.wait_ge(j_zt, b * TB + t + 2)
                    v.tensor_tensor(j_g[:], bank[4][:], uy[:, b * TB + t], ALU.mult).then_inc(j_gate, 1)
                    dve.wait_ge(j_gate, b * TB + t + 2)
                    part = xa[:, bass.ts(b, TB), t * P:(t + 1) * P]
                    own.link(v.tensor_tensor(part, part, j_g[:].rearrange("p (t c) -> p t c", t=TB), ALU.add))
                stats(b, j_stats2)
                dve.wait_ge(j_rstd2, b + 1)
                v.scalar_tensor_tensor(out=nm2[:, bass.ts(b, TB)], in0=mv[:, :, 0], scalar=-1.0,
                                       in1=rs2[:, bass.ts(b, TB)], op0=ALU.mult, op1=ALU.mult).then_inc(j_nm2, 1)
                dve.wait_ge(j_lg, b + 1)
                apart(dve, dve_steps)
                v.tensor_copy(lg[:, bass.ts(b, TB)], bank[7][:, 0:TB * NE].rearrange("p (t e) -> p t e", e=NE)).then_inc(j_lgev, 1)
            own.ended(NB)

            def over_e(a):
                return a[:, :, None].broadcast_to([P, TT, NE])

            dve.wait_ge(j_lgev, NB + 1)
            dve.wait_ge(d_route, 16)
            own.link(v.tensor_reduce(m16[:], lg[:], AX, ALU.max))
            v.tensor_tensor(pr[:], lg[:], over_e(m16), ALU.subtract).then_inc(r_c, 1)
            dve.wait_ge(r_exp, 1)
            own.link(v.tensor_reduce(z16[:], pr[:], AX, ALU.add))
            own.link(v.reciprocal(m16[:], z16[:]))
            own.link(v.tensor_tensor(pr[:], pr[:], over_e(m16), ALU.mult))
            for t in range(TT):
                own.mark(v.max(top8[:, t], pr[:, t]))
            dve.wait_ge(dve_own, own.at)
            for t in range(TT):
                own.mark(v.max_index(ix8[:, t], top8[:, t], pr[:, t]))
            dve.wait_ge(dve_own, own.at)
            own.link(v.tensor_tensor(z16[:], top8[:, :, 0], top8[:, :, 1], ALU.add))
            own.link(v.tensor_scalar(z16[:], z16[:], 1e-20, None, ALU.add))
            own.link(v.reciprocal(m16[:], z16[:]))
            for j in range(2):
                own.mark(v.tensor_tensor(w12[:, j], top8[:, :, j], m16[:], ALU.mult))
                own.link(v.tensor_copy(ixf[:, j], ix8[:, :, j]))
                own.link(v.tensor_tensor(oh[:, j], iota_e, over_e(ixf[:, j]), ALU.is_equal))
            v.tensor_tensor(ohB[:], oh[:, 0], oh[:, 1], ALU.add).then_inc(r_mask, 1)
            dve.wait_ge(r_rank, 1)
            own.link(v.tensor_copy(cnt[:], bank[1][:, 0:TT * NE].rearrange("p (t e) -> p e t", e=NE)))
            own.link(v.tensor_tensor_scan(incl[:].rearrange("p e t -> p (e t)"), c_route[:, TT * NE:2 * TT * NE],
                                          cnt[:].rearrange("p e t -> p (e t)"), 0.0, ALU.mult, ALU.add))
            own.mark(v.tensor_tensor(cnt[:], incl[:], cnt[:], ALU.subtract))
            own.mark(v.memset(ones8[:], 1.0))
            own.link(v.tensor_scalar(nt[:, 0], incl[:, :, TT - 1], 1.0 / P, 127.0 / 256, ALU.mult, ALU.add))
            own.link(v.tensor_scalar(nt[:, 1], nt[:, 0], ROUND, None, ALU.add))
            own.link(v.tensor_scalar(nt[:, 0], nt[:, 1], ROUND, None, ALU.subtract))
            own.link(v.tensor_tensor_scan(nt[:, 2], ones8[:], nt[:, 0], 0.0, ALU.mult, ALU.add))
            own.link(v.tensor_tensor(nt[:, 3], nt[:, 2], nt[:, 0], ALU.subtract))
            own.link(v.tensor_scalar(nt[:, 3], nt[:, 3], float(P), None, ALU.mult))
            own.link(v.tensor_tensor(smat[:], bank[0][:, 0:TT * NE].rearrange("p (t e) -> p t e", e=NE),
                                     cnt[:].rearrange("p e t -> p t e"), ALU.add))
            own.link(v.tensor_tensor(smat[:], smat[:], nt[:, 3:4].broadcast_to([P, TT, NE]), ALU.add))
            for j in range(2):
                own.link(v.tensor_tensor(sx[:], smat[:], oh[:, j], ALU.mult))
                own.link(v.tensor_reduce(slf[:, j], sx[:], AX, ALU.add))
            own.mark(v.tensor_copy(slot[:], slf[:]))
            own.link(v.tensor_tensor(cmp[:], tile_no, nt[:, 2:3].broadcast_to([P, TILES, NE]), ALU.is_ge))
            own.link(v.tensor_reduce(tef[:], cmp[:], AX, ALU.add))
            v.tensor_scalar(tile_e[:], tef[:], float(NE - 1), None, ALU.min).then_inc(r_slots, 1)

            def act(j, c):
                dve.wait_ge(e_silu, j + 1)
                dve.wait_ge(e_at, j + 1)
                v.tensor_tensor(e_a[:, c], e_s[:, c], bank[3 + c][:, 0:FI], ALU.mult).then_inc(e_act, 1)

            def act_back(j, c):
                dve.wait_ge(e_at, j + 3)
                dve.wait_ge(e_d, j + 1)
                v.tensor_copy(e_aT[:, c, 0:FK - 1], bank[5][:, 0:(FK - 1) * P].rearrange("p (f c) -> p f c", c=P))
                v.tensor_copy(e_aT[0:FL, c, FK - 1], bank[5][0:FL, (FK - 1) * P:FK * P]).then_inc(e_atev, 1)

            def rows_out(j, c, half):
                dve.wait_ge(e_d, j + 3)
                dve.wait_ge(d_ey[c], half * 16 + 16)
                v.tensor_copy(e_y[:, c], bank[6 + c][:]).then_inc(e_dev, 1)

            for c in range(4):
                dve.wait_ge(sc_done[c], 8 * TT)
            act(0, 0)
            with dve.Fori(0, TILES // 2 - 1) as i:
                for c in range(2):
                    j = i * 2 + c + 1
                    act_back(j - 1, c)
                    act(j, 1 - c)
                    rows_out(j - 1, c, i)
            act_back(TILES - 2, 0)
            act(TILES - 1, 1)
            rows_out(TILES - 2, 0, TILES // 2 - 1)
            act_back(TILES - 1, 1)
            rows_out(TILES - 1, 1, TILES // 2 - 1)
            for t in range(TT):
                dve.wait_ge(g_row[t % 4], 32 * (t // 4 + 1))
                if t >= 4:
                    dve.wait_ge(d_out[t % 4], 16 * (t // 4))
                own.link(v.scalar_tensor_tensor(out=o_o[:, t % 4], in0=o_r[:, t % 4, 0], scalar=w12[:, 0, t:t + 1],
                                                in1=xa[:, t], op0=ALU.mult, op1=ALU.add))
                v.scalar_tensor_tensor(out=o_o[:, t % 4], in0=o_r[:, t % 4, 1], scalar=w12[:, 1, t:t + 1],
                                       in1=o_o[:, t % 4], op0=ALU.mult, op1=ALU.add).then_inc(o_done, 1)


def kernel(x, ctx_1024, L0_attn_w_q, L0_attn_w_k, L0_attn_w_v, L0_attn_w_o, L0_xattn_in_proj_w, L0_xattn_conv_w,
           L0_xattn_conv_b, L0_xattn_x_proj_w, L0_xattn_dt_proj_w, L0_xattn_dt_proj_b, L0_xattn_A_log, L0_xattn_D,
           L0_ffn_router_w, L0_ffn_w_gate, L0_ffn_w_up, L0_ffn_w_down):
    import numpy as np
    import concourse.bacc as bacc
    from concourse.bass_utils import run_bass_kernel_spmd

    f = np.float32
    a = {}
    a["x"] = np.asarray(x)
    a["ctx_t"] = np.asarray(ctx_1024).transpose(0, 2, 1)
    a["w_attn_t"] = np.stack([np.asarray(w).T for w in (L0_attn_w_q, L0_attn_w_k, L0_attn_w_v, L0_attn_w_o)])
    a["in_w_t"] = np.asarray(L0_xattn_in_proj_w).T
    a["ssm_par"] = np.concatenate([
        np.asarray(L0_xattn_conv_w), np.asarray(L0_xattn_conv_b)[:, None], np.asarray(L0_xattn_dt_proj_b)[:, None],
        np.asarray(L0_xattn_D)[:, None], np.asarray(L0_xattn_A_log)], axis=1)
    xp = np.asarray(L0_xattn_x_proj_w)
    a["xp_t"] = np.concatenate([xp[DR:], xp[DR:], xp[DR:], xp[:DR]]).T
    a["dt_w_t"] = np.concatenate([np.zeros((3 * NBC, E), f), np.asarray(L0_xattn_dt_proj_w).T])
    a["router_t"] = np.asarray(L0_ffn_router_w).T
    a["wg_t"] = np.asarray(L0_ffn_w_gate).transpose(0, 2, 1)
    a["wu_t"] = np.asarray(L0_ffn_w_up).transpose(0, 2, 1)
    a["wd_t"] = np.asarray(L0_ffn_w_down).transpose(0, 2, 1)
    i, j = np.arange(P)[:, None], np.arange(P)[None, :]
    a["k_square"] = np.stack([(i == j).astype(f), np.where(j > i, f(-1e30), f(0)), np.where(i > j, f(-1e30), f(0)),
                              (i < j).astype(f)])
    a["k_sel"] = np.tile(np.eye(NBC, dtype=f), (3, 1))
    sh = np.zeros((P, HG, P), f)
    for r in range(2 * HG):
        sh[r, r % HG] = -1
    a["k_shift"] = sh
    a["k_head"] = np.repeat(np.eye(HG, dtype=f), HD, axis=0)
    keep = np.ones((NE, TT), f)
    keep[:, 0] = 0
    row = np.concatenate([np.tile(np.arange(NE, dtype=f), TT), keep.ravel(), np.repeat(np.arange(TILES, dtype=f), NE)])
    a["k_route"] = np.tile(row, (P, 1))
    nc = bacc.Bacc("TRN2", target_bir_lowering=False, num_devices=1)
    arrays = {f"in_{n}": np.ascontiguousarray(v) for n, v in a.items()}
    args = {n: nc.dram_tensor(f"in_{n}", v.shape, mybir.dt.from_np(v.dtype), kind="ExternalInput").ap()
            for n, v in a.items()}
    out = nc.dram_tensor("out", (TOK, E), F32, kind="ExternalOutput").ap()
    decoder_layer(nc, **args, out=out)
    r = run_bass_kernel_spmd(nc, [arrays], core_ids=[0])
    return r.results[0]["out"].reshape(NB, S, E)
```

```python
from contextlib import ExitStack

import concourse.bass as bass
from concourse import mybir

P = 128
NB, S, E = 4, 512, 512
KT = E // P
TOK = NB * S
TT = TOK // P
TB = S // P
HD, HG = 32, 4
NG = 4
NST = 16
DCX, KC = 256, 2
DC = 4
DR = 16
NBC = 2 * NST
XR = 3 * NBC + DR
TURNS = NB * NG
NE, FI = 8, 352
FK = 3
FL = FI - 2 * P
TILES = (2 * TOK) // P + NE
EPS = 1e-5
ROUND = 1.5 * 2.0**23
KB = 1024
FRONT_DVE, JOIN_DVE = 37, 29

ALU = mybir.AluOpType
ACT = mybir.ActivationFunctionType
AX = mybir.AxisListType.X
F32 = mybir.dt.float32
BF16 = mybir.dt.bfloat16
I32 = mybir.dt.int32
U32 = mybir.dt.uint32

MAX_STEP = [[m for m in range(16) if 1 + m // 3 == n] for n in range(NST)]
AT_STEP = [[i for i in range(16) if 8 + i // 2 == n] for n in range(NST)]
QZ_STEP = {3: [0], 4: [1], 10: [2], 12: [3]}
HEAD_STEP = [11, 13, 15, NST]
MT_STEP = 7
NDA, NBS, NH, NHC, NPT = 4, 4, 3, 4, 3


class Chain:

    def __init__(self, eng, sem):
        self.eng, self.sem, self.done, self.at, self.n, self.per = eng, sem, 0, 0, 0, None

    def turn(self, i, per):
        self.at, self.n, self.per = i * per + self.done, 0, per

    def ended(self, turns):
        assert self.n == self.per, (self.n, self.per)
        self.done, self.n, self.per = self.done + turns * self.per, 0, None
        self.at = self.done

    def mark(self, ins):
        ins.then_inc(self.sem, 1)
        self.n += 1
        if self.per is None:
            self.done, self.at, self.n = self.done + 1, self.done + 1, 0
        return self.at + self.n

    def link(self, ins):
        self.eng.wait_ge(self.sem, self.mark(ins))


def apart(eng, steps):
    eng.sem_inc(steps, 1)


def decoder_layer(nc, x, ctx_t, w_attn_t, in_w_t, ssm_par, xp_t, dt_w_t, router_t, wg_t, wu_t, wd_t,
                  k_square, k_sel, k_shift, k_head, k_route, out):
    x_tok = x.rearrange("b (t p) c -> b p t c", p=P)
    with ExitStack() as ctx:
        base = (nc.sbuf_base + 63) // 64 * 64

        def at(name, offset, shape, dt):
            return nc.alloc_sbuf_tensor_at(name, shape, dt, offset=base + int(offset))

        def psum(name, shape, dt):
            return ctx.enter_context(nc.psum_tensor(name, shape, dt))

        def sem(name):
            return ctx.enter_context(nc.semaphore(name))

        o = 0

        def take(name, shape, dt, size):
            nonlocal o
            t = at(name, o, shape, dt)
            o += size
            return t

        delta = take("delta", [P, 2, S], F32, 4 * KB)
        du = take("du", [P, 2, S], F32, 4 * KB)
        dA = take("dA", [P, NDA, S], F32, NDA * 2 * KB)
        dBu = take("dBu", [P, NDA, S], F32, NDA * 2 * KB)
        Bs = take("Bs", [P, NBS, S], F32, NBS * 2 * KB)
        hC = take("hC", [P, NHC, S], F32, NHC * 2 * KB)
        qf = take("qf", [P, S], F32, 2 * KB)
        kf = take("kf", [P, S], F32, 2 * KB)
        q16 = take("q16", [P, S], BF16, KB)
        k16 = take("k16", [P, S], BF16, KB)
        vf = take("vf", [P, TB, HG, HD + 1], F32, 2112)
        pT = take("pT", [P, NPT, S], F32, NPT * 2 * KB)
        sp_ab = take("sp_ab", [P, S], F32, 2 * KB)
        sp_ex = take("sp_ex", [P, S], F32, 2 * KB)
        sp_u1 = take("sp_u1", [P, S], F32, 2 * KB)
        sp_one = take("sp_one", [P, 1], F32, 32)
        dt_wc = take("dt_wc", [XR, P], F32, 512)
        mT = take("mT", [P, S], BF16, KB)
        xqT = take("xqT", [P, KT, TOK], BF16, 16 * KB)
        scale_row = take("scale_row", [P, TOK], F32, 8 * KB)
        assert o <= 86 * KB, o
        f_junk = at("f_junk", 0, [P, KT, E], F32)
        f_xc = at("f_xc", 8 * KB, [P, TB, E], F32)
        f_xm = at("f_xm", 16 * KB, [P, TB, E], F32)
        f_xq = at("f_xq", 24 * KB, [P, TB, E], BF16)
        f_dg = at("f_dg", 28 * KB, [P, TB, P], F32)
        f_ctx = at("f_ctx", 30 * KB, [P, NB, KC, S], F32)
        f_xp = at("f_xp", 46 * KB, [P, NG, S + DC - 1], F32)
        f_cv = at("f_cv", 55 * KB, [P, 2, S], F32)
        f_r1 = at("f_r1", 134 * KB, [P, S], F32)
        uy = at("uy", 88 * KB, [P, TURNS, S], F32)
        w_stage = at("w_stage", 88 * KB, [P, 4, KT, E], F32)
        bcs = at("bcs", 120 * KB, [3 * NBC, TOK], BF16)
        dt_w = at("dt_w", 124 * KB, [XR, E], F32)
        in_w = at("in_w", 126 * KB, [P, KC, E], F32)
        h = at("h", 126 * KB, [P, NH, S], F32)
        xp_w = at("xp_w", 130 * KB, [P, NG, XR], F32)
        Du = at("Du", 134 * KB, [P, S], F32)
        qz = [at("qz0", 86 * KB, [P, S], F32), at("qz1", 132 * KB, [P, S], F32)]
        zeros = at("zeros", 132 * KB, [P, E], F32)
        j_z = at("j_z", 120 * KB, [P, TB, E], F32)
        j_x = at("j_x", 128 * KB, [P, TB, E], F32)
        wT = at("wT", 136 * KB, [P, 4, KT, E], BF16)
        j_q = at("j_q", 136 * KB, [P, TB, E], BF16)
        j_qT = at("j_qT", 140 * KB, [P, KT, S], BF16)
        j_m = at("j_m", 144 * KB, [P, 2, E], F32)
        j_g = at("j_g", 136 * KB, [P, E], F32)
        xa = at("xa", 152 * KB, [P, TT, E], F32)
        o = 184 * KB
        identF = take("identF", [P, P], F32, 512)
        identB = take("identB", [P, P], BF16, 256)
        maskQ = take("maskQ", [P, P], BF16, 256)
        maskK = take("maskK", [P, P], BF16, 256)
        triB = take("triB", [P, P], BF16, 256)
        onesF = take("onesF", [P, P], F32, 512)
        onesB = take("onesB", [P, P], BF16, 256)
        headm = take("headm", [P, HG], F32, 32)
        sel = take("sel", [3 * NBC, NBC, P], BF16, 8 * KB)
        shift = take("shift", [P, HG, P], BF16, KB)
        par = take("par", [P, NG, DC + 3 + NST], F32, 384)
        negA = take("negA", [P, NG, NST], F32, 256)
        wstat = take("wstat", [P, 3, 4], F32, 64)
        cqk = take("cqk", [P, 2], F32, 64)
        dq = take("dq", [P, TT], F32, 64)
        dqv = take("dqv", [P, TT], F32, 64)
        bn6 = take("bn6", [P, TB, 6], F32, 128)
        mv = take("mv", [P, TB, 2], F32, 64)
        nmean = take("nmean", [P, TB], F32, 32)
        vare = take("vare", [P, TB], F32, 32)
        halfs = take("halfs", [P, TB], F32, 32)
        rstd = take("rstd", [P, TB], F32, 32)
        amax = take("amax", [P, TB], F32, 32)
        clip = take("clip", [P, TB], F32, 32)
        qs = take("qs", [P, TB], F32, 32)
        tmp4 = take("tmp4", [P, TB], F32, 32)
        mx = take("mx", [P, TB, HG], F32, 64)
        mhl = take("mhl", [P, TB, 2 * HG], BF16, 64)
        rden = take("rden", [P, HG, TB], F32, 64)
        nm2 = take("nm2", [P, TT], F32, 64)
        rs2 = take("rs2", [P, TT], F32, 64)
        w12 = take("w12", [P, 2, TT], F32, 128)
        slot = take("slot", [P, 2, TT], I32, 128)
        tile_e = take("tile_e", [P, TILES], I32, 192)
        rw = take("rw", [P, KT, NE], F32, 128)
        assert o <= 198 * KB + 256, o / KB
        xd = at("xd", 199 * KB, [XR, TOK], F32)
        j_n = at("j_n", 199 * KB, [P, 2, E], F32)
        j_nT = at("j_nT", 203 * KB, [P, 2, E], F32)
        c_sq = at("c_sq", 84 * KB, [P, 4, P], F32)
        c_sel = at("c_sel", 86 * KB, [3 * NBC, NBC], F32)
        c_shift = at("c_shift", 199 * KB, [P, HG, P], F32)
        wg = at("wg", 0, [P, NE, KT, FI], F32)
        wu = at("wu", 44 * KB, [P, NE, KT, FI], F32)
        wd = at("wd", 88 * KB, [P, NE, FK, E], F32)
        e_x = at("e_x", 136 * KB, [P, 2, E], F32)
        e_xT = at("e_xT", 140 * KB, [P, 2, E], F32)
        e_s = at("e_s", 144 * KB, [P, 2, FI], F32)
        e_a = at("e_a", 147 * KB, [P, 2, FI], F32)
        e_aT = at("e_aT", 199 * KB, [P, 2, FK, P], F32)
        e_y = at("e_y", 203 * KB, [P, 2, E], F32)
        o_r = at("o_r", 0, [P, 4, 2, E], F32)
        o_o = at("o_o", 20 * KB, [P, 4, E], F32)
        j_n4 = at("j_n4", 199 * KB, [P, 4, E], F32)
        ro = 136 * KB
        lg = at("lg", 198 * KB + 256, [P, TT, NE], F32)
        o = ro
        pr = take("pr", [P, TT, NE], F32, 512)
        m16 = take("m16", [P, TT], F32, 64)
        z16 = take("z16", [P, TT], F32, 64)
        top8 = take("top8", [P, TT, 8], F32, 512)
        ix8 = take("ix8", [P, TT, 8], U32, 512)
        ixf = take("ixf", [P, 2, TT], F32, 128)
        oh = take("oh", [P, 2, TT, NE], F32, 1024)
        ohB = take("ohB", [P, TT, NE], BF16, 256)
        cnt = take("cnt", [P, NE, TT], F32, 512)
        keep = take("keep", [P, NE, TT], F32, 512)
        incl = take("incl", [P, NE, TT], F32, 512)
        nt = take("nt", [P, 4, NE], F32, 128)
        ones8 = take("ones8", [P, NE], F32, 32)
        smat = take("smat", [P, TT, NE], F32, 512)
        sx = take("sx", [P, TT, NE], F32, 512)
        slf = take("slf", [P, 2, TT], F32, 128)
        cmp = take("cmp", [P, TILES, NE], F32, 1280)
        tef = take("tef", [P, TILES], F32, 192)
        c_route = take("c_route", [P, TT * NE + NE * TT + TILES * NE], F32, 2304)
        assert o <= 148 * KB, o / KB
        iota_e = c_route[:, 0:TT * NE].rearrange("p (t e) -> p t e", e=NE)
        keep_c = c_route[:, TT * NE:2 * TT * NE].rearrange("p (e t) -> p e t", t=TT)
        tile_no = c_route[:, 2 * TT * NE:].rearrange("p (j e) -> p j e", e=NE)

        bank = [psum(f"bank{i}", [P, 512], F32) for i in range(8)]
        ps_misc, ps_sc, ps_o, ps_y, ps_C, ps_B = bank[0], bank[1:3], [bank[0], bank[3]], bank[4], bank[5:7], bank[7]
        ps_k, ps_v, ps_max = bank[1], bank[2], bank[1:4]
        ps_z = bank[4:7]

        slots_x = nc.dram_tensor("slots_x", (TILES * P, E), F32, kind="Internal").ap()
        slots_y = nc.dram_tensor("slots_y", (TILES * P, E), F32, kind="Internal").ap()

        d_const, d_ssm, d_ctx = sem("d_const"), sem("d_ssm"), sem("d_ctx")
        d_w = [sem(f"d_w{i}") for i in range(4)]
        d_x = [sem(f"d_x{i}") for i in range(NB)]
        d_zero, d_route = sem("d_zero"), sem("d_route")
        consts, zeroed = sem("consts"), sem("zeroed")
        wabs_done, wsum_done, wt_done = sem("wabs_done"), sem("wsum_done"), sem("wt_done")
        negA_done = sem("negA_done")
        dve_steps, act_steps, pe_steps = sem("dve_steps"), sem("act_steps"), sem("pe_steps")
        dve_own, act_own, pool_own = sem("dve_own"), sem("act_own"), sem("pool_own")
        f_stats, f_rstd, f_centred, f_quant, f_tr, f_trev, f_diag, f_row, f_rowev = map(
            sem, ("f_stats", "f_rstd", "f_centred", "f_quant", "f_tr", "f_trev", "f_diag", "f_row", "f_rowev"))
        f_in, f_inev, f_conv, f_silu, f_xd, f_xdev, f_split = map(
            sem, ("f_in", "f_inev", "f_conv", "f_silu", "f_xd", "f_xdev", "f_split"))
        dt_ps, dt_abs, dt_exp, dt_u1, dt_ln, dt_relu, dt_done, du_done = map(
            sem, ("dt_ps", "dt_abs", "dt_exp", "dt_u1", "dt_ln", "dt_relu", "dt_done", "du_done"))
        dA_done, B_ps, B_ev, dBu_done, scan_done, C_ps, hC_done, y_acc, y_ev, Du_done = map(
            sem, ("dA_done", "B_ps", "B_ev", "dBu_done", "scan_done", "C_ps", "hC_done", "y_acc",
                  "y_ev", "Du_done"))
        q_ps, q_ev, k_ps, k_ev, v_ps, v_ev, s_ps, max_done, mhl_done, mT_ps, mT_ev = map(
            sem, ("q_ps", "q_ev", "k_ps", "k_ev", "v_ps", "v_ev", "s_ps", "max_done", "mhl_done",
                  "mT_ps", "mT_ev"))
        q16_done, k16_done, qz_done = sem("q16_done"), sem("k16_done"), sem("qz_done")
        st_ps, exp_done, pv_done, o_ev, dtw_ev = map(sem, ("st_ps", "exp_done", "pv_done", "o_ev", "dtw_ev"))
        main_done = sem("main_done")
        d_jx, j_used, j_quant, j_tr, j_trev, j_proj, j_x1, j_stats, j_rstd, j_silu, j_zt, j_gate, j_x2 = map(
            sem, ("d_jx", "j_used", "j_quant", "j_tr", "j_trev", "j_proj", "j_x1", "j_stats", "j_rstd",
                  "j_silu", "j_zt", "j_gate", "j_x2"))
        j_stats2, j_rstd2, j_nm2, j_norm, j_nt, j_ntev, j_lg, j_lgev = map(
            sem, ("j_stats2", "j_rstd2", "j_nm2", "j_norm", "j_nt", "j_ntev", "j_lg", "j_lgev"))
        r_c, r_exp, r_mask, r_rank, r_slots, r_norm = map(
            sem, ("r_c", "r_exp", "r_mask", "r_rank", "r_slots", "r_norm"))
        sc_done = [sem(f"sc_done{i}") for i in range(4)]
        d_wg, d_wu, d_wd = sem("d_wg"), sem("d_wu"), sem("d_wd")
        d_ex = [sem("d_ex0"), sem("d_ex1")]
        d_ey = [sem("d_ey0"), sem("d_ey1")]
        e_tr, e_trev, e_g, e_silu, e_act, e_at, e_atev, e_d, e_dev = map(
            sem, ("e_tr", "e_trev", "e_g", "e_silu", "e_act", "e_at", "e_atev", "e_d", "e_dev"))
        vf_ones = sem("vf_ones")
        g_row = [sem(f"g_row{i}") for i in range(4)]
        o_done = sem("o_done")
        d_out = [sem(f"d_out{i}") for i in range(4)]

        block = ctx.enter_context(nc.Block())

        @block.sync
        def _(sp):
            for w in range(4):
                sp.dma_start(w_stage[:, w], w_attn_t[w].rearrange("(k p) o -> p k o", p=P)).then_inc(d_w[w], 16)
            sp.dma_start(c_sq[:], k_square.rearrange("k p c -> p k c")).then_inc(d_const, 16)
            sp.dma_start(c_sel[:], k_sel).then_inc(d_const, 16)
            sp.dma_start(c_shift[:], k_shift).then_inc(d_const, 16)
            sp.dma_start(headm[:], k_head).then_inc(d_const, 16)
            sp.dma_start(par[:], ssm_par.rearrange("(g p) c -> p g c", p=P)).then_inc(d_ssm, 16)
            sp.dma_start(in_w[:], in_w_t.rearrange("(k p) o -> p k o", p=P)).then_inc(d_ssm, 16)
            sp.dma_start(dt_w[:], dt_w_t).then_inc(d_ssm, 16)
            sp.dma_start(xp_w[:], xp_t.rearrange("(g p) c -> p g c", p=P)).then_inc(d_ssm, 16)
            sp.dma_start(rw[:], router_t.rearrange("(k p) e -> p k e", p=P)).then_inc(d_const, 16)
            for b in range(NB):
                sp.dma_start(xa[:, b * TB:(b + 1) * TB], x_tok[b]).then_inc(d_x[b], 16)
            sp.dma_start(f_ctx[:], ctx_t.rearrange("b (k p) l -> p (b k) l", p=P).rearrange(
                "p (b k) l -> p b k l", k=KC)).then_inc(d_ctx, 16)
            sp.wait_ge(zeroed, 1)
            sp.dma_start(slots_x.rearrange("(t p) c -> p t c", p=P),
                         zeros[:, None, :].broadcast_to([P, TILES, E])).then_inc(d_zero, 16)
            sp.wait_ge(main_done, 4)
            with sp.Fori(0, NB) as b:
                sp.wait_ge(j_used, b + 1)
                sp.dma_start(j_x[:], x_tok[b]).then_inc(d_jx, 16)
            sp.dma_start(wg[:], wg_t.rearrange("e (k p) i -> p (e k) i", p=P).rearrange(
                "p (e k) i -> p e k i", k=KT)).then_inc(d_wg, 16)
            sp.dma_start(wu[:], wu_t.rearrange("e (k p) i -> p (e k) i", p=P).rearrange(
                "p (e k) i -> p e k i", k=KT)).then_inc(d_wu, 16)
            sp.wait_ge(j_lgev, NB + 1)
            sp.dma_start(c_route[:], k_route).then_inc(d_route, 16)
            for c in range(2):
                sp.dma_start(wd[:, :, c], wd_t[:, c * P:(c + 1) * P, :].rearrange("e p o -> p e o")).then_inc(d_wd, 16)
            sp.dma_start(wd[0:FL, :, 2], wd_t[:, 2 * P:FI, :].rearrange("e p o -> p e o")).then_inc(d_wd, 16)
            for c in range(4):
                sp.wait_ge(sc_done[c], 8 * TT)
            slots_xt = slots_x.rearrange("(t p) c -> t p c", p=P)
            with sp.Fori(0, TILES // 2) as i:
                for c in range(2):
                    sp.wait_ge(e_tr, i * 2 + c + 1)
                    sp.dma_start(e_x[:, c], slots_xt[i * 2 + c]).then_inc(d_ex[c], 16)
            for c in range(4):
                sp.wait_ge(d_out[c], 16 * (TT // 4))

        @block.gpsimd
        def _(pool):
            own = Chain(pool, pool_own)
            nc.gpsimd.memset(zeros[:], 0.0).then_inc(zeroed, 1)
            nc.gpsimd.memset(onesF[:], 1.0).then_inc(consts, 1)
            nc.gpsimd.memset(onesB[:], 1.0).then_inc(consts, 1)
            own.link(nc.gpsimd.memset(halfs[:], -0.5))
            pool.sem_inc(dBu_done, NBS)
            with pool.Fori(0, NB) as b:
                pool.wait_ge(f_stats, b + 1)
                nc.gpsimd.tensor_tensor(rstd[:], vare[:], halfs[:], ALU.pow).then_inc(f_rstd, 1)

            def softplus_end(nx, par_, i, part):
                if part == 0:
                    pool.wait_ge(dt_u1, i)
                    own.link(nc.gpsimd.tensor_tensor(sp_ab[:], sp_u1[:], sp_one[:, 0:1].broadcast_to([P, S]), ALU.subtract))
                elif part == 1:
                    own.link(nc.gpsimd.tensor_tensor(sp_ex[:], sp_ex[:], sp_ab[:], ALU.subtract))
                elif part == 2:
                    pool.wait_ge(dt_relu, i)
                    own.link(nc.gpsimd.tensor_tensor(sp_ab[:], sp_ex[:], du[:, par_], ALU.add))
                elif part == 3:
                    pool.wait_ge(dt_ln, i)
                    own.link(nc.gpsimd.tensor_tensor(delta[:, par_], delta[:, par_], sp_ab[:], ALU.add))
                    pool.sem_inc(dt_done, 1)
                else:
                    nc.gpsimd.tensor_tensor(du[:, par_], delta[:, par_], uy[:, nx], ALU.mult).then_inc(du_done, 1)

            pool.wait_ge(f_split, NB)
            own.link(nc.gpsimd.memset(sp_one[:], 1.0))
            for part in range(5):
                softplus_end(0, 0, 1, part)
            with pool.Fori(0, TURNS // 2) as pair:
              own.turn(pair, 8)
              for c in range(2):
                it = pair * 2 + c
                pool.wait_ge(du_done, it + 1)
                for n in range(NST):
                    pool.wait_ge(B_ev, it * NST + n + 2)
                    pool.wait_ge(scan_done, it * NST + n + 1)
                    nc.gpsimd.tensor_tensor(dBu[:, n % NDA], du[:, c], Bs[:, n % NBS],
                                            ALU.mult).then_inc(dBu_done, 1)
                    if 7 <= n < 12:
                        softplus_end((it + 1) % TURNS, 1 - c, it + 2, n - 7)
            own.ended(TURNS // 2)
            pool.wait_ge(du_done, TURNS + 1)
            pool.sem_inc(main_done, 1)
            def rstd_1(b):
                pool.wait_ge(j_stats, b + 1)
                nc.gpsimd.tensor_tensor(rstd[:], vare[:], halfs[:], ALU.pow).then_inc(j_rstd, 1)

            def rstd_2(b):
                pool.wait_ge(j_stats2, b + 1)
                nc.gpsimd.tensor_tensor(rs2[:, bass.ts(b, TB)], vare[:], halfs[:], ALU.pow).then_inc(j_rstd2, 1)

            rstd_1(0)
            with pool.Fori(0, NB - 1) as b:
                rstd_2(b)
                rstd_1(b + 1)
            rstd_2(NB - 1)
            pool.wait_ge(r_slots, 1)
            pool.wait_ge(d_zero, 16)
            for t in range(TT):
                pool.wait_ge(r_norm, t + 1)
                for j in range(2):
                    pool.indirect_dma_start(
                        out=slots_x, out_offset=bass.IndirectOffsetOnAxis(ap=slot[:, j, t:t + 1], axis=0),
                        in_=j_n4[:, t % 4], in_offset=None).then_inc(sc_done[t % 4], 16)
            for c in range(2):
                pool.wait_ge(d_ey[c], 16 * (TILES // 2) + 16)
            for t in range(TT):
                if t >= 4:
                    pool.wait_ge(o_done, t - 3)
                for j in range(2):
                    pool.indirect_dma_start(
                        out=o_r[:, t % 4, j], out_offset=None, in_=slots_y,
                        in_offset=bass.IndirectOffsetOnAxis(ap=slot[:, j, t:t + 1], axis=0)).then_inc(g_row[t % 4], 16)

        @block.scalar
        def _(act):
            own = Chain(act, act_own)
            for free, count in ((B_ev, 1), (exp_done, 1), (y_ev, 1), (f_trev, 2), (f_rowev, 1), (f_inev, 2),
                                (f_xdev, 1), (f_silu, 2), (j_trev, 2), (j_ntev, 2), (e_trev, 1), (d_ey[0], 16),
                                (d_ey[1], 16)):
                act.sem_inc(free, count)
            for w in range(4):
                act.wait_ge(d_w[w], 16)
                own.link(nc.scalar.activation(f_junk[:], w_stage[:, w], ACT.Abs, accum_out=wstat[:, 0, w:w + 1]))
                act.sem_inc(wabs_done, 1)
            act.wait_ge(d_ssm, 64)
            own.link(nc.scalar.activation(negA[:], par[:, :, DC + 3:], ACT.Exp))
            nc.scalar.activation(negA[:], negA[:], ACT.Copy, scale=-1.0).then_inc(negA_done, 1)

            def take_in(b, g):
                act.wait_ge(f_in, b * NG + g + 1)
                nc.scalar.activation(f_xp[:, g, DC - 1:], bank[3 + g % 2][:], ACT.Copy).then_inc(f_inev, 1)

            def silu_u(b, g):
                act.wait_ge(f_conv, b * NG + g + 1)
                nc.scalar.activation(uy[:, b * NG + g], f_cv[:, g % 2], ACT.Silu).then_inc(f_silu, 1)

            def take_xd(b):
                act.wait_ge(f_xd, b + 1)
                nc.scalar.activation(xd[:, bass.ts(b, S)], bank[5][0:XR, :], ACT.Copy).then_inc(f_xdev, 1)

            def front(b, before):
                take_in(b, 0)
                take_in(b, 1)
                act.wait_ge(f_stats, b + 1)
                for t in range(TB):
                    nc.scalar.activation(f_xc[:, t], xa[:, b * TB + t], ACT.Identity,
                                         bias=nmean[:, t:t + 1]).then_inc(f_centred, 1)
                take_in(b, 2)
                take_in(b, 3)
                if before is not None:
                    take_xd(before)
                silu_u(b, 0)
                silu_u(b, 1)
                for t in range(TB):
                    act.wait_ge(f_tr, b * TB + t + 1)
                    nc.scalar.activation(xqT[:, :, bass.ds(b * S + t * P, P)],
                                         bank[t % 2].bitcast(BF16)[:, 0:E].rearrange("p (k c) -> p k c", k=KT),
                                         ACT.Copy).then_inc(f_trev, 1)
                act.wait_ge(f_row, b + 1)
                nc.scalar.activation(scale_row[:, bass.ts(b, S)], bank[2][:], ACT.Copy).then_inc(f_rowev, 1)
                silu_u(b, 2)
                silu_u(b, 3)

            front(0, None)
            with act.Fori(0, NB - 1) as i:
                front(i + 1, i)
            take_xd(NB - 1)

            dtb = DC + 1

            def softplus_mid(g, i, to, part):
                if part == 0:
                    act.wait_ge(dt_ps, i)
                    nc.scalar.activation(du[:, to], ps_misc[:], ACT.Relu, bias=par[:, g, dtb:dtb + 1]).then_inc(dt_relu, 1)
                    nc.scalar.activation(sp_ab[:], ps_misc[:], ACT.Abs, bias=par[:, g, dtb:dtb + 1]).then_inc(dt_abs, 1)
                elif part == 1:
                    act.wait_ge(dt_abs, i)
                    nc.scalar.activation(sp_ex[:], sp_ab[:], ACT.Exp, scale=-1.0).then_inc(dt_exp, 1)
                elif part == 2:
                    act.wait_ge(dt_exp, i)
                    nc.scalar.activation(sp_u1[:], sp_ex[:], ACT.Copy, bias=1.0).then_inc(dt_u1, 1)
                else:
                    act.wait_ge(dt_u1, i)
                    nc.scalar.activation(delta[:, to], sp_u1[:], ACT.Ln).then_inc(dt_ln, 1)

            act.wait_ge(f_split, NB)
            nc.scalar.preload_act_table_set("natural_log_exp_and_others")
            for part in range(4):
                softplus_mid(0, 1, 0, part)
            act.wait_ge(d_zero, 16)
            act.wait_ge(vf_ones, 1)
            act.wait_ge(B_ps, 1)
            nc.scalar.activation(Bs[:, 0], ps_B[:], ACT.Copy).then_inc(B_ev, 1)
            act.wait_ge(dt_done, 1)
            for n in range(2):
                nc.scalar.activation(dA[:, n], delta[:, 0], ACT.Exp, scale=negA[:, 0, n:n + 1]).then_inc(dA_done, 1)
            with act.Fori(0, TURNS) as it:
                b, g = it // NG, it % NG
                for n in range(NST):
                    act.wait_ge(B_ps, it * NST + n + 2)
                    act.wait_ge(dBu_done, it * NST + n + 2)
                    nc.scalar.activation(Bs[:, (n + 1) % NBS], ps_B[:], ACT.Copy).then_inc(B_ev, 1)
                    if n == NST - 2:
                        act.wait_ge(dt_done, it + 2)
                    act.wait_ge(scan_done, it * NST + n + 3)
                    nx = it if n < NST - 2 else it + 1
                    nc.scalar.activation(dA[:, (n + 2) % NDA], delta[:, nx % 2], ACT.Exp,
                                         scale=negA[:, nx % NG, (n + 2) % NST:(n + 2) % NST + 1]).then_inc(dA_done, 1)
                    if n == 0:
                        act.wait_ge(y_acc, it * NST + NHC)
                        nc.scalar.activation(Du[:], uy[:, it], ACT.Identity,
                                             scale=par[:, g, DC + 2:DC + 3]).then_inc(Du_done, 1)
                        act.wait_ge(q_ev, it + 1)
                        apart(act, act_steps)
                        nc.scalar.activation(q16[:], qf[:], ACT.Copy).then_inc(q16_done, 1)
                        act.wait_ge(k_ev, it + 1)
                        apart(act, act_steps)
                        nc.scalar.activation(k16[:], kf[:], ACT.Copy).then_inc(k16_done, 1)
                        act.wait_ge(v_ps, it + 1)
                        for t in range(TB):
                            ins = nc.scalar.activation(vf[:, t, :, 0:HD],
                                                       ps_v[:, t * P:(t + 1) * P].rearrange("p (h d) -> p h d", d=HD),
                                                       ACT.Identity, scale=dqv[:, bass.ds(b * TB + t, 1)])
                        ins.then_inc(v_ev, 1)
                    if n == 1:
                        nc.scalar.activation(dt_wc[:], dt_w[:, bass.ds((it + 1) % NG * P, P)], ACT.Copy).then_inc(dtw_ev, 1)
                    for hh in QZ_STEP.get(n, []):
                        act.wait_ge(st_ps, it * 16 + max(hh - 1, 0) * TB)
                        apart(act, act_steps)
                        nc.scalar.activation(qz[hh % 2][:], qf[:], ACT.Copy, scale=headm[:, hh:hh + 1]).then_inc(qz_done, 1)
                    if n == MT_STEP:
                        act.wait_ge(mT_ps, it + 1)
                        nc.scalar.activation(mT[0:2 * HG], ps_misc.bitcast(BF16)[0:2 * HG, 0:S], ACT.Copy).then_inc(mT_ev, 1)
                    if 4 <= n < 8:
                        softplus_mid((it + 1) % NG, it + 2, (it + 1) % 2, n - 4)
                    for i in AT_STEP[n]:
                        hh, kt = i // TB, i % TB
                        w = S - kt * P
                        act.wait_ge(st_ps, it * 16 + i + 1)
                        act.wait_ge(pv_done, it * 16 + (i + 1 if i else NPT))
                        nc.scalar.activation(pT[:, i % NPT, 0:w], ps_sc[i % 2][:, 0:w], ACT.Exp).then_inc(exp_done, 1)
                act.wait_ge(y_acc, it * NST + NST + NHC)
                apart(act, act_steps)
                nc.scalar.activation(uy[:, it], ps_y[:], ACT.Copy).then_inc(y_ev, 1)
            act.wait_ge(y_ev, TURNS + 1)
            act.sem_inc(main_done, 1)
            def rows_back(b, t):
                act.wait_ge(j_tr, b * TB + t + 1)
                nc.scalar.activation(j_qT[:, :, t * P:(t + 1) * P],
                                     bank[t % 2].bitcast(BF16)[:, 0:E].rearrange("p (k c) -> p k c", k=KT),
                                     ACT.Copy).then_inc(j_trev, 1)

            def gate(b, t):
                nc.scalar.activation(j_z[:, t], xa[:, b * TB + t], ACT.Silu, bias=nmean[:, t:t + 1],
                                     scale=rstd[:, t:t + 1]).then_inc(j_silu, 1)

            def norm(b):
                act.wait_ge(j_nm2, b * 2 + 2)

                def norm_back(t):
                    act.wait_ge(j_nt, b * TB + t + 3)
                    nc.scalar.activation(j_nT[:, t % 2], bank[5 + t % 2][:], ACT.Copy).then_inc(j_ntev, 1)

                for t in range(TB):
                    act.wait_ge(j_nt, b * TB + t + 1)
                    nc.scalar.activation(j_n[:, t % 2], xa[:, b * TB + t], ACT.Identity,
                                         bias=nm2[:, bass.ds(b * TB + t, 1)],
                                         scale=rs2[:, bass.ds(b * TB + t, 1)]).then_inc(j_norm, 1)
                    if t >= 1:
                        norm_back(t - 1)
                norm_back(TB - 1)

            for t in range(TB):
                rows_back(0, t)
            with act.Fori(0, NB - 1) as b:
                act.wait_ge(j_nm2, b * 2 + 1)
                act.wait_ge(j_zt, b * TB + 1)
                for t in range(TB):
                    gate(b, t)
                    rows_back(b + 1, t)
                norm(b)
            act.wait_ge(j_nm2, NB * 2 - 1)
            act.wait_ge(j_zt, (NB - 1) * TB + 1)
            for t in range(TB):
                gate(NB - 1, t)
            norm(NB - 1)
            act.wait_ge(r_c, 1)
            nc.scalar.activation(pr[:], pr[:], ACT.Exp).then_inc(r_exp, 1)
            act.wait_ge(r_slots, 1)
            for t in range(TT):
                if t >= 4:
                    act.wait_ge(sc_done[t % 4], 32 * (t // 4))
                nc.scalar.activation(j_n4[:, t % 4], xa[:, t], ACT.Identity, bias=nm2[:, t:t + 1],
                                     scale=rs2[:, t:t + 1]).then_inc(r_norm, 1)

            slots_yt = slots_y.rearrange("(t p) c -> t p c", p=P)

            def transposed(j, c):
                act.wait_ge(e_tr, j + 3)
                act.wait_ge(e_g, j + 1)
                nc.scalar.activation(e_xT[:, c], bank[0][:], ACT.Copy).then_inc(e_trev, 1)

            def silu(j, c):
                act.wait_ge(e_g, j + 3)
                act.wait_ge(e_act, j + 1)
                nc.scalar.activation(e_s[:, c], bank[1 + c][:, 0:FI], ACT.Silu).then_inc(e_silu, 1)

            def store(j, c):
                act.wait_ge(e_dev, j + 3)
                act.dma_start(slots_yt[j], e_y[:, c]).then_inc(d_ey[c], 16)

            transposed(0, 0)
            transposed(1, 1)
            silu(0, 0)
            with act.Fori(0, TILES // 2 - 1) as i:
                for c in range(2):
                    j = i * 2 + c + 1
                    transposed(j + 1, c)
                    silu(j, 1 - c)
                    store(j - 1, c)
            silu(TILES - 1, 1)
            store(TILES - 2, 0)
            store(TILES - 1, 1)
            for t in range(TT):
                act.wait_ge(o_done, t + 1)
                act.dma_start(out[t * P:(t + 1) * P, :], o_o[:, t % 4]).then_inc(d_out[t % 4], 16)

        @block.tensor
        def _(pe):
            mm = nc.tensor.matmul
            for free, count in ((y_acc, NHC), (pv_done, NPT), (j_zt, 1), (j_nt, 2), (e_tr, 2),
                                (e_g, 2), (e_at, 2), (e_d, 2)):
                pe.sem_inc(free, count)
            pe.wait_ge(consts, 3)
            pe.wait_ge(wabs_done, 4)
            mm(bank[6][:, 0:4], onesF[:], wstat[:, 0, :], start=True, stop=True).then_inc(wsum_done, 1)
            pe.wait_ge(d_ssm, 64)
            pe.wait_ge(d_ctx, 16)

            def project_in(b, g):
                pe.wait_ge(f_inev, b * NG + g + 1)
                for k in range(KC):
                    last = mm(bank[3 + g % 2][:], in_w[:, k, g * P:(g + 1) * P], f_ctx[:, b, k],
                              start=k == 0, stop=k == KC - 1)
                last.then_inc(f_in, 1)

            def project_xd(b):
                pe.wait_ge(f_silu, b * NG + NG + 2)
                pe.wait_ge(f_xdev, b + 1)
                for g in range(NG):
                    last = mm(bank[5][0:XR, :], xp_w[:, g], uy[:, b * NG + g], start=g == 0, stop=g == NG - 1)
                last.then_inc(f_xd, 1)

            def front(b, before):
                project_in(b, 0)
                project_in(b, 1)
                if before is not None:
                    project_xd(before)
                project_in(b, 2)
                project_in(b, 3)
                for t in range(TB):
                    pe.wait_ge(f_quant, b * TB + t + 1)
                    pe.wait_ge(f_trev, b * TB + t + 1)
                    for k in range(KT):
                        last = nc.tensor.transpose(bank[t % 2].bitcast(BF16)[:, k * P:(k + 1) * P],
                                                   f_xq[:, t, k * P:(k + 1) * P], identB[:])
                    last.then_inc(f_tr, 1)
                pe.wait_ge(f_diag, b + 1)
                pe.wait_ge(f_rowev, b + 1)
                mm(bank[2][:], onesF[:], f_dg[:].rearrange("p t c -> p (t c)"), start=True, stop=True).then_inc(f_row, 1)

            front(0, None)
            with pe.Fori(0, NB - 1) as i:
                front(i + 1, i)
            project_xd(NB - 1)

            pe.wait_ge(f_split, NB)
            pe.wait_ge(wt_done, 4)
            pe.wait_ge(vf_ones, 1)
            mm(ps_misc[:], dt_w[:, 0:P], xd[:, 0:S], start=True, stop=True).then_inc(dt_ps, 1)
            mm(ps_B[:], sel[:, 0], bcs[:, 0:S], start=True, stop=True).then_inc(B_ps, 1)
            with pe.Fori(0, TURNS) as it:
                b, g = it // NG, it % NG

                def accumulate(n):
                    pe.wait_ge(hC_done, it * NST + n + 3)
                    if n == 0:
                        pe.wait_ge(y_ev, it + 1)
                    for t in range(TB):
                        last = mm(ps_y[:, t * P:(t + 1) * P], hC[:, n % NHC, t * P:(t + 1) * P], identF[:],
                                  start=n == 0 and t == 0, stop=n == NST - 1, is_transpose=True, skip_group_check=True)
                    last.then_inc(y_acc, 1)

                def scores(m):
                    hh, qt = m // TB, m % TB
                    if m == 0:
                        pe.wait_ge(q16_done, it + 1)
                        pe.wait_ge(k16_done, it + 1)
                    elif m == 1:
                        pe.wait_ge(v_ev, it + 1)
                    elif m == 2:
                        pe.wait_ge(o_ev, it * HG + 1)
                    else:
                        pe.wait_ge(max_done, it * 16 + m - 2)
                    w = (qt + 1) * P
                    r = slice(hh * HD, (hh + 1) * HD)
                    mm(ps_max[m % 3][:, 0:w], q16[r, qt * P:(qt + 1) * P], k16[r, 0:w],
                       start=True, stop=False, skip_group_check=True)
                    mm(ps_max[m % 3][:, w - P:w], identB[:], maskQ[:], start=False, stop=True,
                       skip_group_check=True).then_inc(s_ps, 1)

                def scores_t(i):
                    hh, kt = i // TB, i % TB
                    if i == 0:
                        pe.wait_ge(max_done, it * 16 + 16)
                        pe.wait_ge(mT_ev, it + 1)
                    if i >= 2:
                        pe.wait_ge(exp_done, it * 16 + i)
                    w = S - kt * P
                    if kt == 0:
                        pe.wait_ge(qz_done, it * HG + hh + 1)
                    mm(ps_sc[i % 2][:, 0:w], kf[:, kt * P:(kt + 1) * P], qz[hh % 2][:, kt * P:S],
                       start=True, stop=False, skip_group_check=True)
                    mm(ps_sc[i % 2][:, 0:P], identB[:], maskK[:], start=False, stop=False, skip_group_check=True)
                    mm(ps_sc[i % 2][:, 0:w], shift[:, hh], mT[:, kt * P:S], start=False, stop=True,
                       skip_group_check=True).then_inc(st_ps, 1)

                def values(i):
                    hh, kt = i // TB, i % TB
                    pe.wait_ge(exp_done, it * 16 + i + 2)
                    if kt == 0 and hh >= 2:
                        pe.wait_ge(o_ev, it * HG + hh)
                    for qt in range(kt, TB):
                        last = mm(ps_o[hh % 2][:, qt * (HD + 1):(qt + 1) * (HD + 1)], pT[:, i % NPT, (qt - kt) * P:(qt - kt + 1) * P],
                                  vf[:, kt, hh], start=kt == 0 and qt == 0, stop=kt == qt, skip_group_check=True)
                    last.then_inc(pv_done, 1)

                for n in range(NST):
                    pe.wait_ge(B_ev, it * NST + n + 2)
                    b_n = b if n < NST - 1 else (it + 1) % TURNS // NG
                    mm(ps_B[:], sel[:, (n + 1) % NST], bcs[:, bass.ds(b_n * S, S)], start=True, stop=True).then_inc(B_ps, 1)
                    pe.wait_ge(hC_done, it * NST + n + 1)
                    mm(ps_C[n % 2][:], sel[:, NST + n], bcs[:, bass.ds(b * S, S)], start=True, stop=True).then_inc(C_ps, 1)
                    if n >= 2:
                        accumulate(n - 2)
                    if n == 4:
                        pe.wait_ge(Du_done, it + 1)
                        for t in range(TB):
                            mm(ps_y[:, t * P:(t + 1) * P], Du[:, t * P:(t + 1) * P], identF[:], start=False, stop=False,
                               is_transpose=True, skip_group_check=True)
                    if n == 0:
                        pe.wait_ge(dt_abs, it + 1)
                        pe.wait_ge(dt_relu, it + 1)
                        pe.wait_ge(o_ev, it * HG)
                        for k in range(KT):
                            last = mm(ps_misc[:], wT[:, 0, k, bass.ds(g * P, P)], xqT[:, k, bass.ds(b * S, S)],
                                      start=k == 0, stop=k == KT - 1)
                        last.then_inc(q_ps, 1)
                        pe.wait_ge(exp_done, it * 16 + 1)
                        for k in range(KT):
                            last = mm(ps_k[:], wT[:, 1, k, bass.ds(g * P, P)], xqT[:, k, bass.ds(b * S, S)],
                                      start=k == 0, stop=k == KT - 1)
                        last.then_inc(k_ps, 1)
                        for t in range(TB):
                            for k in range(KT):
                                last = mm(ps_v[:, t * P:(t + 1) * P], xqT[:, k, bass.ds(b * S + t * P, P)],
                                          wT[:, 2, k, bass.ds(g * P, P)], start=k == 0, stop=k == KT - 1)
                        last.then_inc(v_ps, 1)
                    for m in MAX_STEP[n]:
                        scores(m)
                    if n == MT_STEP:
                        pe.wait_ge(mhl_done, it + 1)
                        pe.wait_ge(dt_abs, it + 2)
                        for t in range(TB):
                            last = nc.tensor.transpose(ps_misc.bitcast(BF16)[0:2 * HG, t * P:(t + 1) * P],
                                                       mhl[:, t], identB[:])
                        last.then_inc(mT_ps, 1)
                    for i in AT_STEP[n]:
                        scores_t(i)
                        if i >= 1:
                            values(i - 1)
                    if n == 3:
                        pe.wait_ge(q_ev, it + 1)
                        pe.wait_ge(dtw_ev, it + 1)
                        mm(ps_misc[:], dt_wc[:], xd[:, bass.ds((it + 1) % TURNS // NG * S, S)],
                           start=True, stop=True).then_inc(dt_ps, 1)
                accumulate(14)
                values(15)
                accumulate(15)

            pe.wait_ge(y_acc, TURNS * NST + NHC)
            pe.sem_inc(main_done, 1)
            def rows_t(b):
                for t in range(TB):
                    pe.wait_ge(j_quant, b * TB + t + 1)
                    pe.wait_ge(j_trev, b * TB + t + 1)
                    for k in range(KT):
                        last = nc.tensor.transpose(bank[t % 2].bitcast(BF16)[:, k * P:(k + 1) * P],
                                                   j_q[:, t, k * P:(k + 1) * P], identB[:])
                    last.then_inc(j_tr, 1)

            def project(b):
                for t in range(TB):
                    pe.wait_ge(j_trev, b * TB + t + 3)
                    pe.wait_ge(j_x1, b * TB + t + 1)
                    for k in range(KT):
                        last = mm(bank[2 + t % 2][:], j_qT[:, k, t * P:(t + 1) * P], wT[:, 3, k],
                                  start=k == 0, stop=k == KT - 1)
                    last.then_inc(j_proj, 1)

            def gate_t(b):
                for t in range(TB):
                    pe.wait_ge(j_silu, b * TB + t + 1)
                    pe.wait_ge(j_gate, b * TB + (t - 1 if t == 3 else 1))
                    for k in range(KT):
                        last = nc.tensor.transpose(ps_z[t % 3][:, k * P:(k + 1) * P], j_z[:, t, k * P:(k + 1) * P],
                                                   identF[:])
                    last.then_inc(j_zt, 1)

            def route(b):
                def logits(t):
                    pe.wait_ge(j_ntev, b * TB + t + 3)
                    for k in range(KT):
                        last = mm(bank[7][:, t * NE:(t + 1) * NE], j_nT[:, t % 2, k * P:(k + 1) * P], rw[:, k],
                                  start=k == 0, stop=k == KT - 1)
                    return last

                for t in range(TB):
                    pe.wait_ge(j_norm, b * TB + t + 1)
                    pe.wait_ge(j_ntev, b * TB + t + 1)
                    for k in range(KT):
                        last = nc.tensor.transpose(bank[5 + t % 2][:, k * P:(k + 1) * P], j_n[:, t % 2, k * P:(k + 1) * P],
                                                   identF[:])
                    last.then_inc(j_nt, 1)
                    if t == 1:
                        pe.wait_ge(j_lgev, b + 1)
                    if t >= 1:
                        logits(t - 1)
                logits(TB - 1).then_inc(j_lg, 1)

            rows_t(0)
            project(0)
            with pe.Fori(0, NB - 1) as b:
                rows_t(b + 1)
                gate_t(b)
                project(b + 1)
                route(b)
            gate_t(NB - 1)
            route(NB - 1)
            pe.wait_ge(r_mask, 1)
            mm(bank[0][:, 0:TT * NE], triB[:], ohB[:].rearrange("p t e -> p (t e)"), start=True, stop=True)
            mm(bank[1][:, 0:TT * NE], onesB[:], ohB[:].rearrange("p t e -> p (t e)"),
               start=True, stop=True).then_inc(r_rank, 1)
            pe.wait_ge(r_slots, 1)

            def rows_t(j, c, half):
                pe.wait_ge(d_ex[c], half * 16 + 16)
                pe.wait_ge(e_trev, j + 1)
                for k in range(KT):
                    last = nc.tensor.transpose(bank[0][:, k * P:(k + 1) * P], e_x[:, c, k * P:(k + 1) * P], identF[:])
                last.then_inc(e_tr, 1)

            def gate_up(j, c):
                pe.wait_ge(e_trev, j + 2)
                pe.wait_ge(e_act, j + 1)
                apart(pe, pe_steps)
                e = pe.value_load(tile_e[0:1, bass.ds(j, 1)], min_val=0, max_val=NE - 1)
                for k in range(KT):
                    mm(bank[1 + c][:, 0:FI], e_xT[:, c, k * P:(k + 1) * P], wg[:, e, k], start=k == 0, stop=k == KT - 1)
                for k in range(KT):
                    last = mm(bank[3 + c][:, 0:FI], e_xT[:, c, k * P:(k + 1) * P], wu[:, e, k],
                              start=k == 0, stop=k == KT - 1)
                last.then_inc(e_g, 1)

            def act_t(j, c):
                pe.wait_ge(e_act, j + 3)
                pe.wait_ge(e_atev, j + 1)
                for f in range(FK):
                    w = P if f < FK - 1 else FL
                    last = nc.tensor.transpose(bank[5][0:w, f * P:(f + 1) * P], e_a[:, c, f * P:f * P + w], identF[:])
                last.then_inc(e_at, 1)

            def down(j, c):
                pe.wait_ge(e_atev, j + 2)
                pe.wait_ge(e_dev, j + 1)
                apart(pe, pe_steps)
                e = pe.value_load(tile_e[0:1, bass.ds(j, 1)], min_val=0, max_val=NE - 1)
                for f in range(FK):
                    w = P if f < FK - 1 else FL
                    last = mm(bank[6 + c][:], e_aT[0:w, c, f], wd[0:w, e, f], start=f == 0, stop=f == FK - 1)
                last.then_inc(e_d, 1)

            rows_t(0, 0, 0)
            rows_t(1, 1, 0)
            pe.wait_ge(d_wg, 16)
            pe.wait_ge(d_wu, 16)
            gate_up(0, 0)
            pe.wait_ge(d_wd, 48)
            with pe.Fori(0, TILES // 2 - 1) as i:
                for c in range(2):
                    j = i * 2 + c + 1
                    rows_t(j + 1, c, i + 1)
                    act_t(j - 1, c)
                    gate_up(j, 1 - c)
                    down(j - 1, c)
            act_t(TILES - 2, 0)
            gate_up(TILES - 1, 1)
            down(TILES - 2, 0)
            act_t(TILES - 1, 1)
            down(TILES - 1, 1)

        @block.vector
        def _(dve):
            own = Chain(dve, dve_own)
            v = nc.vector
            for free, count in ((scan_done, NDA), (hC_done, 2), (o_ev, 1), (j_x1, 2), (j_gate, 1), (j_used, 1),
                                (j_lgev, 1), (e_act, 2), (e_atev, 1), (e_dev, 2)):
                dve.sem_inc(free, count)
            own.link(v.memset(f_xp[:, :, 0:DC - 1], 0.0))
            dve.wait_ge(d_const, 80)
            v.tensor_copy(identF[:], c_sq[:, 0])
            v.tensor_copy(identB[:], c_sq[:, 0])
            v.tensor_copy(maskQ[:], c_sq[:, 1])
            v.tensor_copy(maskK[:], c_sq[:, 2])
            v.tensor_copy(triB[:], c_sq[:, 3])
            v.tensor_copy(shift[:], c_shift[:])
            v.tensor_copy(sel[:], c_sel[:, :, None].broadcast_to([3 * NBC, NBC, P])).then_inc(consts, 1)
            dve.wait_ge(wsum_done, 1)
            own.link(v.tensor_scalar(wstat[:, 1], bank[6][:, 0:4], 1.0 / (E * E), 1e-5, ALU.mult, ALU.max))
            own.link(v.reciprocal(wstat[:, 2], wstat[:, 1]))
            own.link(v.tensor_scalar(cqk[:, 0:1], wstat[:, 1, 0:1], wstat[:, 1, 1:2], HD ** -0.5, ALU.mult, ALU.mult))
            for w in range(4):
                own.link(v.tensor_scalar(w_stage[:, w], w_stage[:, w], wstat[:, 2, w:w + 1], 1.0, ALU.mult, ALU.min))
                own.link(v.tensor_scalar(w_stage[:, w], w_stage[:, w], -1.0, ROUND, ALU.max, ALU.add))
                v.tensor_scalar(wT[:, w], w_stage[:, w], ROUND, None, ALU.subtract).then_inc(wt_done, 1)

            dve.wait_ge(wt_done, 4)
            for bb in range(NB):
                dve.wait_ge(d_x[bb], 16)
            def stats_x(b):
                for t in range(TB):
                    own.mark(v.bn_stats(bn6[:, t], xa[:, b * TB + t]))
                dve.wait_ge(dve_own, own.at + own.n)
                apart(dve, dve_steps)
                for t in range(TB):
                    own.mark(v.bn_aggr(mv[:, t], bn6[:, t]))
                dve.wait_ge(dve_own, own.at + own.n)
                own.mark(v.tensor_scalar(nmean[:], mv[:, :, 0], -1.0, None, ALU.mult))
                v.tensor_scalar(vare[:], mv[:, :, 1], EPS, None, ALU.add).then_inc(f_stats, 1)

            def quantise_x(b):
                dve.wait_ge(f_centred, b * TB + TB)
                own.link(v.tensor_reduce(amax[:], f_xc[:], AX, ALU.max, apply_absolute_value=True))
                dve.wait_ge(f_rstd, b + 1)
                own.link(v.tensor_tensor(clip[:], amax[:], rstd[:], ALU.mult))
                own.link(v.tensor_scalar(clip[:], clip[:], 1e-5, None, ALU.max))
                own.mark(v.tensor_scalar(dq[:, bass.ts(b, TB)], clip[:], 1.0 / 127, None, ALU.mult))
                own.mark(v.tensor_scalar(dqv[:, bass.ts(b, TB)], clip[:], 1.0 / 127, wstat[:, 1, 2:3], ALU.mult, ALU.mult))
                own.link(v.reciprocal(tmp4[:], clip[:]))
                own.link(v.scalar_tensor_tensor(out=qs[:], in0=tmp4[:], scalar=127.0, in1=rstd[:], op0=ALU.mult, op1=ALU.mult))
                for t in range(TB):
                    own.link(v.tensor_scalar(f_xm[:, t], f_xc[:, t], qs[:, t:t + 1], ROUND, ALU.mult, ALU.add))
                    v.tensor_scalar(f_xq[:, t], f_xm[:, t], ROUND, 127.0, ALU.subtract, ALU.min).then_inc(f_quant, 1)
                for t in range(TB):
                    last = v.tensor_scalar(f_dg[:, t], identF[:], dq[:, bass.ds(b * TB + t, 1)], None, ALU.mult)
                last.then_inc(f_diag, 1)

            def convolve(b, g):
                dve.wait_ge(f_inev, b * NG + g + 3)
                dve.wait_ge(f_silu, b * NG + g + 1)
                own.link(v.tensor_scalar(f_cv[:, g % 2], f_xp[:, g, 0:S], par[:, g, 0:1], par[:, g, DC:DC + 1],
                                         ALU.mult, ALU.add))
                for j in range(1, DC):
                    ins = v.scalar_tensor_tensor(out=f_cv[:, g % 2], in0=f_xp[:, g, j:j + S], scalar=par[:, g, j:j + 1],
                                                 in1=f_cv[:, g % 2], op0=ALU.mult, op1=ALU.add)
                    if j < DC - 1:
                        own.link(ins)
                ins.then_inc(f_conv, 1)

            def split_bc(b):
                dve.wait_ge(f_xdev, b + 2)
                apart(dve, dve_steps)
                cols = bass.ts(b, S)
                own.link(v.tensor_copy(bcs[:, cols], xd[0:3 * NBC, cols]))
                own.link(v.tensor_tensor(f_r1[0:3 * NBC], xd[0:3 * NBC, cols], bcs[:, cols], ALU.subtract))
                apart(dve, dve_steps)
                own.mark(v.tensor_copy(bcs[NBC:2 * NBC, cols], f_r1[NBC:2 * NBC]))
                own.link(v.tensor_copy(bcs[2 * NBC:, cols], f_r1[2 * NBC:3 * NBC]))
                own.link(v.tensor_tensor(f_r1[2 * NBC:3 * NBC], f_r1[2 * NBC:3 * NBC], bcs[2 * NBC:, cols], ALU.subtract))
                apart(dve, dve_steps)
                v.tensor_copy(bcs[2 * NBC:, cols], f_r1[2 * NBC:3 * NBC]).then_inc(f_split, 1)

            def front(b, before):
                stats_x(b)
                convolve(b, 0)
                convolve(b, 1)
                quantise_x(b)
                if before is not None:
                    split_bc(before)
                convolve(b, 2)
                convolve(b, 3)

            front(0, None)
            with dve.Fori(0, NB - 1) as i:
                own.turn(i, FRONT_DVE)
                front(i + 1, i)
            own.ended(NB - 1)
            split_bc(NB - 1)

            dve.wait_ge(f_split, NB)
            v.memset(mT[:], 0.0)
            v.memset(vf[:, :, :, HD:], 1.0).then_inc(vf_ones, 1)
            with dve.Fori(0, TURNS) as it:
                own.turn(it, 1 + HG)
                b, g = it // NG, it % NG

                def times_C(n):
                    dve.wait_ge(scan_done, it * NST + n + 1 + NDA)
                    dve.wait_ge(C_ps, it * NST + n + 1)
                    dve.wait_ge(y_acc, it * NST + n + 1)
                    v.tensor_tensor(hC[:, n % NHC], h[:, n % NH], ps_C[n % 2][:], ALU.mult).then_inc(hC_done, 1)

                def head_out(hh):
                    dve.wait_ge(pv_done, it * 16 + (hh + 1) * TB + NPT)
                    po = ps_o[hh % 2][:, 0:TB * (HD + 1)].rearrange("p (t d) -> p t d", d=HD + 1)
                    own.link(v.reciprocal(rden[:, hh], po[:, :, HD]))
                    v.tensor_tensor(xa[:, bass.ts(b, TB), bass.ds(g * P + hh * HD, HD)], po[:, :, 0:HD],
                                    rden[:, hh, :, None].broadcast_to([P, TB, HD]), ALU.mult).then_inc(o_ev, 1)

                for n in range(NST):
                    dve.wait_ge(hC_done, it * NST + (n if n else 2))
                    dve.wait_ge(dA_done, it * NST + n + 1)
                    dve.wait_ge(dBu_done, it * NST + n + 1 + NBS)
                    v.tensor_tensor_scan(h[:, n % NH], dA[:, n % NDA], dBu[:, n % NDA], 0.0,
                                         ALU.mult, ALU.add).then_inc(scan_done, 1)
                    if n >= 1:
                        times_C(n - 1)
                    if n == 0:
                        dve.wait_ge(q_ps, it + 1)
                        v.scalar_tensor_tensor(out=qf[:], in0=ps_misc[:], scalar=cqk[:, 0:1],
                                               in1=scale_row[:, bass.ts(b, S)], op0=ALU.mult, op1=ALU.mult).then_inc(q_ev, 1)
                        dve.wait_ge(k_ps, it + 1)
                        v.tensor_tensor(kf[:], ps_k[:], scale_row[:, bass.ts(b, S)], ALU.mult).then_inc(k_ev, 1)
                    for m in MAX_STEP[n]:
                        hh, qt = m // TB, m % TB
                        dve.wait_ge(s_ps, it * 16 + m + 1)
                        v.tensor_reduce(mx[:, qt, hh:hh + 1], ps_max[m % 3][:, 0:(qt + 1) * P], AX, ALU.max).then_inc(max_done, 1)
                    if n == 6:
                        dve.wait_ge(max_done, it * 16 + 16)
                        own.link(v.tensor_copy(mhl[:, :, 0:HG], mx[:]))
                        v.tensor_tensor(mhl[:, :, HG:], mx[:], mhl[:, :, 0:HG], ALU.subtract).then_inc(mhl_done, 1)
                    if n in HEAD_STEP:
                        head_out(HEAD_STEP.index(n))
                times_C(NST - 1)
                head_out(HG - 1)
            own.ended(TURNS)
            dve.wait_ge(o_ev, TURNS * HG + 1)
            dve.sem_inc(main_done, 1)

            def stats(b, done):
                apart(dve, dve_steps)
                for t in range(TB):
                    own.mark(v.bn_stats(bn6[:, t], xa[:, b * TB + t]))
                dve.wait_ge(dve_own, own.at + own.n)
                apart(dve, dve_steps)
                for t in range(TB):
                    own.mark(v.bn_aggr(mv[:, t], bn6[:, t]))
                dve.wait_ge(dve_own, own.at + own.n)
                v.tensor_scalar(vare[:], mv[:, :, 1], EPS, None, ALU.add).then_inc(done, 1)

            def quantise(b):
                own.link(v.tensor_reduce(amax[:], xa[:, bass.ts(b, TB)], AX, ALU.max, apply_absolute_value=True))
                own.link(v.tensor_scalar(clip[:], amax[:], 1e-5, None, ALU.max))
                own.link(v.reciprocal(qs[:], clip[:]))
                own.mark(v.tensor_scalar(tmp4[:], clip[:], 1.0 / 127, wstat[:, 1, 3:4], ALU.mult, ALU.mult))
                own.link(v.tensor_scalar(qs[:], qs[:], 127.0, None, ALU.mult))
                for t in range(TB):
                    own.link(v.tensor_scalar(j_m[:, t % 2], xa[:, b * TB + t], qs[:, t:t + 1], ROUND, ALU.mult, ALU.add))
                    v.tensor_scalar(j_q[:, t], j_m[:, t % 2], ROUND, 127.0, ALU.subtract, ALU.min).then_inc(j_quant, 1)

            def residual(b):
                dve.wait_ge(d_jx, b * 16 + 16)
                for t in range(TB):
                    dve.wait_ge(j_proj, b * TB + t + 1)
                    v.scalar_tensor_tensor(out=xa[:, b * TB + t], in0=bank[2 + t % 2][:], scalar=tmp4[:, t:t + 1],
                                           in1=j_x[:, t], op0=ALU.mult, op1=ALU.add).then_inc(j_x1, 1)
                dve.wait_ge(j_x1, b * TB + TB + 2)
                dve.sem_inc(j_used, 1)
                stats(b, j_stats)
                dve.wait_ge(j_rstd, b + 1)
                v.scalar_tensor_tensor(out=nmean[:], in0=mv[:, :, 0], scalar=-1.0, in1=rstd[:], op0=ALU.mult,
                                       op1=ALU.mult).then_inc(j_nm2, 1)

            def gated(b):
                dve.wait_ge(j_silu, b * TB + TB)
                for t in range(TB):
                    dve.wait_ge(j_zt, b * TB + t + 2)
                    v.tensor_tensor(j_g[:], ps_z[t % 3][:], uy[:, b * TB + t], ALU.mult).then_inc(j_gate, 1)
                    dve.wait_ge(j_gate, b * TB + t + 2)
                    part = xa[:, bass.ts(b, TB), t * P:(t + 1) * P]
                    own.link(v.tensor_tensor(part, part, j_g[:].rearrange("p (t c) -> p t c", t=TB), ALU.add))
                stats(b, j_stats2)
                dve.wait_ge(j_rstd2, b + 1)
                v.scalar_tensor_tensor(out=nm2[:, bass.ts(b, TB)], in0=mv[:, :, 0], scalar=-1.0,
                                       in1=rs2[:, bass.ts(b, TB)], op0=ALU.mult, op1=ALU.mult).then_inc(j_nm2, 1)

            def take_logits(b):
                dve.wait_ge(j_lg, b + 1)
                apart(dve, dve_steps)
                v.tensor_copy(lg[:, bass.ts(b, TB)], bank[7][:, 0:TB * NE].rearrange("p (t e) -> p t e", e=NE)).then_inc(j_lgev, 1)

            quantise(0)
            residual(0)
            with dve.Fori(0, NB - 1) as b:
                own.turn(b, JOIN_DVE)
                quantise(b + 1)
                gated(b)
                residual(b + 1)
                take_logits(b)
            own.ended(NB - 1)
            gated(NB - 1)
            take_logits(NB - 1)

            def over_e(a):
                return a[:, :, None].broadcast_to([P, TT, NE])

            dve.wait_ge(j_lgev, NB + 1)
            dve.wait_ge(d_route, 16)
            own.link(v.tensor_reduce(m16[:], lg[:], AX, ALU.max))
            v.tensor_tensor(pr[:], lg[:], over_e(m16), ALU.subtract).then_inc(r_c, 1)
            dve.wait_ge(r_exp, 1)
            own.link(v.tensor_reduce(z16[:], pr[:], AX, ALU.add))
            own.link(v.reciprocal(m16[:], z16[:]))
            own.link(v.tensor_tensor(pr[:], pr[:], over_e(m16), ALU.mult))
            for t in range(TT):
                own.mark(v.max(top8[:, t], pr[:, t]))
            dve.wait_ge(dve_own, own.at)
            for t in range(TT):
                own.mark(v.max_index(ix8[:, t], top8[:, t], pr[:, t]))
            dve.wait_ge(dve_own, own.at)
            own.link(v.tensor_tensor(z16[:], top8[:, :, 0], top8[:, :, 1], ALU.add))
            own.link(v.tensor_scalar(z16[:], z16[:], 1e-20, None, ALU.add))
            own.link(v.reciprocal(m16[:], z16[:]))
            for j in range(2):
                own.mark(v.tensor_tensor(w12[:, j], top8[:, :, j], m16[:], ALU.mult))
                own.link(v.tensor_copy(ixf[:, j], ix8[:, :, j]))
                own.link(v.tensor_tensor(oh[:, j], iota_e, over_e(ixf[:, j]), ALU.is_equal))
            v.tensor_tensor(ohB[:], oh[:, 0], oh[:, 1], ALU.add).then_inc(r_mask, 1)
            dve.wait_ge(r_rank, 1)
            own.link(v.tensor_copy(cnt[:], bank[1][:, 0:TT * NE].rearrange("p (t e) -> p e t", e=NE)))
            own.link(v.tensor_tensor_scan(incl[:].rearrange("p e t -> p (e t)"), c_route[:, TT * NE:2 * TT * NE],
                                          cnt[:].rearrange("p e t -> p (e t)"), 0.0, ALU.mult, ALU.add))
            own.mark(v.tensor_tensor(cnt[:], incl[:], cnt[:], ALU.subtract))
            own.mark(v.memset(ones8[:], 1.0))
            own.link(v.tensor_scalar(nt[:, 0], incl[:, :, TT - 1], 1.0 / P, 127.0 / 256, ALU.mult, ALU.add))
            own.link(v.tensor_scalar(nt[:, 1], nt[:, 0], ROUND, None, ALU.add))
            own.link(v.tensor_scalar(nt[:, 0], nt[:, 1], ROUND, None, ALU.subtract))
            own.link(v.tensor_tensor_scan(nt[:, 2], ones8[:], nt[:, 0], 0.0, ALU.mult, ALU.add))
            own.link(v.tensor_tensor(nt[:, 3], nt[:, 2], nt[:, 0], ALU.subtract))
            own.link(v.tensor_scalar(nt[:, 3], nt[:, 3], float(P), None, ALU.mult))
            own.link(v.tensor_tensor(smat[:], bank[0][:, 0:TT * NE].rearrange("p (t e) -> p t e", e=NE),
                                     cnt[:].rearrange("p e t -> p t e"), ALU.add))
            own.link(v.tensor_tensor(smat[:], smat[:], nt[:, 3:4].broadcast_to([P, TT, NE]), ALU.add))
            for j in range(2):
                own.link(v.tensor_tensor(sx[:], smat[:], oh[:, j], ALU.mult))
                own.link(v.tensor_reduce(slf[:, j], sx[:], AX, ALU.add))
            own.mark(v.tensor_copy(slot[:], slf[:]))
            own.link(v.tensor_tensor(cmp[:], tile_no, nt[:, 2:3].broadcast_to([P, TILES, NE]), ALU.is_ge))
            own.link(v.tensor_reduce(tef[:], cmp[:], AX, ALU.add))
            v.tensor_scalar(tile_e[:], tef[:], float(NE - 1), None, ALU.min).then_inc(r_slots, 1)

            def act(j, c):
                dve.wait_ge(e_silu, j + 1)
                dve.wait_ge(e_at, j + 1)
                v.tensor_tensor(e_a[:, c], e_s[:, c], bank[3 + c][:, 0:FI], ALU.mult).then_inc(e_act, 1)

            def act_back(j, c):
                dve.wait_ge(e_at, j + 3)
                dve.wait_ge(e_d, j + 1)
                v.tensor_copy(e_aT[:, c, 0:FK - 1], bank[5][:, 0:(FK - 1) * P].rearrange("p (f c) -> p f c", c=P))
                v.tensor_copy(e_aT[0:FL, c, FK - 1], bank[5][0:FL, (FK - 1) * P:FK * P]).then_inc(e_atev, 1)

            def rows_out(j, c, half):
                dve.wait_ge(e_d, j + 3)
                dve.wait_ge(d_ey[c], half * 16 + 16)
                v.tensor_copy(e_y[:, c], bank[6 + c][:]).then_inc(e_dev, 1)

            for c in range(4):
                dve.wait_ge(sc_done[c], 8 * TT)
            act(0, 0)
            with dve.Fori(0, TILES // 2 - 1) as i:
                for c in range(2):
                    j = i * 2 + c + 1
                    act_back(j - 1, c)
                    act(j, 1 - c)
                    rows_out(j - 1, c, i)
            act_back(TILES - 2, 0)
            act(TILES - 1, 1)
            rows_out(TILES - 2, 0, TILES // 2 - 1)
            act_back(TILES - 1, 1)
            rows_out(TILES - 1, 1, TILES // 2 - 1)
            for t in range(TT):
                dve.wait_ge(g_row[t % 4], 32 * (t // 4 + 1))
                if t >= 4:
                    dve.wait_ge(d_out[t % 4], 16 * (t // 4))
                own.link(v.scalar_tensor_tensor(out=o_o[:, t % 4], in0=o_r[:, t % 4, 0], scalar=w12[:, 0, t:t + 1],
                                                in1=xa[:, t], op0=ALU.mult, op1=ALU.add))
                v.scalar_tensor_tensor(out=o_o[:, t % 4], in0=o_r[:, t % 4, 1], scalar=w12[:, 1, t:t + 1],
                                       in1=o_o[:, t % 4], op0=ALU.mult, op1=ALU.add).then_inc(o_done, 1)


def kernel(x, ctx_1024, L0_attn_w_q, L0_attn_w_k, L0_attn_w_v, L0_attn_w_o, L0_xattn_in_proj_w, L0_xattn_conv_w,
           L0_xattn_conv_b, L0_xattn_x_proj_w, L0_xattn_dt_proj_w, L0_xattn_dt_proj_b, L0_xattn_A_log, L0_xattn_D,
           L0_ffn_router_w, L0_ffn_w_gate, L0_ffn_w_up, L0_ffn_w_down):
    import numpy as np
    import concourse.bacc as bacc
    from concourse.bass_utils import run_bass_kernel_spmd

    f = np.float32
    a = {}
    a["x"] = np.asarray(x)
    a["ctx_t"] = np.asarray(ctx_1024).transpose(0, 2, 1)
    a["w_attn_t"] = np.stack([np.asarray(w).T for w in (L0_attn_w_q, L0_attn_w_k, L0_attn_w_v, L0_attn_w_o)])
    a["in_w_t"] = np.asarray(L0_xattn_in_proj_w).T
    a["ssm_par"] = np.concatenate([
        np.asarray(L0_xattn_conv_w), np.asarray(L0_xattn_conv_b)[:, None], np.asarray(L0_xattn_dt_proj_b)[:, None],
        np.asarray(L0_xattn_D)[:, None], np.asarray(L0_xattn_A_log)], axis=1)
    xp = np.asarray(L0_xattn_x_proj_w)
    a["xp_t"] = np.concatenate([xp[DR:], xp[DR:], xp[DR:], xp[:DR]]).T
    a["dt_w_t"] = np.concatenate([np.zeros((3 * NBC, E), f), np.asarray(L0_xattn_dt_proj_w).T])
    a["router_t"] = np.asarray(L0_ffn_router_w).T
    a["wg_t"] = np.asarray(L0_ffn_w_gate).transpose(0, 2, 1)
    a["wu_t"] = np.asarray(L0_ffn_w_up).transpose(0, 2, 1)
    a["wd_t"] = np.asarray(L0_ffn_w_down).transpose(0, 2, 1)
    i, j = np.arange(P)[:, None], np.arange(P)[None, :]
    a["k_square"] = np.stack([(i == j).astype(f), np.where(j > i, f(-1e30), f(0)), np.where(i > j, f(-1e30), f(0)),
                              (i < j).astype(f)])
    a["k_sel"] = np.tile(np.eye(NBC, dtype=f), (3, 1))
    sh = np.zeros((P, HG, P), f)
    for r in range(2 * HG):
        sh[r, r % HG] = -1
    a["k_shift"] = sh
    a["k_head"] = np.repeat(np.eye(HG, dtype=f), HD, axis=0)
    keep = np.ones((NE, TT), f)
    keep[:, 0] = 0
    row = np.concatenate([np.tile(np.arange(NE, dtype=f), TT), keep.ravel(), np.repeat(np.arange(TILES, dtype=f), NE)])
    a["k_route"] = np.tile(row, (P, 1))
    nc = bacc.Bacc("TRN2", target_bir_lowering=False, num_devices=1)
    arrays = {f"in_{n}": np.ascontiguousarray(v) for n, v in a.items()}
    args = {n: nc.dram_tensor(f"in_{n}", v.shape, mybir.dt.from_np(v.dtype), kind="ExternalInput").ap()
            for n, v in a.items()}
    out = nc.dram_tensor("out", (TOK, E), F32, kind="ExternalOutput").ap()
    decoder_layer(nc, **args, out=out)
    r = run_bass_kernel_spmd(nc, [arrays], core_ids=[0])
    return r.results[0]["out"].reshape(NB, S, E)
```

```python
from contextlib import ExitStack

import concourse.bass as bass
from concourse import mybir

P = 128
NB, S, E = 4, 512, 512
KT = E // P
TOK = NB * S
TT = TOK // P
TB = S // P
HD, HG = 32, 4
NG = 4
NST = 16
DCX = 256
KC = DCX // P
DC = 4
DR = 16
NBC = 2 * NST
XR = 3 * NBC + DR
TURNS = NB * NG
NE, FI = 8, 352
FK = 3
FL = FI - 2 * P
TILES = (2 * TOK) // P + NE - 1
LAST = TILES - 1
EPS = 1e-5
ROUND = 1.5 * 2.0**23
KB = 1024
W_UP = 16.0
CHUNKS = 2 * NE
FRONT_DVE, JOIN_DVE = 27, 29

ALU = mybir.AluOpType
ACT = mybir.ActivationFunctionType
AX = mybir.AxisListType.X
F32 = mybir.dt.float32
BF16 = mybir.dt.bfloat16
I32 = mybir.dt.int32
U32 = mybir.dt.uint32
F16 = mybir.dt.float16

MAX_STEP = [[m for m in range(16) if 1 + m // 3 == n] for n in range(NST)]
AT_STEP = [[i for i in range(16) if 8 + i // 2 == n] for n in range(NST)]
QZ_STEP = {3: [0], 4: [1], 10: [2], 12: [3]}
HEAD_STEP = [11, 13, 14, NST]
SUM_FIRST, SUM_LAST = 9, 14
NSUM = SUM_LAST - SUM_FIRST + 1
NACC = NST - NSUM
DELTA_STEP = [7, 9, 10, 12, 13]
MT_STEP = 7
NDA, NBS, NH, NHC, NPT = 4, 4, 3, 4, 3


class Chain:

    def __init__(self, eng, sem):
        self.eng, self.sem, self.done, self.at, self.n, self.per = eng, sem, 0, 0, 0, None

    def turn(self, i, per):
        self.at, self.n, self.per = i * per + self.done, 0, per

    def ended(self, turns):
        assert self.n == self.per, (self.n, self.per)
        self.done, self.n, self.per = self.done + turns * self.per, 0, None
        self.at = self.done

    def mark(self, ins):
        ins.then_inc(self.sem, 1)
        self.n += 1
        if self.per is None:
            self.done, self.at, self.n = self.done + 1, self.done + 1, 0
        return self.at + self.n

    def link(self, ins):
        self.eng.wait_ge(self.sem, self.mark(ins))


def apart(eng, steps):
    eng.sem_inc(steps, 1)


def decoder_layer(nc, x, ctx_t, w_attn_t, in_w_t, ssm_par, xp_t, dt_w_t, router_t, wg_t, wu_t, wd_t,
                  k_square, k_sel, k_shift, k_head, k_route, out):
    x_tok = x.rearrange("b (t p) c -> b p t c", p=P)
    with ExitStack() as ctx:
        base = (nc.sbuf_base + 63) // 64 * 64

        def at(name, offset, shape, dt):
            return nc.alloc_sbuf_tensor_at(name, shape, dt, offset=base + int(offset))

        def psum(name, shape, dt):
            return ctx.enter_context(nc.psum_tensor(name, shape, dt))

        def sem(name):
            return ctx.enter_context(nc.semaphore(name))

        o = 0

        def take(name, shape, dt, size):
            nonlocal o
            t = at(name, o, shape, dt)
            o += size
            return t

        delta = take("delta", [P, 2, S], F32, 4 * KB)
        du = take("du", [P, 2, S], F32, 4 * KB)
        dA = take("dA", [P, NDA, S], F32, NDA * 2 * KB)
        dBu = take("dBu", [P, NDA, S], F32, NDA * 2 * KB)
        Bs = take("Bs", [P, NBS, S], F32, NBS * 2 * KB)
        hC = take("hC", [P, NHC, S], F32, NHC * 2 * KB)
        qf = take("qf", [P, S], F32, 2 * KB)
        kf = take("kf", [P, S], F32, 2 * KB)
        q16 = take("q16", [P, S], BF16, KB)
        k16 = take("k16", [P, S], BF16, KB)
        vf = take("vf", [P, TB, HG, HD + 1], F32, 2112)
        pT = take("pT", [P, NPT, S], F32, NPT * 2 * KB)
        sp_ab = take("sp_ab", [P, S], F32, 2 * KB)
        sp_ex = take("sp_ex", [P, S], F32, 2 * KB)
        sp_u1 = take("sp_u1", [P, S], F32, 2 * KB)
        sp_one = take("sp_one", [P, 1], F32, 32)
        dt_wc = take("dt_wc", [XR, P], F32, 512)
        mT = take("mT", [P, S], BF16, KB)
        xqT = take("xqT", [P, KT, TOK], BF16, 16 * KB)
        scale_row = take("scale_row", [P, TOK], F32, 8 * KB)
        assert o <= 86 * KB, o
        f_junk = at("f_junk", 0, [P, KT, E], F32)
        f_xc = at("f_xc", 8 * KB, [P, TB, E], F32)
        f_xm = at("f_xm", 16 * KB, [P, TB, E], F32)
        f_xq = at("f_xq", 24 * KB, [P, TB, E], BF16)
        f_dg = at("f_dg", 28 * KB, [P, TB, P], F32)
        f_ctx = at("f_ctx", 30 * KB, [P, NB, KC, S], F32)
        f_xp = at("f_xp", 46 * KB, [P, NG, S + DC - 1], F32)
        f_cv = at("f_cv", 55 * KB, [P, 2, S], F32)
        f_r1 = at("f_r1", 134 * KB, [P, S], F32)
        uy = at("uy", 88 * KB, [P, TURNS, S], F32)
        w_stage = at("w_stage", 88 * KB, [P, 4, KT, E], F32)
        bcs = at("bcs", 120 * KB, [3 * NBC, TOK], BF16)
        dt_w = at("dt_w", 124 * KB, [XR, E], F32)
        in_w = at("in_w", 126 * KB, [P, KC, E], F32)
        h = at("h", 126 * KB, [P, NH, S], F32)
        xp_w = at("xp_w", 130 * KB, [P, NG, XR], F32)
        Du = at("Du", 134 * KB, [P, S], F32)
        qz = [at("qz0", 86 * KB, [P, S], F32), at("qz1", 132 * KB, [P, S], F32)]
        zeros = at("zeros", 132 * KB, [P, E], F32)
        j_z = at("j_z", 120 * KB, [P, TB, E], F32)
        j_x = at("j_x", 128 * KB, [P, TB, E], F32)
        wT = at("wT", 136 * KB, [P, 4, KT, E], BF16)
        j_q = at("j_q", 136 * KB, [P, TB, E], BF16)
        j_qT = at("j_qT", 140 * KB, [P, KT, S], BF16)
        j_m = at("j_m", 144 * KB, [P, 2, E], F32)
        j_g = at("j_g", 144 * KB, [P, E], F32)
        xa = at("xa", 152 * KB, [P, TT, E], F32)
        o = 184 * KB
        identF = take("identF", [P, P], F32, 512)
        identB = take("identB", [P, P], BF16, 256)
        maskQ = take("maskQ", [P, P], BF16, 256)
        maskK = take("maskK", [P, P], BF16, 256)
        triB = take("triB", [P, P], BF16, 256)
        onesF = take("onesF", [P, P], F32, 512)
        onesB = take("onesB", [P, P], BF16, 256)
        headm = take("headm", [P, HG], F32, 32)
        sel = take("sel", [3 * NBC, NBC, P], BF16, 8 * KB)
        shift = take("shift", [P, HG, P], BF16, KB)
        par = take("par", [P, NG, DC + 3 + NST], F32, 384)
        negA = take("negA", [P, NG, NST], F32, 256)
        wstat = take("wstat", [P, 3, 4], F32, 64)
        cqk = take("cqk", [P, 2], F32, 64)
        dq = take("dq", [P, TT], F32, 64)
        dqv = take("dqv", [P, TT], F32, 64)
        bn6 = take("bn6", [P, TB, 6], F32, 128)
        mv = take("mv", [P, TB, 2], F32, 64)
        nmean = take("nmean", [P, TB], F32, 32)
        vare = take("vare", [P, TB], F32, 32)
        halfs = take("halfs", [P, TB], F32, 32)
        rstd = take("rstd", [P, TB], F32, 32)
        amax = take("amax", [P, TB], F32, 32)
        clip = take("clip", [P, TB], F32, 32)
        qs = take("qs", [P, TB], F32, 32)
        tmp4 = take("tmp4", [P, TB], F32, 32)
        mx = take("mx", [P, TB, HG], F32, 64)
        mhl = take("mhl", [P, TB, 2 * HG], BF16, 64)
        rden = take("rden", [P, HG, TB], F32, 64)
        nm2 = take("nm2", [P, TT], F32, 64)
        rs2 = take("rs2", [P, TT], F32, 64)
        w12 = take("w12", [P, 2, TT], F32, 128)
        slot = take("slot", [P, 2, TT], I32, 128)
        tile_e = take("tile_e", [P, TILES], I32, 192)
        rw = take("rw", [P, KT, NE], F32, 128)
        assert o <= 198 * KB + 256, o / KB
        xd = at("xd", 199 * KB, [XR, TOK], F32)
        j_n = at("j_n", 199 * KB, [P, 2, E], F32)
        j_nT = at("j_nT", 203 * KB, [P, 2, E], F32)
        c_sq = at("c_sq", 84 * KB, [P, 4, P], F32)
        c_sel = at("c_sel", 86 * KB, [3 * NBC, NBC], F32)
        c_shift = at("c_shift", 199 * KB, [P, HG, P], F32)
        wg = at("wg", 0, [P, NE, KT, FI], F32)
        wu = at("wu", 44 * KB, [P, NE, KT, FI], F32)
        wd = at("wd", 88 * KB, [P, NE, FK, E], F32)
        e_x = at("e_x", 136 * KB, [P, 2, E], F32)
        wg16 = at("wg16", 0, [P, NE, KT, FI, 2], F16)
        wu16 = at("wu16", 44 * KB, [P, NE, KT, FI, 2], F16)
        w_hi = at("w_hi", 146 * KB, [P, 2, KT, FI], F16)
        e_xT = at("e_xT", 140 * KB, [P, 2, 2, E], F16)
        e_s = at("e_s", 144 * KB, [P, 2, FI], F32)
        e_a = at("e_a", 147 * KB, [P, 2, FI], F32)
        e_aT = at("e_aT", 199 * KB, [P, 2, FK, P], F32)
        e_y = at("e_y", 203 * KB, [P, 2, E], F32)
        o_r = at("o_r", 0, [P, 4, 2, E], F32)
        o_o = at("o_o", 20 * KB, [P, 4, E], F32)
        j_n4 = at("j_n4", 199 * KB, [P, 4, E], F32)
        ro = 136 * KB
        lg = at("lg", 198 * KB + 256, [P, TT, NE], F32)
        o = ro
        pr = take("pr", [P, TT, NE], F32, 512)
        m16 = take("m16", [P, TT], F32, 64)
        z16 = take("z16", [P, TT], F32, 64)
        top8 = take("top8", [P, TT, 8], F32, 512)
        ix8 = take("ix8", [P, TT, 8], U32, 512)
        ixf = take("ixf", [P, 2, TT], F32, 128)
        oh = take("oh", [P, 2, TT, NE], F32, 1024)
        ohB = take("ohB", [P, TT, NE], BF16, 256)
        cnt = take("cnt", [P, NE, TT], F32, 512)
        keep = take("keep", [P, NE, TT], F32, 512)
        incl = take("incl", [P, NE, TT], F32, 512)
        nt = take("nt", [P, 4, NE], F32, 128)
        ones8 = take("ones8", [P, NE], F32, 32)
        smat = take("smat", [P, TT, NE], F32, 512)
        sx = take("sx", [P, TT, NE], F32, 512)
        slf = take("slf", [P, 2, TT], F32, 128)
        cmp = take("cmp", [P, TILES, NE], F32, 1280)
        tef = take("tef", [P, TILES], F32, 192)
        c_route = take("c_route", [P, TT * NE + NE * TT + TILES * NE], F32, 2304)
        assert o <= 146 * KB, o / KB
        iota_e = c_route[:, 0:TT * NE].rearrange("p (t e) -> p t e", e=NE)
        keep_c = c_route[:, TT * NE:2 * TT * NE].rearrange("p (e t) -> p e t", t=TT)
        tile_no = c_route[:, 2 * TT * NE:].rearrange("p (j e) -> p j e", e=NE)

        bank = [psum(f"bank{i}", [P, 512], F32) for i in range(8)]
        ps_misc, ps_sc, ps_o, ps_y, ps_C, ps_B = bank[0], bank[1:3], [bank[0], bank[3]], bank[4], bank[5:7], bank[7]
        ps_k, ps_v, ps_max = bank[1], bank[2], bank[1:4]
        ps_z = bank[4:7]

        slots_x = nc.dram_tensor("slots_x", (TILES * P, E), F32, kind="Internal").ap()
        slots_y = nc.dram_tensor("slots_y", (TILES * P, E), F32, kind="Internal").ap()

        d_const, d_ssm, d_ctx = sem("d_const"), sem("d_ssm"), [sem("d_ctx0"), sem("d_ctx1")]
        d_w = [sem(f"d_w{i}") for i in range(4)]
        d_x = [sem(f"d_x{i}") for i in range(NB)]
        d_zero, d_route = sem("d_zero"), sem("d_route")
        consts, zeroed = sem("consts"), sem("zeroed")
        wabs_done, wsum_done, wt_done = sem("wabs_done"), sem("wsum_done"), sem("wt_done")
        dve_steps, act_steps, pool_steps = sem("dve_steps"), sem("act_steps"), sem("pool_steps")
        dve_own, act_own, pool_own = sem("dve_own"), sem("act_own"), sem("pool_own")
        f_stats, f_rstd, f_centred, f_quant, f_tr, f_trev, f_diag, f_row, f_rowev = map(
            sem, ("f_stats", "f_rstd", "f_centred", "f_quant", "f_tr", "f_trev", "f_diag", "f_row", "f_rowev"))
        f_in, f_inev, f_conv, f_silu, f_xd, f_xdev, f_split = map(
            sem, ("f_in", "f_inev", "f_conv", "f_silu", "f_xd", "f_xdev", "f_split"))
        f_tap, bc_1, bc_2, rest_1, rest_2 = map(sem, ("f_tap", "bc_1", "bc_2", "rest_1", "rest_2"))
        dt_ps, dt_abs, dt_exp, dt_u1, dt_ln, dt_relu, dt_done, du_done = map(
            sem, ("dt_ps", "dt_abs", "dt_exp", "dt_u1", "dt_ln", "dt_relu", "dt_done", "du_done"))
        dA_done, B_ps, B_ev, dBu_done, scan_done, C_ps, hC_done, y_acc, y_ev, Du_done = map(
            sem, ("dA_done", "B_ps", "B_ev", "dBu_done", "scan_done", "C_ps", "hC_done", "y_acc",
                  "y_ev", "Du_done"))
        q_ps, q_ev, k_ps, k_ev, v_ps, v_ev, s_ps, max_done, mhl_done, mT_ps, mT_ev = map(
            sem, ("q_ps", "q_ev", "k_ps", "k_ev", "v_ps", "v_ev", "s_ps", "max_done", "mhl_done",
                  "mT_ps", "mT_ev"))
        sum_done = sem("sum_done")
        q16_done, k16_done, qz_done = sem("q16_done"), sem("k16_done"), sem("qz_done")
        st_ps, exp_done, pv_done, o_ev, dtw_ev = map(sem, ("st_ps", "exp_done", "pv_done", "o_ev", "dtw_ev"))
        main_done = sem("main_done")
        d_jx, j_used, j_quant, j_tr, j_trev, j_proj, j_x1, j_stats, j_rstd, j_silu, j_zt, j_gate = map(
            sem, ("d_jx", "j_used", "j_quant", "j_tr", "j_trev", "j_proj", "j_x1", "j_stats", "j_rstd",
                  "j_silu", "j_zt", "j_gate"))
        j_stats2, j_rstd2, j_nm2, j_norm, j_nt, j_ntev, j_lg, j_lgev = map(
            sem, ("j_stats2", "j_rstd2", "j_nm2", "j_norm", "j_nt", "j_ntev", "j_lg", "j_lgev"))
        r_c, r_exp, r_mask, r_rank, r_slots, r_norm = map(
            sem, ("r_c", "r_exp", "r_mask", "r_rank", "r_slots", "r_norm"))
        sc_done = [sem(f"sc_done{i}") for i in range(4)]
        d_wg, d_wu, d_wd = sem("d_wg"), sem("d_wu"), sem("d_wd")
        d_ex = [sem("d_ex0"), sem("d_ex1")]
        d_ey = [sem("d_ey0"), sem("d_ey1")]
        hi_done, w_split, e_hi = sem("hi_done"), sem("w_split"), sem("e_hi")
        e_tr, e_trev, e_g, e_silu, e_act, e_at, e_atev, e_d, e_dev = map(
            sem, ("e_tr", "e_trev", "e_g", "e_silu", "e_act", "e_at", "e_atev", "e_d", "e_dev"))
        vf_ones = sem("vf_ones")
        g_row = [sem(f"g_row{i}") for i in range(4)]
        o_done = sem("o_done")
        d_out = [sem(f"d_out{i}") for i in range(4)]

        block = ctx.enter_context(nc.Block())

        @block.sync
        def _(sp):
            def load_w(w):
                sp.dma_start(w_stage[:, w], w_attn_t[w].rearrange("(k p) o -> p k o", p=P)).then_inc(d_w[w], 16)

            def load_x(b):
                sp.dma_start(xa[:, b * TB:(b + 1) * TB], x_tok[b]).then_inc(d_x[b], 16)

            def load_ctx(b):
                sp.dma_start(f_ctx[:, b], ctx_t[b].rearrange("(k p) l -> p k l", p=P)).then_inc(d_ctx[b > 0], 16)

            load_w(0)
            sp.dma_start(c_sq[:], k_square.rearrange("k p c -> p k c")).then_inc(d_const, 16)
            load_x(0)
            sp.dma_start(c_sel[:], k_sel).then_inc(d_const, 16)
            sp.dma_start(c_shift[:], k_shift).then_inc(d_const, 16)
            sp.dma_start(headm[:], k_head).then_inc(d_const, 16)
            sp.dma_start(par[:], ssm_par.rearrange("(g p) c -> p g c", p=P)).then_inc(d_ssm, 16)
            sp.dma_start(in_w[:], in_w_t.rearrange("(k p) o -> p k o", p=P)).then_inc(d_ssm, 16)
            load_ctx(0)
            sp.dma_start(dt_w[:], dt_w_t).then_inc(d_ssm, 16)
            sp.dma_start(xp_w[:], xp_t.rearrange("(g p) c -> p g c", p=P)).then_inc(d_ssm, 16)
            sp.dma_start(rw[:], router_t.rearrange("(k p) e -> p k e", p=P)).then_inc(d_const, 16)
            for w in range(1, 4):
                load_w(w)
            for b in range(1, NB):
                load_x(b)
                load_ctx(b)
            sp.wait_ge(zeroed, 1)
            sp.dma_start(slots_x.rearrange("(t p) c -> p t c", p=P),
                         zeros[:, None, :].broadcast_to([P, TILES, E])).then_inc(d_zero, 16)
            sp.wait_ge(main_done, 4)
            def load_wd(experts):
                for e in experts:
                    sp.dma_start(wd[:, e, 0:FK - 1], wd_t[e, 0:(FK - 1) * P].rearrange("(f p) o -> p f o", p=P)).then_inc(d_wd, 16)
                    sp.dma_start(wd[0:FL, e, FK - 1], wd_t[e, (FK - 1) * P:FI]).then_inc(d_wd, 16)

            for b in range(NB):
                sp.wait_ge(j_used, b + 1)
                sp.dma_start(j_x[:], x_tok[b]).then_inc(d_jx, 16)
                w, w_t, done = ((wg, wg_t, d_wg), (wu, wu_t, d_wu))[b // 2]
                half = slice(b % 2 * NE // 2, (b % 2 + 1) * NE // 2)
                for e in range(half.start, half.stop):
                    sp.dma_start(w[:, e], w_t[e].rearrange("(k p) i -> p k i", p=P)).then_inc(done, 16)
                if b >= 2:
                    sp.wait_ge(j_nm2, 2 * (b - 1))
                    load_wd([b - 2])
            sp.wait_ge(j_nm2, 2 * (NB - 1))
            load_wd([2, 3])
            sp.wait_ge(j_nm2, 2 * NB)
            sp.dma_start(c_route[:], k_route).then_inc(d_route, 16)
            load_wd(range(4, NE))
            for c in range(4):
                sp.wait_ge(sc_done[c], 8 * TT)
            slots_xt = slots_x.rearrange("(t p) c -> t p c", p=P)
            with sp.Fori(0, TILES // 2) as i:
                for c in range(2):
                    sp.wait_ge(e_tr, i * 2 + c + 1)
                    sp.dma_start(e_x[:, c], slots_xt[i * 2 + c]).then_inc(d_ex[c], 16)
            sp.wait_ge(e_tr, LAST + 1)
            sp.dma_start(e_x[:, 0], slots_xt[LAST]).then_inc(d_ex[0], 16)
            for c in range(4):
                sp.wait_ge(d_out[c], 16 * (TT // 4))

        @block.gpsimd
        def _(pool):
            own = Chain(pool, pool_own)
            nc.gpsimd.memset(zeros[:], 0.0).then_inc(zeroed, 1)
            nc.gpsimd.memset(onesF[:], 1.0).then_inc(consts, 1)
            nc.gpsimd.memset(onesB[:], 1.0).then_inc(consts, 1)
            own.link(nc.gpsimd.memset(halfs[:], -0.5))
            pool.sem_inc(dBu_done, NBS)
            def deviation(b):
                pool.wait_ge(f_stats, b + 1)
                nc.gpsimd.tensor_tensor(rstd[:], vare[:], halfs[:], ALU.pow).then_inc(f_rstd, 1)

            deviation(0)
            with pool.Fori(0, NB - 1) as i:
                deviation(i + 1)
                cols = bass.ts(i, S)
                pool.wait_ge(bc_1, i + 1)
                apart(pool, pool_steps)
                nc.gpsimd.tensor_tensor(f_r1[0:3 * NBC], xd[0:3 * NBC, cols], bcs[:, cols], ALU.subtract).then_inc(rest_1, 1)
                pool.wait_ge(bc_2, i + 1)
                apart(pool, pool_steps)
                nc.gpsimd.tensor_tensor(f_r1[2 * NBC:3 * NBC], f_r1[2 * NBC:3 * NBC], bcs[2 * NBC:, cols],
                                        ALU.subtract).then_inc(rest_2, 1)
                pool.wait_ge(rest_2, i + 1)

            def softplus_end(nx, par_, i, part):
                if part == 0:
                    pool.wait_ge(dt_u1, i)
                    own.link(nc.gpsimd.tensor_tensor(sp_ab[:], sp_u1[:], sp_one[:, 0:1].broadcast_to([P, S]), ALU.subtract))
                elif part == 1:
                    own.link(nc.gpsimd.tensor_tensor(sp_ex[:], sp_ex[:], sp_ab[:], ALU.subtract))
                elif part == 2:
                    pool.wait_ge(dt_relu, i)
                    own.link(nc.gpsimd.tensor_tensor(sp_ab[:], sp_ex[:], du[:, par_], ALU.add))
                elif part == 3:
                    pool.wait_ge(dt_ln, i)
                    own.link(nc.gpsimd.tensor_tensor(delta[:, par_], delta[:, par_], sp_ab[:], ALU.add))
                    pool.sem_inc(dt_done, 1)
                else:
                    nc.gpsimd.tensor_tensor(du[:, par_], delta[:, par_], uy[:, nx], ALU.mult).then_inc(du_done, 1)

            pool.wait_ge(dt_u1, 1)
            own.link(nc.gpsimd.memset(sp_one[:], 1.0))
            for part in range(5):
                softplus_end(0, 0, 1, part)
            with pool.Fori(0, TURNS // 2) as pair:
              own.turn(pair, 8)
              for c in range(2):
                it = pair * 2 + c
                pool.wait_ge(du_done, it + 1)
                for n in range(NST):
                    pool.wait_ge(B_ev, it * NST + n + 2)
                    pool.wait_ge(scan_done, it * NST + n + 1)
                    nc.gpsimd.tensor_tensor(dBu[:, n % NDA], du[:, c], Bs[:, n % NBS],
                                            ALU.mult).then_inc(dBu_done, 1)
                    if n in DELTA_STEP:
                        softplus_end((it + 1) % TURNS, 1 - c, it + 2, DELTA_STEP.index(n))
            own.ended(TURNS // 2)
            pool.wait_ge(du_done, TURNS + 1)
            pool.sem_inc(main_done, 1)
            def rstd_1(b):
                pool.wait_ge(j_stats, b + 1)
                nc.gpsimd.tensor_tensor(rstd[:], vare[:], halfs[:], ALU.pow).then_inc(j_rstd, 1)

            def rstd_2(b):
                pool.wait_ge(j_stats2, b + 1)
                nc.gpsimd.tensor_tensor(rs2[:, bass.ts(b, TB)], vare[:], halfs[:], ALU.pow).then_inc(j_rstd2, 1)

            rstd_1(0)
            with pool.Fori(0, NB - 1) as b:
                rstd_2(b)
                rstd_1(b + 1)
            rstd_2(NB - 1)
            pool.wait_ge(r_slots, 1)
            pool.wait_ge(d_zero, 16)
            for t in range(TT):
                pool.wait_ge(r_norm, t + 1)
                for j in range(2):
                    pool.indirect_dma_start(
                        out=slots_x, out_offset=bass.IndirectOffsetOnAxis(ap=slot[:, j, t:t + 1], axis=0),
                        in_=j_n4[:, t % 4], in_offset=None).then_inc(sc_done[t % 4], 16)
            for c in range(2):
                pool.wait_ge(d_ey[c], 16 * ((TILES + 1 - c) // 2) + 16)
            for t in range(TT):
                if t >= 4:
                    pool.wait_ge(o_done, t - 3)
                for j in range(2):
                    pool.indirect_dma_start(
                        out=o_r[:, t % 4, j], out_offset=None, in_=slots_y,
                        in_offset=bass.IndirectOffsetOnAxis(ap=slot[:, j, t:t + 1], axis=0)).then_inc(g_row[t % 4], 16)

        @block.scalar
        def _(act):
            own = Chain(act, act_own)
            for free, count in ((B_ev, 1), (exp_done, 1), (y_ev, 1), (f_trev, 2), (f_rowev, 1), (f_inev, 2),
                                (f_xdev, 1), (f_silu, 2), (j_trev, 2), (j_ntev, 2), (d_ey[0], 16),
                                (d_ey[1], 16)):
                act.sem_inc(free, count)
            def magnitudes(w):
                act.wait_ge(d_w[w], 16)
                own.link(nc.scalar.activation(f_junk[:], w_stage[:, w], ACT.Abs, accum_out=wstat[:, 0, w:w + 1]))
                act.sem_inc(wabs_done, 1)

            magnitudes(0)

            def take_in(b, g):
                act.wait_ge(f_in, b * NG + g + 1)
                nc.scalar.activation(f_xp[:, g, DC - 1:], bank[3 + g % 2][:], ACT.Copy).then_inc(f_inev, 1)

            def first_tap(b, g):
                act.wait_ge(f_inev, b * NG + g + 3)
                act.wait_ge(f_silu, b * NG + g + 1)
                nc.scalar.activation(f_cv[:, g % 2], f_xp[:, g, 0:S], ACT.Identity, bias=par[:, g, DC:DC + 1],
                                     scale=par[:, g, 0:1]).then_inc(f_tap, 1)

            def bc_first(b):
                act.wait_ge(f_xdev, b + 2)
                apart(act, act_steps)
                nc.scalar.activation(bcs[:, bass.ts(b, S)], xd[0:3 * NBC, bass.ts(b, S)], ACT.Copy).then_inc(bc_1, 1)

            def bc_second(b):
                act.wait_ge(rest_1, b + 1)
                apart(act, act_steps)
                for rows in (slice(NBC, 2 * NBC), slice(2 * NBC, 3 * NBC)):
                    ins = nc.scalar.activation(bcs[rows, bass.ts(b, S)], f_r1[rows], ACT.Copy)
                ins.then_inc(bc_2, 1)

            def bc_third(b):
                act.wait_ge(rest_2, b + 1)
                apart(act, act_steps)
                nc.scalar.activation(bcs[2 * NBC:, bass.ts(b, S)], f_r1[2 * NBC:3 * NBC], ACT.Copy).then_inc(f_split, 1)

            def silu_u(b, g):
                act.wait_ge(f_conv, b * NG + g + 1)
                nc.scalar.activation(uy[:, b * NG + g], f_cv[:, g % 2], ACT.Silu).then_inc(f_silu, 1)

            def take_xd(b):
                act.wait_ge(f_xd, b + 1)
                nc.scalar.activation(xd[:, bass.ts(b, S)], bank[5][0:XR, :], ACT.Copy).then_inc(f_xdev, 1)

            def front(b, before):
                take_in(b, 0)
                take_in(b, 1)
                first_tap(b, 0)
                first_tap(b, 1)
                act.wait_ge(f_stats, b + 1)
                for t in range(TB):
                    nc.scalar.activation(f_xc[:, t], xa[:, b * TB + t], ACT.Identity,
                                         bias=nmean[:, t:t + 1]).then_inc(f_centred, 1)
                take_in(b, 2)
                take_in(b, 3)
                if before is None:
                    magnitudes(1)
                else:
                    take_xd(before)
                    bc_first(before)
                silu_u(b, 0)
                first_tap(b, 2)
                silu_u(b, 1)
                first_tap(b, 3)
                if before is None:
                    magnitudes(2)
                else:
                    bc_second(before)
                for t in range(TB):
                    act.wait_ge(f_tr, b * TB + t + 1)
                    nc.scalar.activation(xqT[:, :, bass.ds(b * S + t * P, P)],
                                         bank[t % 2].bitcast(BF16)[:, 0:E].rearrange("p (k c) -> p k c", k=KT),
                                         ACT.Copy).then_inc(f_trev, 1)
                if before is None:
                    magnitudes(3)
                else:
                    bc_third(before)
                act.wait_ge(f_row, b + 1)
                nc.scalar.activation(scale_row[:, bass.ts(b, S)], bank[2][:], ACT.Copy).then_inc(f_rowev, 1)
                silu_u(b, 2)
                silu_u(b, 3)

            front(0, None)
            with act.Fori(0, NB - 1) as i:
                front(i + 1, i)
            dtb = DC + 1

            def softplus_mid(g, i, to, part):
                if part == 0:
                    act.wait_ge(dt_ps, i)
                    nc.scalar.activation(du[:, to], ps_misc[:], ACT.Relu, bias=par[:, g, dtb:dtb + 1]).then_inc(dt_relu, 1)
                    nc.scalar.activation(sp_ab[:], ps_misc[:], ACT.Abs, bias=par[:, g, dtb:dtb + 1]).then_inc(dt_abs, 1)
                elif part == 1:
                    act.wait_ge(dt_abs, i)
                    nc.scalar.activation(sp_ex[:], sp_ab[:], ACT.Exp, scale=-1.0).then_inc(dt_exp, 1)
                elif part == 2:
                    act.wait_ge(dt_exp, i)
                    nc.scalar.activation(sp_u1[:], sp_ex[:], ACT.Copy, bias=1.0).then_inc(dt_u1, 1)
                else:
                    act.wait_ge(dt_u1, i)
                    nc.scalar.activation(delta[:, to], sp_u1[:], ACT.Ln).then_inc(dt_ln, 1)

            act.wait_ge(f_silu, NB * NG + 2)
            nc.scalar.preload_act_table_set("natural_log_exp_and_others")
            own.link(nc.scalar.activation(negA[:], par[:, :, DC + 3:], ACT.Exp))
            own.link(nc.scalar.activation(negA[:], negA[:], ACT.Copy, scale=-1.0))
            for part in range(4):
                softplus_mid(0, 1, 0, part)
            take_xd(NB - 1)
            act.wait_ge(d_zero, 16)
            act.wait_ge(f_split, NB)
            act.wait_ge(vf_ones, 1)
            act.wait_ge(B_ps, 1)
            nc.scalar.activation(Bs[:, 0], ps_B[:], ACT.Copy).then_inc(B_ev, 1)
            act.wait_ge(dt_done, 1)
            for n in range(2):
                nc.scalar.activation(dA[:, n], delta[:, 0], ACT.Exp, scale=negA[:, 0, n:n + 1]).then_inc(dA_done, 1)
            with act.Fori(0, TURNS) as it:
                b, g = it // NG, it % NG
                for n in range(NST):
                    act.wait_ge(B_ps, it * NST + n + 2)
                    act.wait_ge(dBu_done, it * NST + n + 2)
                    nc.scalar.activation(Bs[:, (n + 1) % NBS], ps_B[:], ACT.Copy).then_inc(B_ev, 1)
                    if n == NST - 2:
                        act.wait_ge(dt_done, it + 2)
                    act.wait_ge(scan_done, it * NST + n + 3)
                    nx = it if n < NST - 2 else it + 1
                    nc.scalar.activation(dA[:, (n + 2) % NDA], delta[:, nx % 2], ACT.Exp,
                                         scale=negA[:, nx % NG, (n + 2) % NST:(n + 2) % NST + 1]).then_inc(dA_done, 1)
                    if n == 0:
                        act.wait_ge(y_acc, it * NACC + NHC)
                        nc.scalar.activation(Du[:], uy[:, it], ACT.Identity,
                                             scale=par[:, g, DC + 2:DC + 3]).then_inc(Du_done, 1)
                        act.wait_ge(q_ev, it + 1)
                        apart(act, act_steps)
                        nc.scalar.activation(q16[:], qf[:], ACT.Copy).then_inc(q16_done, 1)
                        act.wait_ge(k_ev, it + 1)
                        apart(act, act_steps)
                        nc.scalar.activation(k16[:], kf[:], ACT.Copy).then_inc(k16_done, 1)
                        act.wait_ge(v_ps, it + 1)
                        for t in range(TB):
                            ins = nc.scalar.activation(vf[:, t, :, 0:HD],
                                                       ps_v[:, t * P:(t + 1) * P].rearrange("p (h d) -> p h d", d=HD),
                                                       ACT.Identity, scale=dqv[:, bass.ds(b * TB + t, 1)])
                        ins.then_inc(v_ev, 1)
                    if n == 1:
                        nc.scalar.activation(dt_wc[:], dt_w[:, bass.ds((it + 1) % NG * P, P)], ACT.Copy).then_inc(dtw_ev, 1)
                    for hh in QZ_STEP.get(n, []):
                        nc.scalar.activation(qz[hh % 2][:], qf[:], ACT.Copy, scale=headm[:, hh:hh + 1]).then_inc(qz_done, 1)
                    if n == MT_STEP:
                        act.wait_ge(mT_ps, it + 1)
                        nc.scalar.activation(mT[0:2 * HG], ps_misc.bitcast(BF16)[0:2 * HG, 0:S], ACT.Copy).then_inc(mT_ev, 1)
                    if 4 <= n < 8:
                        softplus_mid((it + 1) % NG, it + 2, (it + 1) % 2, n - 4)
                    for i in AT_STEP[n]:
                        hh, kt = i // TB, i % TB
                        w = S - kt * P
                        act.wait_ge(st_ps, it * 16 + i + 1)
                        act.wait_ge(pv_done, it * 16 + (i + 1 if i else NPT))
                        nc.scalar.activation(pT[:, i % NPT, 0:w], ps_sc[i % 2][:, 0:w], ACT.Exp).then_inc(exp_done, 1)
                act.wait_ge(y_acc, it * NACC + NACC + NHC)
                apart(act, act_steps)
                nc.scalar.activation(uy[:, it], ps_y[:], ACT.Copy).then_inc(y_ev, 1)
            act.wait_ge(y_ev, TURNS + 1)
            act.sem_inc(main_done, 1)
            def rows_back(b, t):
                act.wait_ge(j_tr, b * TB + t + 1)
                nc.scalar.activation(j_qT[:, :, t * P:(t + 1) * P],
                                     bank[t % 2].bitcast(BF16)[:, 0:E].rearrange("p (k c) -> p k c", k=KT),
                                     ACT.Copy).then_inc(j_trev, 1)

            def gate(b, t):
                nc.scalar.activation(j_z[:, t], xa[:, b * TB + t], ACT.Silu, bias=nmean[:, t:t + 1],
                                     scale=rstd[:, t:t + 1]).then_inc(j_silu, 1)

            def norm(b):
                act.wait_ge(j_nm2, b * 2 + 2)

                def norm_back(t):
                    act.wait_ge(j_nt, b * TB + t + 3)
                    nc.scalar.activation(j_nT[:, t % 2], bank[5 + t % 2][:], ACT.Copy).then_inc(j_ntev, 1)

                for t in range(TB):
                    act.wait_ge(j_nt, b * TB + t + 1)
                    nc.scalar.activation(j_n[:, t % 2], xa[:, b * TB + t], ACT.Identity,
                                         bias=nm2[:, bass.ds(b * TB + t, 1)],
                                         scale=rs2[:, bass.ds(b * TB + t, 1)]).then_inc(j_norm, 1)
                    if t >= 1:
                        norm_back(t - 1)
                norm_back(TB - 1)

            for t in range(TB):
                rows_back(0, t)
            with act.Fori(0, NB - 1) as b:
                act.wait_ge(j_nm2, b * 2 + 1)
                act.wait_ge(j_zt, b * TB + 1)
                for t in range(TB):
                    gate(b, t)
                for t in range(TB):
                    rows_back(b + 1, t)
                norm(b)
            def high_part(c):
                w = (wg, wu)[c // NE]
                if c % NE == 0:
                    act.wait_ge((d_wg, d_wu)[c // NE], 16 * NE)
                if c >= 2:
                    act.wait_ge(w_split, c - 1)
                nc.scalar.activation(w_hi[:, c % 2], w[:, c % NE], ACT.Copy, scale=W_UP).then_inc(hi_done, 1)

            act.wait_ge(j_nm2, NB * 2 - 1)
            act.wait_ge(j_zt, (NB - 1) * TB + 1)
            for t in range(TB):
                gate(NB - 1, t)
            high_part(0)
            high_part(1)
            norm(NB - 1)
            high_part(2)
            high_part(3)
            act.wait_ge(r_c, 1)
            nc.scalar.activation(pr[:], pr[:], ACT.Exp).then_inc(r_exp, 1)
            act.wait_ge(r_slots, 1)
            for t in range(TT):
                if t >= 4:
                    act.wait_ge(sc_done[t % 4], 32 * (t // 4))
                nc.scalar.activation(j_n4[:, t % 4], xa[:, t], ACT.Identity, bias=nm2[:, t:t + 1],
                                     scale=rs2[:, t:t + 1]).then_inc(r_norm, 1)
                if 4 <= t + 1 < CHUNKS:
                    high_part(t + 1)

            slots_yt = slots_y.rearrange("(t p) c -> t p c", p=P)

            def transposed(j, c):
                act.wait_ge(e_tr, j + 3)
                act.wait_ge(e_g, j + 1)
                nc.scalar.activation(e_xT[:, c, 0], bank[0][:], ACT.Copy).then_inc(e_hi, 1)

            def silu(j, c):
                act.wait_ge(e_g, j + 3)
                act.wait_ge(e_act, j + 1)
                nc.scalar.activation(e_s[:, c], bank[1 + c][:, 0:FI], ACT.Silu, scale=1 / W_UP).then_inc(e_silu, 1)

            def store(j, c):
                act.wait_ge(e_dev, j + 3)
                act.dma_start(slots_yt[j], e_y[:, c]).then_inc(d_ey[c], 16)

            transposed(0, 0)
            transposed(1, 1)
            silu(0, 0)
            with act.Fori(0, TILES // 2 - 1) as i:
                for c in range(2):
                    j = i * 2 + c + 1
                    transposed(j + 1, c)
                    silu(j, 1 - c)
                    store(j - 1, c)
            transposed(LAST, 0)
            silu(LAST - 1, 1)
            store(LAST - 2, 0)
            silu(LAST, 0)
            store(LAST - 1, 1)
            store(LAST, 0)
            for t in range(TT):
                act.wait_ge(o_done, t + 1)
                act.dma_start(out[t * P:(t + 1) * P, :], o_o[:, t % 4]).then_inc(d_out[t % 4], 16)

        @block.tensor
        def _(pe):
            mm = nc.tensor.matmul
            for free, count in ((y_acc, NHC), (pv_done, NPT), (j_zt, 1), (j_nt, 2), (e_tr, 2),
                                (e_g, 2), (e_at, 2), (e_d, 2)):
                pe.sem_inc(free, count)
            pe.wait_ge(consts, 3)
            pe.wait_ge(wabs_done, 1)
            mm(bank[6][:, 0:1], onesF[:], wstat[:, 0, 0:1], start=True, stop=True).then_inc(wsum_done, 1)
            pe.wait_ge(d_ssm, 64)
            pe.wait_ge(d_ctx[0], 16)

            def project_in(b, g):
                pe.wait_ge(f_inev, b * NG + g + 1)
                for k in range(KC):
                    last = mm(bank[3 + g % 2][:], in_w[:, k, g * P:(g + 1) * P], f_ctx[:, b, k],
                              start=k == 0, stop=k == KC - 1)
                last.then_inc(f_in, 1)

            def project_xd(b):
                pe.wait_ge(f_silu, b * NG + NG + 2)
                pe.wait_ge(f_xdev, b + 1)
                for g in range(NG):
                    last = mm(bank[5][0:XR, :], xp_w[:, g], uy[:, b * NG + g], start=g == 0, stop=g == NG - 1)
                last.then_inc(f_xd, 1)

            def front(b, before):
                project_in(b, 0)
                project_in(b, 1)
                if before is not None:
                    project_xd(before)
                project_in(b, 2)
                project_in(b, 3)
                for t in range(TB):
                    pe.wait_ge(f_quant, b * TB + t + 1)
                    pe.wait_ge(f_trev, b * TB + t + 1)
                    for k in range(KT):
                        last = nc.tensor.transpose(bank[t % 2].bitcast(BF16)[:, k * P:(k + 1) * P],
                                                   f_xq[:, t, k * P:(k + 1) * P], identB[:])
                    last.then_inc(f_tr, 1)
                pe.wait_ge(f_diag, b + 1)
                pe.wait_ge(f_rowev, b + 1)
                mm(bank[2][:], onesF[:], f_dg[:].rearrange("p t c -> p (t c)"), start=True, stop=True).then_inc(f_row, 1)

            front(0, None)
            pe.wait_ge(wabs_done, 4)
            mm(bank[7][:, 0:3], onesF[:], wstat[:, 0, 1:], start=True, stop=True).then_inc(wsum_done, 1)
            pe.wait_ge(d_ctx[1], 16 * (NB - 1))
            with pe.Fori(0, NB - 1) as i:
                front(i + 1, i)
            pe.wait_ge(f_trev, TT + 2)
            mm(ps_misc[:], dt_w[:, 0:P], xd[:, 0:S], start=True, stop=True).then_inc(dt_ps, 1)
            project_xd(NB - 1)

            pe.wait_ge(f_xdev, NB + 1)
            pe.wait_ge(f_split, 1)
            pe.wait_ge(wt_done, 4)
            pe.wait_ge(vf_ones, 1)
            mm(ps_B[:], sel[:, 0], bcs[:, 0:S], start=True, stop=True).then_inc(B_ps, 1)
            with pe.Fori(0, TURNS) as it:
                b, g = it // NG, it % NG
                pe.wait_ge(f_split, (it + 1) % TURNS // NG + 1)

                def accumulate(n):
                    if n == SUM_LAST:
                        pe.wait_ge(sum_done, it * NSUM + NSUM + 1)
                    else:
                        pe.wait_ge(hC_done, it * NST + n + 3)
                    if n == 0:
                        pe.wait_ge(y_ev, it + 1)
                    for t in range(TB):
                        last = mm(ps_y[:, t * P:(t + 1) * P], hC[:, n % NHC, t * P:(t + 1) * P], identF[:],
                                  start=n == 0 and t == 0, stop=n == NST - 1, is_transpose=True, skip_group_check=True)
                    last.then_inc(y_acc, 1)

                def scores(m):
                    hh, qt = m // TB, m % TB
                    if m == 0:
                        pe.wait_ge(q16_done, it + 1)
                        pe.wait_ge(k16_done, it + 1)
                    elif m == 1:
                        pe.wait_ge(v_ev, it + 1)
                    elif m == 2:
                        pe.wait_ge(o_ev, it * HG + 2)
                    else:
                        pe.wait_ge(max_done, it * 16 + m - 2)
                    w = (qt + 1) * P
                    r = slice(hh * HD, (hh + 1) * HD)
                    mm(ps_max[m % 3][:, 0:w], q16[r, qt * P:(qt + 1) * P], k16[r, 0:w],
                       start=True, stop=False, skip_group_check=True)
                    mm(ps_max[m % 3][:, w - P:w], identB[:], maskQ[:], start=False, stop=True,
                       skip_group_check=True).then_inc(s_ps, 1)

                def scores_t(i):
                    hh, kt = i // TB, i % TB
                    if i == 0:
                        pe.wait_ge(max_done, it * 16 + 16)
                        pe.wait_ge(mT_ev, it + 1)
                    if i >= 2:
                        pe.wait_ge(exp_done, it * 16 + i)
                    w = S - kt * P
                    if kt == 0:
                        pe.wait_ge(qz_done, it * HG + hh + 1)
                    mm(ps_sc[i % 2][:, 0:w], kf[:, kt * P:(kt + 1) * P], qz[hh % 2][:, kt * P:S],
                       start=True, stop=False, skip_group_check=True)
                    mm(ps_sc[i % 2][:, 0:P], identB[:], maskK[:], start=False, stop=False, skip_group_check=True)
                    mm(ps_sc[i % 2][:, 0:w], shift[:, hh], mT[:, kt * P:S], start=False, stop=True,
                       skip_group_check=True).then_inc(st_ps, 1)

                def values(i):
                    hh, kt = i // TB, i % TB
                    pe.wait_ge(exp_done, it * 16 + i + 2)
                    if kt == 0 and hh >= 2:
                        pe.wait_ge(o_ev, it * HG + hh + 1)
                    for qt in range(kt, TB):
                        last = mm(ps_o[hh % 2][:, qt * (HD + 1):(qt + 1) * (HD + 1)], pT[:, i % NPT, (qt - kt) * P:(qt - kt + 1) * P],
                                  vf[:, kt, hh], start=kt == 0 and qt == 0, stop=kt == qt, skip_group_check=True)
                    last.then_inc(pv_done, 1)

                for n in range(NST):
                    pe.wait_ge(B_ev, it * NST + n + 2)
                    b_n = b if n < NST - 1 else (it + 1) % TURNS // NG
                    mm(ps_B[:], sel[:, (n + 1) % NST], bcs[:, bass.ds(b_n * S, S)], start=True, stop=True).then_inc(B_ps, 1)
                    pe.wait_ge(hC_done, it * NST + n + 1)
                    mm(ps_C[n % 2][:], sel[:, NST + n], bcs[:, bass.ds(b * S, S)], start=True, stop=True).then_inc(C_ps, 1)
                    if 2 <= n < SUM_FIRST + 1:
                        accumulate(n - 2)
                    if n == 4:
                        pe.wait_ge(Du_done, it + 1)
                        for t in range(TB):
                            mm(ps_y[:, t * P:(t + 1) * P], Du[:, t * P:(t + 1) * P], identF[:], start=False, stop=False,
                               is_transpose=True, skip_group_check=True)
                    if n == 0:
                        pe.wait_ge(dt_abs, it + 1)
                        pe.wait_ge(dt_relu, it + 1)
                        pe.wait_ge(o_ev, it * HG + 1)
                        for k in range(KT):
                            last = mm(ps_misc[:], wT[:, 0, k, bass.ds(g * P, P)], xqT[:, k, bass.ds(b * S, S)],
                                      start=k == 0, stop=k == KT - 1)
                        last.then_inc(q_ps, 1)
                        pe.wait_ge(exp_done, it * 16 + 1)
                        for k in range(KT):
                            last = mm(ps_k[:], wT[:, 1, k, bass.ds(g * P, P)], xqT[:, k, bass.ds(b * S, S)],
                                      start=k == 0, stop=k == KT - 1)
                        last.then_inc(k_ps, 1)
                        for t in range(TB):
                            for k in range(KT):
                                last = mm(ps_v[:, t * P:(t + 1) * P], xqT[:, k, bass.ds(b * S + t * P, P)],
                                          wT[:, 2, k, bass.ds(g * P, P)], start=k == 0, stop=k == KT - 1)
                        last.then_inc(v_ps, 1)
                    for m in MAX_STEP[n]:
                        scores(m)
                    if n == MT_STEP:
                        pe.wait_ge(mhl_done, it + 1)
                        pe.wait_ge(dt_abs, it + 2)
                        for t in range(TB):
                            last = nc.tensor.transpose(ps_misc.bitcast(BF16)[0:2 * HG, t * P:(t + 1) * P],
                                                       mhl[:, t], identB[:])
                        last.then_inc(mT_ps, 1)
                    for i in AT_STEP[n]:
                        scores_t(i)
                        if i >= 1:
                            values(i - 1)
                    if n == 3:
                        pe.wait_ge(q_ev, it + 1)
                        pe.wait_ge(dtw_ev, it + 1)
                        mm(ps_misc[:], dt_wc[:], xd[:, bass.ds((it + 1) % TURNS // NG * S, S)],
                           start=True, stop=True).then_inc(dt_ps, 1)
                accumulate(14)
                values(15)
                accumulate(15)

            pe.wait_ge(y_acc, TURNS * NACC + NHC)
            pe.sem_inc(main_done, 1)
            def rows_t(b):
                for t in range(TB):
                    pe.wait_ge(j_quant, b * TB + t + 1)
                    pe.wait_ge(j_trev, b * TB + t + 1)
                    for k in range(KT):
                        last = nc.tensor.transpose(bank[t % 2].bitcast(BF16)[:, k * P:(k + 1) * P],
                                                   j_q[:, t, k * P:(k + 1) * P], identB[:])
                    last.then_inc(j_tr, 1)

            def project(b):
                for t in range(TB):
                    pe.wait_ge(j_trev, b * TB + t + 3)
                    pe.wait_ge(j_x1, b * TB + t + 1)
                    for k in range(KT):
                        last = mm(bank[2 + t % 2][:], j_qT[:, k, t * P:(t + 1) * P], wT[:, 3, k],
                                  start=k == 0, stop=k == KT - 1)
                    last.then_inc(j_proj, 1)

            def gate_t(b, tiles):
                for t in tiles:
                    pe.wait_ge(j_silu, b * TB + t + 1)
                    pe.wait_ge(j_gate, b * TB + (t - 1 if t == 3 else 1))
                    for k in range(KT):
                        last = nc.tensor.transpose(ps_z[t % 3][:, k * P:(k + 1) * P], j_z[:, t, k * P:(k + 1) * P],
                                                   identF[:])
                    last.then_inc(j_zt, 1)

            def route(b):
                def logits(t):
                    pe.wait_ge(j_ntev, b * TB + t + 3)
                    for k in range(KT):
                        last = mm(bank[7][:, t * NE:(t + 1) * NE], j_nT[:, t % 2, k * P:(k + 1) * P], rw[:, k],
                                  start=k == 0, stop=k == KT - 1)
                    return last

                for t in range(TB):
                    pe.wait_ge(j_norm, b * TB + t + 1)
                    pe.wait_ge(j_ntev, b * TB + t + 1)
                    for k in range(KT):
                        last = nc.tensor.transpose(bank[5 + t % 2][:, k * P:(k + 1) * P], j_n[:, t % 2, k * P:(k + 1) * P],
                                                   identF[:])
                    last.then_inc(j_nt, 1)
                    if t == 1:
                        pe.wait_ge(j_lgev, b + 1)
                    if t >= 1:
                        logits(t - 1)
                logits(TB - 1).then_inc(j_lg, 1)

            rows_t(0)
            project(0)
            with pe.Fori(0, NB - 1) as b:
                gate_t(b, range(TB - 1))
                rows_t(b + 1)
                gate_t(b, [TB - 1])
                project(b + 1)
                route(b)
            gate_t(NB - 1, range(TB))
            route(NB - 1)
            pe.wait_ge(r_mask, 1)
            mm(bank[0][:, 0:TT * NE], triB[:], ohB[:].rearrange("p t e -> p (t e)"), start=True, stop=True)
            mm(bank[1][:, 0:TT * NE], onesB[:], ohB[:].rearrange("p t e -> p (t e)"),
               start=True, stop=True).then_inc(r_rank, 1)
            pe.wait_ge(r_slots, 1)

            def expert(j):
                return pe.value_load(tile_e[0:1, bass.ds(j, 1)], min_val=0, max_val=NE - 1)

            def rows_t(j, c, half):
                pe.wait_ge(d_ex[c], half * 16 + 16)
                pe.wait_ge(e_trev, j + 1)
                for k in range(KT):
                    last = nc.tensor.transpose(bank[0][:, k * P:(k + 1) * P], e_x[:, c, k * P:(k + 1) * P], identF[:])
                last.then_inc(e_tr, 1)

            def gate_up(j, c, e):
                pe.wait_ge(e_trev, j + 2)
                pe.wait_ge(e_act, j + 1)
                for k in range(KT):
                    x_hi, x_lo = (e_xT[:, c, part, k * P:(k + 1) * P] for part in range(2))
                    for n_term, (xs, part) in enumerate(((x_hi, 0), (x_hi, 1), (x_lo, 0))):
                        first, final = k == 0 and n_term == 0, k == KT - 1 and n_term == 2
                        mm(bank[1 + c][:, 0:FI], xs, wg16[:, e, k, :, part], start=first, stop=final)
                        last = mm(bank[3 + c][:, 0:FI], xs, wu16[:, e, k, :, part], start=first, stop=final)
                last.then_inc(e_g, 1)

            def act_t(j, c):
                pe.wait_ge(e_act, j + 3)
                pe.wait_ge(e_atev, j + 1)
                for f in range(FK):
                    w = P if f < FK - 1 else FL
                    last = nc.tensor.transpose(bank[5][0:w, f * P:(f + 1) * P], e_a[:, c, f * P:f * P + w], identF[:])
                last.then_inc(e_at, 1)

            def down(j, c, e):
                pe.wait_ge(e_atev, j + 2)
                pe.wait_ge(e_dev, j + 1)
                for f in range(FK):
                    w = P if f < FK - 1 else FL
                    last = mm(bank[6 + c][:], e_aT[0:w, c, f], wd[0:w, e, f], start=f == 0, stop=f == FK - 1)
                last.then_inc(e_d, 1)

            rows_t(0, 0, 0)
            rows_t(1, 1, 0)
            pe.wait_ge(w_split, CHUNKS)
            gate_up(0, 0, expert(0))
            pe.wait_ge(d_wd, 2 * NE * 16)
            with pe.Fori(0, TILES // 2 - 1) as i:
                for c in range(2):
                    j = i * 2 + c + 1
                    e_before, e = expert(j - 1), expert(j)
                    rows_t(j + 1, c, i + 1)
                    act_t(j - 1, c)
                    gate_up(j, 1 - c, e)
                    down(j - 1, c, e_before)
            rows_t(LAST, 0, LAST // 2)
            for j in (LAST - 1, LAST):
                act_t(j - 1, (j - 1) % 2)
                gate_up(j, j % 2, expert(j))
                down(j - 1, (j - 1) % 2, expert(j - 1))
            act_t(LAST, 0)
            down(LAST, 0, expert(LAST))

        @block.vector
        def _(dve):
            own = Chain(dve, dve_own)
            v = nc.vector
            for free, count in ((scan_done, NDA), (hC_done, 2), (o_ev, 2), (sum_done, 1), (j_x1, 2), (j_gate, 1), (j_used, 1),
                                (j_lgev, 1), (e_trev, 1), (e_act, 2), (e_atev, 1), (e_dev, 2)):
                dve.sem_inc(free, count)
            own.link(v.memset(f_xp[:, :, 0:DC - 1], 0.0))
            dve.wait_ge(d_const, 80)
            v.tensor_copy(identF[:], c_sq[:, 0])
            v.tensor_copy(identB[:], c_sq[:, 0])
            v.tensor_copy(maskQ[:], c_sq[:, 1])
            v.tensor_copy(maskK[:], c_sq[:, 2])
            v.tensor_copy(triB[:], c_sq[:, 3])
            v.tensor_copy(shift[:], c_shift[:])
            v.tensor_copy(sel[:], c_sel[:, :, None].broadcast_to([3 * NBC, NBC, P])).then_inc(consts, 1)
            def ternary(ws, sums, w_0):
                r = slice(w_0, w_0 + ws)
                own.link(v.tensor_scalar(wstat[:, 1, r], sums, 1.0 / (E * E), 1e-5, ALU.mult, ALU.max))
                own.link(v.reciprocal(wstat[:, 2, r], wstat[:, 1, r]))
                for w in range(w_0, w_0 + ws):
                    own.link(v.tensor_scalar(w_stage[:, w], w_stage[:, w], wstat[:, 2, w:w + 1], 1.0, ALU.mult, ALU.min))
                    own.link(v.tensor_scalar(w_stage[:, w], w_stage[:, w], -1.0, ROUND, ALU.max, ALU.add))
                    v.tensor_scalar(wT[:, w], w_stage[:, w], ROUND, None, ALU.subtract).then_inc(wt_done, 1)

            def stats_x(b):
                for t in range(TB):
                    own.mark(v.bn_stats(bn6[:, t], xa[:, b * TB + t]))
                dve.wait_ge(dve_own, own.at + own.n)
                apart(dve, dve_steps)
                for t in range(TB):
                    own.mark(v.bn_aggr(mv[:, t], bn6[:, t]))
                dve.wait_ge(dve_own, own.at + own.n)
                own.mark(v.tensor_scalar(nmean[:], mv[:, :, 0], -1.0, None, ALU.mult))
                v.tensor_scalar(vare[:], mv[:, :, 1], EPS, None, ALU.add).then_inc(f_stats, 1)

            def quantise_x(b):
                dve.wait_ge(f_centred, b * TB + TB)
                own.link(v.tensor_reduce(amax[:], f_xc[:], AX, ALU.max, apply_absolute_value=True))
                dve.wait_ge(f_rstd, b + 1)
                own.link(v.tensor_tensor(clip[:], amax[:], rstd[:], ALU.mult))
                own.link(v.tensor_scalar(clip[:], clip[:], 1e-5, None, ALU.max))
                own.mark(v.tensor_scalar(dq[:, bass.ts(b, TB)], clip[:], 1.0 / 127, None, ALU.mult))
                own.link(v.reciprocal(tmp4[:], clip[:]))
                own.link(v.scalar_tensor_tensor(out=qs[:], in0=tmp4[:], scalar=127.0, in1=rstd[:], op0=ALU.mult, op1=ALU.mult))
                for t in range(TB):
                    own.link(v.tensor_scalar(f_xm[:, t], f_xc[:, t], qs[:, t:t + 1], ROUND, ALU.mult, ALU.add))
                    v.tensor_scalar(f_xq[:, t], f_xm[:, t], ROUND, 127.0, ALU.subtract, ALU.min).then_inc(f_quant, 1)
                for t in range(TB):
                    last = v.tensor_scalar(f_dg[:, t], identF[:], dq[:, bass.ds(b * TB + t, 1)], None, ALU.mult)
                last.then_inc(f_diag, 1)

            def convolve(b, g):
                dve.wait_ge(f_tap, b * NG + g + 1)
                for j in range(1, DC):
                    ins = v.scalar_tensor_tensor(out=f_cv[:, g % 2], in0=f_xp[:, g, j:j + S], scalar=par[:, g, j:j + 1],
                                                 in1=f_cv[:, g % 2], op0=ALU.mult, op1=ALU.add)
                    if j < DC - 1:
                        own.link(ins)
                ins.then_inc(f_conv, 1)

            def split_bc(b):
                dve.wait_ge(f_xdev, b + 2)
                apart(dve, dve_steps)
                cols = bass.ts(b, S)
                own.link(v.tensor_copy(bcs[:, cols], xd[0:3 * NBC, cols]))
                own.link(v.tensor_tensor(f_r1[0:3 * NBC], xd[0:3 * NBC, cols], bcs[:, cols], ALU.subtract))
                apart(dve, dve_steps)
                own.mark(v.tensor_copy(bcs[NBC:2 * NBC, cols], f_r1[NBC:2 * NBC]))
                own.link(v.tensor_copy(bcs[2 * NBC:, cols], f_r1[2 * NBC:3 * NBC]))
                own.link(v.tensor_tensor(f_r1[2 * NBC:3 * NBC], f_r1[2 * NBC:3 * NBC], bcs[2 * NBC:, cols], ALU.subtract))
                apart(dve, dve_steps)
                v.tensor_copy(bcs[2 * NBC:, cols], f_r1[2 * NBC:3 * NBC]).then_inc(f_split, 1)

            def front(b):
                stats_x(b)
                convolve(b, 0)
                convolve(b, 1)
                quantise_x(b)
                convolve(b, 2)
                convolve(b, 3)

            dve.wait_ge(wsum_done, 1)
            ternary(1, bank[6][:, 0:1], 0)
            dve.wait_ge(wt_done, 1)
            dve.wait_ge(d_x[0], 16)
            front(0)
            dve.wait_ge(wsum_done, 2)
            ternary(3, bank[7][:, 0:3], 1)
            own.link(v.tensor_scalar(cqk[:, 0:1], wstat[:, 1, 0:1], wstat[:, 1, 1:2], HD ** -0.5, ALU.mult, ALU.mult))
            dve.wait_ge(wt_done, 4)
            for b in range(1, NB):
                dve.wait_ge(d_x[b], 16)
            with dve.Fori(0, NB - 1) as i:
                own.turn(i, FRONT_DVE)
                front(i + 1)
            own.ended(NB - 1)
            own.link(v.tensor_scalar(dqv[:], dq[:], wstat[:, 1, 2:3], None, ALU.mult))
            split_bc(NB - 1)

            v.memset(mT[:], 0.0)
            v.memset(vf[:, :, :, HD:], 1.0).then_inc(vf_ones, 1)
            with dve.Fori(0, TURNS) as it:
                own.turn(it, 1 + HG)
                b, g = it // NG, it % NG

                def times_C(n):
                    dve.wait_ge(scan_done, it * NST + n + 1 + NDA)
                    dve.wait_ge(C_ps, it * NST + n + 1)
                    before = n - NHC + (NST if n < NHC else 0)
                    if SUM_FIRST - 1 <= before < SUM_LAST:
                        if n < NHC:
                            dve.wait_ge(sum_done, it * NSUM + 1)
                        else:
                            dve.wait_ge(sum_done, it * NSUM + before - SUM_FIRST + 3)
                    elif n < NHC:
                        dve.wait_ge(y_acc, it * NACC + NHC - (NST - 1 - before))
                    else:
                        dve.wait_ge(y_acc, it * NACC + NHC + before + 1)
                    v.tensor_tensor(hC[:, n % NHC], h[:, n % NH], ps_C[n % 2][:], ALU.mult).then_inc(hC_done, 1)

                def add_before(n):
                    dve.wait_ge(hC_done, it * NST + n + 3)
                    if n > SUM_FIRST:
                        dve.wait_ge(sum_done, it * NSUM + n - SUM_FIRST + 1)
                    v.tensor_tensor(hC[:, n % NHC], hC[:, n % NHC], hC[:, (n - 1) % NHC], ALU.add).then_inc(sum_done, 1)

                def head_out(hh):
                    dve.wait_ge(pv_done, it * 16 + (hh + 1) * TB + NPT)
                    po = ps_o[hh % 2][:, 0:TB * (HD + 1)].rearrange("p (t d) -> p t d", d=HD + 1)
                    own.link(v.reciprocal(rden[:, hh], po[:, :, HD]))
                    v.tensor_tensor(xa[:, bass.ts(b, TB), bass.ds(g * P + hh * HD, HD)], po[:, :, 0:HD],
                                    rden[:, hh, :, None].broadcast_to([P, TB, HD]), ALU.mult).then_inc(o_ev, 1)

                for n in range(NST):
                    dve.wait_ge(hC_done, it * NST + (n if n else 2))
                    dve.wait_ge(dA_done, it * NST + n + 1)
                    dve.wait_ge(dBu_done, it * NST + n + 1 + NBS)
                    v.tensor_tensor_scan(h[:, n % NH], dA[:, n % NDA], dBu[:, n % NDA], 0.0,
                                         ALU.mult, ALU.add).then_inc(scan_done, 1)
                    if n >= 1:
                        times_C(n - 1)
                    if SUM_FIRST <= n - 2 <= SUM_LAST:
                        add_before(n - 2)
                    if n == 0:
                        dve.wait_ge(q_ps, it + 1)
                        v.scalar_tensor_tensor(out=qf[:], in0=ps_misc[:], scalar=cqk[:, 0:1],
                                               in1=scale_row[:, bass.ts(b, S)], op0=ALU.mult, op1=ALU.mult).then_inc(q_ev, 1)
                        dve.wait_ge(k_ps, it + 1)
                        v.tensor_tensor(kf[:], ps_k[:], scale_row[:, bass.ts(b, S)], ALU.mult).then_inc(k_ev, 1)
                    for m in MAX_STEP[n]:
                        hh, qt = m // TB, m % TB
                        dve.wait_ge(s_ps, it * 16 + m + 1)
                        v.tensor_reduce(mx[:, qt, hh:hh + 1], ps_max[m % 3][:, 0:(qt + 1) * P], AX, ALU.max).then_inc(max_done, 1)
                    if n == 6:
                        dve.wait_ge(max_done, it * 16 + 16)
                        own.link(v.tensor_copy(mhl[:, :, 0:HG], mx[:]))
                        v.tensor_tensor(mhl[:, :, HG:], mx[:], mhl[:, :, 0:HG], ALU.subtract).then_inc(mhl_done, 1)
                    if n in HEAD_STEP:
                        head_out(HEAD_STEP.index(n))
                add_before(NST - 2)
                times_C(NST - 1)
                head_out(HG - 1)
            own.ended(TURNS)
            dve.wait_ge(o_ev, TURNS * HG + 2)
            dve.sem_inc(main_done, 1)

            def stats(b, done):
                apart(dve, dve_steps)
                for t in range(TB):
                    own.mark(v.bn_stats(bn6[:, t], xa[:, b * TB + t]))
                dve.wait_ge(dve_own, own.at + own.n)
                apart(dve, dve_steps)
                for t in range(TB):
                    own.mark(v.bn_aggr(mv[:, t], bn6[:, t]))
                dve.wait_ge(dve_own, own.at + own.n)
                v.tensor_scalar(vare[:], mv[:, :, 1], EPS, None, ALU.add).then_inc(done, 1)

            def quantise(b):
                own.link(v.tensor_reduce(amax[:], xa[:, bass.ts(b, TB)], AX, ALU.max, apply_absolute_value=True))
                own.link(v.tensor_scalar(clip[:], amax[:], 1e-5, None, ALU.max))
                own.link(v.reciprocal(qs[:], clip[:]))
                own.mark(v.tensor_scalar(tmp4[:], clip[:], 1.0 / 127, wstat[:, 1, 3:4], ALU.mult, ALU.mult))
                own.link(v.tensor_scalar(qs[:], qs[:], 127.0, None, ALU.mult))
                for t in range(TB):
                    own.link(v.tensor_scalar(j_m[:, t % 2], xa[:, b * TB + t], qs[:, t:t + 1], ROUND, ALU.mult, ALU.add))
                    v.tensor_scalar(j_q[:, t], j_m[:, t % 2], ROUND, 127.0, ALU.subtract, ALU.min).then_inc(j_quant, 1)

            def residual(b, tiles):
                if 0 in tiles:
                    dve.wait_ge(d_jx, b * 16 + 16)
                for t in tiles:
                    dve.wait_ge(j_proj, b * TB + t + 1)
                    v.scalar_tensor_tensor(out=xa[:, b * TB + t], in0=bank[2 + t % 2][:], scalar=tmp4[:, t:t + 1],
                                           in1=j_x[:, t], op0=ALU.mult, op1=ALU.add).then_inc(j_x1, 1)

            def residual_stats(b):
                dve.wait_ge(j_x1, b * TB + TB + 2)
                dve.sem_inc(j_used, 1)
                stats(b, j_stats)

            def gate_mean(b):
                dve.wait_ge(j_rstd, b + 1)
                apart(dve, dve_steps)
                v.scalar_tensor_tensor(out=nmean[:], in0=mv[:, :, 0], scalar=-1.0, in1=rstd[:], op0=ALU.mult,
                                       op1=ALU.mult).then_inc(j_nm2, 1)

            def gated(b, quantised):
                dve.wait_ge(j_quant, quantised * TB)
                dve.wait_ge(j_silu, b * TB + TB)
                apart(dve, dve_steps)
                for t in range(TB):
                    dve.wait_ge(j_zt, b * TB + t + 2)
                    v.tensor_tensor(j_g[:], ps_z[t % 3][:], uy[:, b * TB + t], ALU.mult).then_inc(j_gate, 1)
                    dve.wait_ge(j_gate, b * TB + t + 2)
                    part = xa[:, bass.ts(b, TB), t * P:(t + 1) * P]
                    own.link(v.tensor_tensor(part, part, j_g[:].rearrange("p (t c) -> p t c", t=TB), ALU.add))
                stats(b, j_stats2)

            def router_mean(b):
                dve.wait_ge(j_rstd2, b + 1)
                apart(dve, dve_steps)
                v.scalar_tensor_tensor(out=nm2[:, bass.ts(b, TB)], in0=mv[:, :, 0], scalar=-1.0,
                                       in1=rs2[:, bass.ts(b, TB)], op0=ALU.mult, op1=ALU.mult).then_inc(j_nm2, 1)

            def take_logits(b):
                dve.wait_ge(j_lg, b + 1)
                apart(dve, dve_steps)
                v.tensor_copy(lg[:, bass.ts(b, TB)], bank[7][:, 0:TB * NE].rearrange("p (t e) -> p t e", e=NE)).then_inc(j_lgev, 1)

            def split_weights(c):
                w, w16 = ((wg, wg16), (wu, wu16))[c // NE]
                dve.wait_ge(hi_done, c + 1)
                own.link(v.scalar_tensor_tensor(out=w16[:, c % NE, :, :, 1], in0=w[:, c % NE], scalar=W_UP, in1=w_hi[:, c % 2],
                                                op0=ALU.mult, op1=ALU.subtract))
                v.tensor_copy(w16[:, c % NE, :, :, 0], w_hi[:, c % 2]).then_inc(w_split, 1)

            quantise(0)
            residual(0, range(TB))
            residual_stats(0)
            gate_mean(0)
            with dve.Fori(0, NB - 1) as b:
                own.turn(b, JOIN_DVE)
                quantise(b + 1)
                gated(b, b + 2)
                residual(b + 1, range(2))
                router_mean(b)
                residual(b + 1, range(2, TB))
                residual_stats(b + 1)
                take_logits(b)
                gate_mean(b + 1)
            own.ended(NB - 1)
            gated(NB - 1, NB)
            router_mean(NB - 1)
            split_weights(0)
            split_weights(1)
            take_logits(NB - 1)

            def over_e(a):
                return a[:, :, None].broadcast_to([P, TT, NE])

            dve.wait_ge(j_lgev, NB + 1)
            dve.wait_ge(d_route, 16)
            own.link(v.tensor_reduce(m16[:], lg[:], AX, ALU.max))
            v.tensor_tensor(pr[:], lg[:], over_e(m16), ALU.subtract).then_inc(r_c, 1)
            dve.wait_ge(r_exp, 1)
            own.link(v.tensor_reduce(z16[:], pr[:], AX, ALU.add))
            own.link(v.reciprocal(m16[:], z16[:]))
            own.link(v.tensor_tensor(pr[:], pr[:], over_e(m16), ALU.mult))
            for t in range(TT):
                own.mark(v.max(top8[:, t], pr[:, t]))
            dve.wait_ge(dve_own, own.at)
            for t in range(TT):
                own.mark(v.max_index(ix8[:, t], top8[:, t], pr[:, t]))
            dve.wait_ge(dve_own, own.at)
            own.link(v.tensor_tensor(z16[:], top8[:, :, 0], top8[:, :, 1], ALU.add))
            own.link(v.tensor_scalar(z16[:], z16[:], 1e-20, None, ALU.add))
            own.link(v.reciprocal(m16[:], z16[:]))
            for j in range(2):
                own.mark(v.tensor_tensor(w12[:, j], top8[:, :, j], m16[:], ALU.mult))
                own.link(v.tensor_copy(ixf[:, j], ix8[:, :, j]))
                own.link(v.tensor_tensor(oh[:, j], iota_e, over_e(ixf[:, j]), ALU.is_equal))
            v.tensor_tensor(ohB[:], oh[:, 0], oh[:, 1], ALU.add).then_inc(r_mask, 1)
            dve.wait_ge(r_rank, 1)
            own.link(v.tensor_copy(cnt[:], bank[1][:, 0:TT * NE].rearrange("p (t e) -> p e t", e=NE)))
            own.link(v.tensor_tensor_scan(incl[:].rearrange("p e t -> p (e t)"), c_route[:, TT * NE:2 * TT * NE],
                                          cnt[:].rearrange("p e t -> p (e t)"), 0.0, ALU.mult, ALU.add))
            own.mark(v.tensor_tensor(cnt[:], incl[:], cnt[:], ALU.subtract))
            own.mark(v.memset(ones8[:], 1.0))
            own.link(v.tensor_scalar(nt[:, 0], incl[:, :, TT - 1], 1.0 / P, 127.0 / 256, ALU.mult, ALU.add))
            own.link(v.tensor_scalar(nt[:, 1], nt[:, 0], ROUND, None, ALU.add))
            own.link(v.tensor_scalar(nt[:, 0], nt[:, 1], ROUND, None, ALU.subtract))
            own.link(v.tensor_tensor_scan(nt[:, 2], ones8[:], nt[:, 0], 0.0, ALU.mult, ALU.add))
            own.link(v.tensor_tensor(nt[:, 3], nt[:, 2], nt[:, 0], ALU.subtract))
            own.link(v.tensor_scalar(nt[:, 3], nt[:, 3], float(P), None, ALU.mult))
            own.link(v.tensor_tensor(smat[:], bank[0][:, 0:TT * NE].rearrange("p (t e) -> p t e", e=NE),
                                     cnt[:].rearrange("p e t -> p t e"), ALU.add))
            own.link(v.tensor_tensor(smat[:], smat[:], nt[:, 3:4].broadcast_to([P, TT, NE]), ALU.add))
            for j in range(2):
                own.link(v.tensor_tensor(sx[:], smat[:], oh[:, j], ALU.mult))
                own.link(v.tensor_reduce(slf[:, j], sx[:], AX, ALU.add))
            own.mark(v.tensor_copy(slot[:], slf[:]))
            own.link(v.tensor_tensor(cmp[:], tile_no, nt[:, 2:3].broadcast_to([P, TILES, NE]), ALU.is_ge))
            own.link(v.tensor_reduce(tef[:], cmp[:], AX, ALU.add))
            v.tensor_scalar(tile_e[:], tef[:], float(NE - 1), None, ALU.min).then_inc(r_slots, 1)

            for c in range(2, CHUNKS):
                split_weights(c)

            def low_part(j, c):
                dve.wait_ge(e_hi, j + 1)
                v.tensor_tensor(e_xT[:, c, 1], bank[0][:], e_xT[:, c, 0], ALU.subtract).then_inc(e_trev, 1)

            def act(j, c):
                dve.wait_ge(e_silu, j + 1)
                dve.wait_ge(e_at, j + 1)
                v.scalar_tensor_tensor(out=e_a[:, c], in0=bank[3 + c][:, 0:FI], scalar=1 / W_UP, in1=e_s[:, c],
                                       op0=ALU.mult, op1=ALU.mult).then_inc(e_act, 1)

            def act_back(j, c):
                dve.wait_ge(e_at, j + 3)
                dve.wait_ge(e_d, j + 1)
                v.tensor_copy(e_aT[:, c, 0:FK - 1], bank[5][:, 0:(FK - 1) * P].rearrange("p (f c) -> p f c", c=P))
                v.tensor_copy(e_aT[0:FL, c, FK - 1], bank[5][0:FL, (FK - 1) * P:FK * P]).then_inc(e_atev, 1)

            def rows_out(j, c, half):
                dve.wait_ge(e_d, j + 3)
                dve.wait_ge(d_ey[c], half * 16 + 16)
                v.tensor_copy(e_y[:, c], bank[6 + c][:]).then_inc(e_dev, 1)

            for c in range(4):
                dve.wait_ge(sc_done[c], 8 * TT)
            low_part(0, 0)
            low_part(1, 1)
            act(0, 0)
            with dve.Fori(0, TILES // 2 - 1) as i:
                for c in range(2):
                    j = i * 2 + c + 1
                    low_part(j + 1, c)
                    act_back(j - 1, c)
                    act(j, 1 - c)
                    rows_out(j - 1, c, i)
            low_part(LAST, 0)
            for j in (LAST - 1, LAST):
                act_back(j - 1, (j - 1) % 2)
                act(j, j % 2)
                rows_out(j - 1, (j - 1) % 2, (j - 1) // 2)
            act_back(LAST, 0)
            rows_out(LAST, 0, LAST // 2)
            for t in range(TT):
                dve.wait_ge(g_row[t % 4], 32 * (t // 4 + 1))
                if t >= 4:
                    dve.wait_ge(d_out[t % 4], 16 * (t // 4))
                own.link(v.scalar_tensor_tensor(out=o_o[:, t % 4], in0=o_r[:, t % 4, 0], scalar=w12[:, 0, t:t + 1],
                                                in1=xa[:, t], op0=ALU.mult, op1=ALU.add))
                v.scalar_tensor_tensor(out=o_o[:, t % 4], in0=o_r[:, t % 4, 1], scalar=w12[:, 1, t:t + 1],
                                       in1=o_o[:, t % 4], op0=ALU.mult, op1=ALU.add).then_inc(o_done, 1)


def kernel(x, ctx_1024, L0_attn_w_q, L0_attn_w_k, L0_attn_w_v, L0_attn_w_o, L0_xattn_in_proj_w, L0_xattn_conv_w,
           L0_xattn_conv_b, L0_xattn_x_proj_w, L0_xattn_dt_proj_w, L0_xattn_dt_proj_b, L0_xattn_A_log, L0_xattn_D,
           L0_ffn_router_w, L0_ffn_w_gate, L0_ffn_w_up, L0_ffn_w_down):
    import numpy as np
    import concourse.bacc as bacc
    from concourse.bass_utils import run_bass_kernel_spmd

    f = np.float32
    a = {}
    a["x"] = np.asarray(x)
    a["ctx_t"] = np.asarray(ctx_1024).transpose(0, 2, 1)
    a["w_attn_t"] = np.stack([np.asarray(w).T for w in (L0_attn_w_q, L0_attn_w_k, L0_attn_w_v, L0_attn_w_o)])
    a["in_w_t"] = np.asarray(L0_xattn_in_proj_w).T
    a["ssm_par"] = np.concatenate([
        np.asarray(L0_xattn_conv_w), np.asarray(L0_xattn_conv_b)[:, None], np.asarray(L0_xattn_dt_proj_b)[:, None],
        np.asarray(L0_xattn_D)[:, None], np.asarray(L0_xattn_A_log)], axis=1)
    xp = np.asarray(L0_xattn_x_proj_w)
    a["xp_t"] = np.concatenate([xp[DR:], xp[DR:], xp[DR:], xp[:DR]]).T
    a["dt_w_t"] = np.concatenate([np.zeros((3 * NBC, E), f), np.asarray(L0_xattn_dt_proj_w).T])
    a["router_t"] = np.asarray(L0_ffn_router_w).T
    a["wg_t"] = np.asarray(L0_ffn_w_gate).transpose(0, 2, 1)
    a["wu_t"] = np.asarray(L0_ffn_w_up).transpose(0, 2, 1)
    a["wd_t"] = np.asarray(L0_ffn_w_down).transpose(0, 2, 1)
    i, j = np.arange(P)[:, None], np.arange(P)[None, :]
    a["k_square"] = np.stack([(i == j).astype(f), np.where(j > i, f(-1e30), f(0)), np.where(i > j, f(-1e30), f(0)),
                              (i < j).astype(f)])
    a["k_sel"] = np.tile(np.eye(NBC, dtype=f), (3, 1))
    sh = np.zeros((P, HG, P), f)
    for r in range(2 * HG):
        sh[r, r % HG] = -1
    a["k_shift"] = sh
    a["k_head"] = np.repeat(np.eye(HG, dtype=f), HD, axis=0)
    keep = np.ones((NE, TT), f)
    keep[:, 0] = 0
    row = np.concatenate([np.tile(np.arange(NE, dtype=f), TT), keep.ravel(), np.repeat(np.arange(TILES, dtype=f), NE)])
    a["k_route"] = np.tile(row, (P, 1))
    nc = bacc.Bacc("TRN2", target_bir_lowering=False, num_devices=1)
    arrays = {f"in_{n}": np.ascontiguousarray(v) for n, v in a.items()}
    args = {n: nc.dram_tensor(f"in_{n}", v.shape, mybir.dt.from_np(v.dtype), kind="ExternalInput").ap()
            for n, v in a.items()}
    out = nc.dram_tensor("out", (TOK, E), F32, kind="ExternalOutput").ap()
    decoder_layer(nc, **args, out=out)
    r = run_bass_kernel_spmd(nc, [arrays], core_ids=[0])
    return r.results[0]["out"].reshape(NB, S, E)
```
